# Optimizing a Trainium2 kernel written in Bass

```python
import numpy as np
import jax
import jax.numpy as jnp

def _softmax(x, axis=-1):
    return jax.nn.softmax(x, axis=axis)

def _gelu(x):
    return jax.nn.gelu(x, approximate=True)

def _silu(x):
    return jax.nn.silu(x)

def _sigmoid(x):
    return jax.nn.sigmoid(x)

def _layernorm(x, axis=-1, eps=1e-05):
    m = jnp.mean(x, axis=axis, keepdims=True)
    v = jnp.var(x, axis=axis, keepdims=True)
    return (x - m) / jnp.sqrt(v + eps)

def _scatter_add(tgt, idx, src, axis=0):
    return tgt.at[idx].add(src)

def _segment_sum(src, seg, n):
    return jax.ops.segment_sum(src, seg, n)
kernel_name = 'mk_vit_tower_cls_d1_tok_img512_r4_825433'

def setup_inputs(seed: int=0):
    np.random.seed(seed)
    _w = jnp.asarray

    def _rec_inputs():
        import jax
        import jax.numpy as jnp
        _rk = jax.random.key(seed)
        x = -0.000147625 + 0.999875 * jax.random.normal(jax.random.fold_in(_rk, 1), (64, 3, 224, 224), jnp.float32)
        cls_tok = 0.02 * jax.random.normal(jax.random.fold_in(_rk, 5), (1, 1, 128), jnp.float32)
        return (x, cls_tok)
    x, cls_tok = _rec_inputs()

    def _L0_tok_setup():
        import jax, jax.numpy as jnp
        import numpy as np
        N_PATCHES = 8
        PATCH = 28
        C = 3
        IN_D = C * PATCH * PATCH
        HID = 128
        SEQ = N_PATCHES * N_PATCHES + 1

        def _positional_embedding(seq_len, dim):
            i = np.arange(seq_len)[:, None].astype(np.float32)
            j = np.arange(dim)[None, :].astype(np.float32)
            ang = i / np.power(100000.0, j / dim)
            pe = np.where(j % 2 == 0, np.sin(ang), np.cos(ang))
            return jnp.asarray(pe, dtype=jnp.float32)
        key = jax.random.key(seed)
        k1, k2, k3, k4 = jax.random.split(key, 4)
        B = 64
        X = jax.random.normal(k1, (B, C, 224, 224), dtype=jnp.float32)
        bound = 1.0 / np.sqrt(IN_D)
        W = jax.random.uniform(k2, (HID, IN_D), minval=-bound, maxval=bound, dtype=jnp.float32)
        b = jax.random.uniform(k3, (HID,), minval=-bound, maxval=bound, dtype=jnp.float32)
        class_token = jax.random.uniform(k4, (1, HID), dtype=jnp.float32)
        pos_embed = _positional_embedding(SEQ, HID)
        return {'X': X, 'W': W, 'b': b, 'class_token': class_token, 'pos_embed': pos_embed}
    _L0_tok_all = _L0_tok_setup()
    _L0_tok_in = {k: v for k, v in _L0_tok_all.items() if k in ('W', 'b', 'class_token', 'pos_embed')}
    del _L0_tok_all

    def _L0_attn_setup():
        import jax, jax.numpy as jnp
        import numpy as np
        from jax import lax
        B, L, D_MODEL = (4, 512, 128)
        D_STATE, HEADDIM, NGROUPS, RANK = (128, 64, 1, 4)
        D_INNER = 2 * D_MODEL
        NHEADS = D_INNER // HEADDIM
        HG = NHEADS // NGROUPS
        PC = HEADDIM // RANK
        KCONV = 4
        BC_DIM = NGROUPS * D_STATE * RANK
        CONV_DIM = D_INNER + 2 * BC_DIM
        D_IN = 2 * D_INNER + 2 * BC_DIM + NHEADS
        EPS = 1e-05
        key = jax.random.key(seed)
        ks = jax.random.split(key, 8)
        return {'hidden_states': jax.random.normal(ks[0], (B, L, D_MODEL), jnp.float32), 'W_in': jax.random.normal(ks[1], (D_MODEL, D_IN), jnp.float32) * 0.02, 'conv_w': jax.random.normal(ks[2], (CONV_DIM, KCONV), jnp.float32) * 0.1, 'conv_b': jnp.zeros((CONV_DIM,), jnp.float32), 'dt_bias': jax.random.uniform(ks[3], (NHEADS,), jnp.float32, -4.0, -2.0), 'A_log': jnp.log(jnp.arange(1, NHEADS + 1, dtype=jnp.float32)), 'D_skip': 1.0 + 0.1 * jax.random.normal(ks[4], (NHEADS,), jnp.float32), 'W_out': jax.random.normal(ks[5], (D_INNER, D_MODEL), jnp.float32) * 0.02}
    _L0_attn_all = _L0_attn_setup()
    _L0_attn_in = {k: v for k, v in _L0_attn_all.items() if k in ('W_in', 'conv_w', 'conv_b', 'dt_bias', 'A_log', 'D_skip', 'W_out')}
    del _L0_attn_all

    def _L0_ffn_setup():
        import jax, jax.numpy as jnp
        import numpy as np
        NUM_EXPERTS = 8
        TOP_K = 2
        D_MODEL = 128
        D_FF = 512
        key = jax.random.key(seed)
        ks = jax.random.split(key, 6)
        sd = 1.0 / np.sqrt(D_MODEL)
        sf = 1.0 / np.sqrt(D_FF)
        x = jax.random.normal(ks[0], (8, 512, D_MODEL), dtype=jnp.float32)
        gate_w = jax.random.uniform(ks[1], (NUM_EXPERTS, D_MODEL), jnp.float32, -sd, sd)
        w1 = jax.random.uniform(ks[2], (NUM_EXPERTS, D_MODEL, D_FF), jnp.float32, -sd, sd)
        b1 = jax.random.uniform(ks[3], (NUM_EXPERTS, D_FF), jnp.float32, -sd, sd)
        w2 = jax.random.uniform(ks[4], (NUM_EXPERTS, D_FF, D_MODEL), jnp.float32, -sf, sf)
        b2 = jax.random.uniform(ks[5], (NUM_EXPERTS, D_MODEL), jnp.float32, -sf, sf)
        return {'x': x, 'gate_w': gate_w, 'w1': w1, 'b1': b1, 'w2': w2, 'b2': b2}
    _L0_ffn_all = _L0_ffn_setup()
    _L0_ffn_in = {k: v for k, v in _L0_ffn_all.items() if k in ('gate_w', 'w1', 'b1', 'w2', 'b2')}
    del _L0_ffn_all
    return {'x': x, 'cls_tok': cls_tok, 'L0_tok_W': _L0_tok_in['W'], 'L0_tok_b': _L0_tok_in['b'], 'L0_tok_class_token': _L0_tok_in['class_token'], 'L0_tok_pos_embed': _L0_tok_in['pos_embed'], 'L0_attn_W_in': _L0_attn_in['W_in'], 'L0_attn_conv_w': _L0_attn_in['conv_w'], 'L0_attn_conv_b': _L0_attn_in['conv_b'], 'L0_attn_dt_bias': _L0_attn_in['dt_bias'], 'L0_attn_A_log': _L0_attn_in['A_log'], 'L0_attn_D_skip': _L0_attn_in['D_skip'], 'L0_attn_W_out': _L0_attn_in['W_out'], 'L0_ffn_gate_w': _L0_ffn_in['gate_w'], 'L0_ffn_w1': _L0_ffn_in['w1'], 'L0_ffn_b1': _L0_ffn_in['b1'], 'L0_ffn_w2': _L0_ffn_in['w2'], 'L0_ffn_b2': _L0_ffn_in['b2']}

def reference(x, cls_tok, L0_tok_W, L0_tok_b, L0_tok_class_token, L0_tok_pos_embed, L0_attn_W_in, L0_attn_conv_w, L0_attn_conv_b, L0_attn_dt_bias, L0_attn_A_log, L0_attn_D_skip, L0_attn_W_out, L0_ffn_gate_w, L0_ffn_w1, L0_ffn_b1, L0_ffn_w2, L0_ffn_b2):
    import jax
    import jax.numpy as jnp

    def _L0_tok_ref(X, W, b, class_token, pos_embed):
        import jax, jax.numpy as jnp
        import numpy as np
        N_PATCHES = 8
        PATCH = 28
        C = 3
        IN_D = C * PATCH * PATCH
        HID = 128
        SEQ = N_PATCHES * N_PATCHES + 1

        def _positional_embedding(seq_len, dim):
            i = np.arange(seq_len)[:, None].astype(np.float32)
            j = np.arange(dim)[None, :].astype(np.float32)
            ang = i / np.power(100000.0, j / dim)
            pe = np.where(j % 2 == 0, np.sin(ang), np.cos(ang))
            return jnp.asarray(pe, dtype=jnp.float32)
        B = X.shape[0]
        patches = X.reshape(B, C, N_PATCHES, PATCH, N_PATCHES, PATCH)
        patches = patches.transpose(0, 2, 4, 1, 3, 5).reshape(B, N_PATCHES * N_PATCHES, IN_D)
        tokens = jnp.einsum('bpi,hi->bph', patches, W) + b
        cls = jnp.broadcast_to(class_token[None, :, :], (B, 1, HID))
        tokens = jnp.concatenate([cls, tokens], axis=1)
        return tokens * pos_embed[None, :, :]

    def _L0_attn_ref(hidden_states, W_in, conv_w, conv_b, dt_bias, A_log, D_skip, W_out):
        import jax, jax.numpy as jnp
        import numpy as np
        from jax import lax
        B, L, D_MODEL = (4, 512, 128)
        D_STATE, HEADDIM, NGROUPS, RANK = (128, 64, 1, 4)
        D_INNER = 2 * D_MODEL
        NHEADS = D_INNER // HEADDIM
        HG = NHEADS // NGROUPS
        PC = HEADDIM // RANK
        KCONV = 4
        BC_DIM = NGROUPS * D_STATE * RANK
        CONV_DIM = D_INNER + 2 * BC_DIM
        D_IN = 2 * D_INNER + 2 * BC_DIM + NHEADS
        EPS = 1e-05
        b, l, _ = hidden_states.shape
        zxbcdt = hidden_states @ W_in
        z = zxbcdt[..., :D_INNER]
        xBC = zxbcdt[..., D_INNER:D_INNER + CONV_DIM]
        dt_raw = zxbcdt[..., D_INNER + CONV_DIM:]
        xp = jnp.pad(xBC, ((0, 0), (KCONV - 1, 0), (0, 0)))
        xBC = sum((xp[:, k:k + l, :] * conv_w[:, k] for k in range(KCONV))) + conv_b
        xBC = jax.nn.silu(xBC)
        x = xBC[..., :D_INNER].reshape(b, l, NGROUPS, HG, RANK, PC)
        Bm = xBC[..., D_INNER:D_INNER + BC_DIM].reshape(b, l, NGROUPS, D_STATE, RANK)
        Cm = xBC[..., D_INNER + BC_DIM:].reshape(b, l, NGROUPS, D_STATE, RANK)
        dt = jax.nn.softplus(dt_raw + dt_bias)
        decay = jnp.exp(dt * -jnp.exp(A_log))
        dec = decay.reshape(b, l, NGROUPS, HG)
        dth = dt.reshape(b, l, NGROUPS, HG)

        def step(h, inp):
            dec_t, dt_t, B_t, C_t, X_t = inp
            upd = jnp.einsum('bgnr,bghrp->bghnp', B_t, X_t)
            h = dec_t[..., None, None] * h + dt_t[..., None, None] * upd
            y = jnp.einsum('bgnr,bghnp->bghrp', C_t, h)
            return (h, y)
        h0 = jnp.zeros((b, NGROUPS, HG, D_STATE, PC), hidden_states.dtype)
        xs = (jnp.moveaxis(dec, 1, 0), jnp.moveaxis(dth, 1, 0), jnp.moveaxis(Bm, 1, 0), jnp.moveaxis(Cm, 1, 0), jnp.moveaxis(x, 1, 0))
        _, ys = lax.scan(step, h0, xs)
        y = jnp.moveaxis(ys, 0, 1).reshape(b, l, NHEADS, HEADDIM)
        y = y + x.reshape(b, l, NHEADS, HEADDIM) * D_skip[None, None, :, None]
        y = y.reshape(b, l, D_INNER) * jax.nn.silu(z) @ W_out
        res = hidden_states + y
        var = jnp.mean(res * res, axis=-1, keepdims=True)
        return res * lax.rsqrt(var + EPS)

    def _L0_ffn_ref(x, gate_w, w1, b1, w2, b2):
        import jax, jax.numpy as jnp
        import numpy as np
        NUM_EXPERTS = 8
        TOP_K = 2
        D_MODEL = 128
        D_FF = 512
        xs = x.reshape(-1, x.shape[-1])
        gate_logits = jnp.einsum('td,ed->te', xs, gate_w)
        top_vals, sel = jax.lax.top_k(gate_logits, TOP_K)
        weights = jax.nn.softmax(top_vals.astype(jnp.float32), axis=1)
        combine = jnp.sum(jax.nn.one_hot(sel, NUM_EXPERTS, dtype=weights.dtype) * weights[..., None], axis=1)
        out = jnp.zeros_like(xs)
        for e in range(NUM_EXPERTS):
            h = jax.nn.relu(xs @ w1[e] + b1[e])
            y = h @ w2[e] + b2[e]
            out = out + combine[:, e:e + 1] * y
        return out.reshape(x.shape)
    h = _L0_tok_ref(x, L0_tok_W, L0_tok_b, L0_tok_class_token, L0_tok_pos_embed)
    h = jnp.concatenate([jnp.broadcast_to(cls_tok, (h.shape[0], 1, h.shape[2])), h], axis=1)
    h = h + _L0_attn_ref(_layernorm(h, axis=-1), L0_attn_W_in, L0_attn_conv_w, L0_attn_conv_b, L0_attn_dt_bias, L0_attn_A_log, L0_attn_D_skip, L0_attn_W_out)
    h = h + _L0_ffn_ref(_layernorm(h, axis=-1), L0_ffn_gate_w, L0_ffn_w1, L0_ffn_b1, L0_ffn_w2, L0_ffn_b2)
    return h

_drawn_inputs = setup_inputs


def setup_inputs(seed=0):
    import zlib

    import numpy as np

    out = dict(_drawn_inputs(seed))
    spreads = {'L0_attn_conv_b': (0.0, 0.8)}
    factors = {'L0_attn_W_in': 8.0,
     'L0_attn_conv_w': 8.0,
     'L0_attn_dt_bias': 8.0,
     'L0_attn_A_log': 8.0,
     'L0_attn_D_skip': 8.0,
     'L0_attn_W_out': 8.0,
     'L0_ffn_b1': 5.234,
     'L0_ffn_b2': 4.28}
    for name, (base, spread) in spreads.items():
        noise = np.random.default_rng([zlib.crc32(name.encode()), seed]).standard_normal(out[name].shape)
        drawn = base * np.exp(spread * noise) if base else spread * noise
        out[name] = jnp.asarray(drawn.astype(out[name].dtype))
    for name, factor in factors.items():
        out[name] = (out[name] * factor).astype(out[name].dtype)
    return out
```

```python
from contextlib import ExitStack

import numpy as np

import concourse.bass as bass
from concourse import mybir
from concourse.alu_op_type import AluOpType as ALU

FP32 = mybir.dt.float32
U32 = mybir.dt.uint32
I32 = mybir.dt.int32
ACT = mybir.ActivationFunctionType
AX = mybir.AxisListType

B, NPATCH, PATCH, CH = 64, 64, 28, 3
K_TOK = CH * PATCH * PATCH
D = 128
KC = K_TOK // D
K_TAIL = K_TOK - KC * D
L = NPATCH + 2
GI = 4
NG = B // GI
T = GI * L
HEADS, RANK, PC, NST = 4, 4, 16, 128
HP = 32
TAPS = 4
Q, NC = 22, 3
QR = Q * RANK
EPS = 1e-5
E_N, FF = 8, 512
FC = FF // D
TT = QR
TPG = T // TT
PARTS = 2
GPP = NG // PARTS
JT = GPP * TPG
TOKP = JT * TT
SL = 128
KMAX = -(-TOKP // SL)
NT = (2 * TOKP + E_N * (SL - 1)) // SL
W1C, W2C = FF + FC, FF + D
WCOLS = W1C + W2C
NCH = 12
MASKED = 1.0e4
HIDDEN = 1.0e30

C_ID, C_CEN, C_MEAN = 0, D, 2 * D
S_SEG, S_IT, S_ONE, S_UP, S_ONES, S_IOTA, S_IOTA8, S_KIO, S_TIO, S_MASK = np.cumsum(
    [0, QR, 2 * Q, QR, TT, TT, E_N, E_N, E_N * KMAX, E_N * NT]).tolist()
S_END = S_MASK + E_N * JT


def constants():
    eye = np.eye(D, dtype=np.float32)
    mean = np.full((D, D), 1.0 / D, np.float32)
    c128 = np.concatenate([eye, eye - mean, mean], axis=1)
    c88 = np.zeros((TT, S_END), np.float32)
    u, s = np.arange(Q)[:, None], np.arange(QR)[None, :] // RANK
    c88[:Q, S_SEG:S_SEG + QR] = u > s
    c88[32:32 + Q, S_SEG:S_SEG + QR] = -MASKED * (u <= s)
    t = np.arange(Q)[None, :]
    c88[:Q, S_IT:S_IT + Q] = u == t
    c88[:Q, S_IT + Q:S_IT + 2 * Q] = u <= t
    c88[:Q, S_ONE:S_ONE + QR] = 1.0
    k, p = np.arange(TT)[:, None], np.arange(TT)[None, :]
    c88[:, S_UP:S_UP + TT] = k < p
    c88[:, S_ONES:S_ONES + TT] = 1.0
    c88[:, S_IOTA:S_IOTA + E_N] = np.arange(E_N)
    c88[:, S_IOTA8:S_IOTA8 + E_N] = np.arange(E_N) + E_N
    c88[:, S_KIO:S_KIO + E_N * KMAX] = np.tile(np.arange(KMAX) * SL, E_N)
    c88[:, S_TIO:S_TIO + E_N * NT] = np.repeat(np.arange(NT), E_N)
    c88[:, S_MASK:S_MASK + E_N * JT] = np.tile(np.arange(JT) > 0, E_N)
    seg_rhs = np.zeros((32 + Q, NC * GI * HEADS, Q), np.float32)
    seg_rhs[32:] = (u > t)[:, None, :]
    return c128, c88, seg_rhs.reshape(32 + Q, -1)


class Group:

    def __init__(self, n, parity, before):
        self.n, self.parity, self.before = n, parity, before

    def next(self):
        return Group(self.n + 1, 1 - self.parity, self.before + self.parity)

    def after_next(self):
        return Group(self.n + 2, self.parity, self.before + 1)

    def last(self):
        return Group(self.n - 1, 1 - self.parity, self.before - (1 - self.parity))

    def first(self):
        return isinstance(self.n, int) and self.n == 0


def tower(nc, x_main, x_tail, w_tok, w_tok_tail, tok_cols, w_in, w_dt, conv, dt_row, dt_col, w_out,
          gate_w, experts, c128_d, c88_d, seg_d, out):
    ctx = ExitStack()
    with ctx:
        def sb(name, shape, dt=FP32):
            return ctx.enter_context(nc.sbuf_tensor(name, shape, dt))

        def sem(name):
            return ctx.enter_context(nc.semaphore(name))

        h1_rows = nc.dram_tensor("h1_rows", [NG * TPG, TT, D], FP32).ap()
        slot_x = [nc.dram_tensor(f"slot_x{p}", [NT * SL, D], FP32).ap() for p in range(PARTS)]
        slot_y = [nc.dram_tensor(f"slot_y{p}", [NT * SL, D], FP32).ap() for p in range(PARTS)]

        c128 = sb("c128", [128, 3 * D])
        c88 = sb("c88", [TT, S_END])
        wt = sb("wt", [128, KC, D])
        wtt = sb("wtt", [K_TAIL, D])
        tcol = sb("tcol", [128, 3 + L - 1])
        win = sb("win", [128, 16, D])
        wdt = sb("wdt", [128, HEADS])
        cv = sb("cv", [128, NCH, TAPS + 1])
        dtr = sb("dtr", [Q, 2 * HEADS])
        dtc = sb("dtc", [128, 2])
        wo = sb("wo", [128, RANK, D])
        gw = sb("gw", [128, E_N])
        eps = sb("eps", [128, 1])
        ident, center, mean = c128[:, C_ID:C_ID + D], c128[:, C_CEN:C_CEN + D], c128[:, C_MEAN:C_MEAN + D]

        XCOLS = KC * GI * NPATCH
        big = sb("big", [128, max(2 * XCOLS, E_N * WCOLS)])
        xm = [big[:, i * XCOLS:(i + 1) * XCOLS].rearrange("p (k t) -> p k t", k=KC) for i in range(2)]
        wall = big[:, 0:E_N * WCOLS].rearrange("p (e c) -> p e c", e=E_N)
        xt = [sb(f"xt{i}", [K_TAIL, GI * NPATCH]) for i in range(2)]
        h = [sb(f"h{i}", [128, T]) for i in range(2)]
        xn = [sb(f"xn{i}", [128, T]) for i in range(2)]
        ln_sq = sb("ln_sq_b", [128, T])
        ln_rs = sb("ln_rs_b", [128, T])
        res = sb("res_b", [128, T])
        po_sq = sb("po_sq_b", [128, T])
        po_rs = sb("po_rs_b", [128, T])
        h1 = sb("h1_b", [128, T])
        xs = sb("xs_b", [128, T])
        xs_all = sb("xs_all", [TT, NG * TPG, D])
        h1_t = sb("h1_t", [TT, TPG * D])
        logit = sb("logit", [TT, NG, TPG * E_N])
        NDT = NC * GI * HEADS
        du = sb("du", [Q, NDT])
        dn = sb("dn", [Q, NDT])
        de = sb("de", [Q, NDT])
        dr = sb("dr", [Q, NDT])
        ds_ = sb("ds_", [Q, NDT])
        dq = sb("dq", [Q, NDT])
        dp = sb("dp", [Q, NDT])
        dt_s = sb("dt_s", [Q, NC, GI, HEADS])
        dt_wide = sb("dt_wide", [Q, NC * GI, HEADS * HP])
        da_s = sb("da_s", [Q, NC, GI, HEADS])
        nega_r = sb("nega_r", [Q, HEADS])
        nega_c = sb("nega_c", [128, 1])
        seg_r = sb("seg_r", [32 + Q, NDT, Q])
        acc = sb("acc", [128, NCH, T])
        xc = sb("xc", [128, GI, NC, QR])
        bc = sb("bc", [128, GI, NC, QR])
        cc = sb("cc", [128, GI, NC, QR])
        sz = sb("sz", [128, RANK, T])
        decay = sb("decay", [QR, NC, GI, HEADS, Q])
        grow = sb("grow", [128, 2, GI, Q])
        total = sb("total", [QR, GI, HEADS])
        xdt = sb("xdt", [128, NC, GI, QR])
        xdt_t = sb("xdt_t", [QR, NC, GI, D])
        b_t = sb("b_t", [QR, 2, GI, D])
        xe = sb("xe", [QR, 3, GI, HEADS * PC])
        hs = sb("hs", [128, GI, 2, HEADS, HP])
        m_buf = sb("m_buf", [128, NC * GI * HEADS * QR])
        m = m_buf[0:QR, :].rearrange("p (c i h t) -> p c i h t", c=NC, i=GI, h=HEADS)
        t1 = sb("t1", [128, 2, GI, QR])
        y = xdt
        yg = sb("yg", [128, RANK, T])

        bank = [ctx.enter_context(nc.psum_tensor(f"bank{i}", [128, 512], FP32)) for i in range(8)]
        b_tok, b_c, b_v, w0, w1, w2, w3, b_dt = bank
        RING = [w0, w1, w2, w3]
        XT_B, BT_B, G_B, I_B, Y_B, H_B = [w3, w0, w2], [w1, b_dt], [b_tok, w3, w0], [w1, b_dt], [w2, b_tok, w3], w2

        loaded, zeroed, hs_zeroed, setup_done, nega_done = map(sem, ["loaded", "zeroed", "hs_zeroed", "setup_done", "nega_done"])
        x_loaded = [sem(f"x_loaded{i}") for i in range(2)]
        names = """tok_summed h_ready ln_centered ln_squared ln_var ln_log ln_rstd xn_ready
            out_proj res_ready res_squared res_var res_log res_rstd res_scaled h1_ready po_centered po_squared po_var
            po_log po_rstd xs_ready rows_turned rows_copied rows_stored
            dt_raw dt_exp dt_step seg_ready dt_widened seg_summed decay_ready spread grow_ready total_ready
            proj tap0 conv_step x_act b_act z_act c_act xdt_ready
            x_turned x_turned_copied b_turned b_turned_copied xe_ready states states_copied
            scores m_ready inter inter_read intra y_sum y_total yg_ready""".split()
        S = {n: sem(n) for n in names}
        (tok_summed, h_ready, ln_centered, ln_squared, ln_var, ln_log, ln_rstd, xn_ready,
         out_proj, res_ready, res_squared, res_var, res_log, res_rstd, res_scaled, h1_ready, po_centered, po_squared,
         po_var, po_log, po_rstd, xs_ready, rows_turned, rows_copied, rows_stored,
         dt_raw, dt_exp, dt_step, seg_ready, dt_widened, seg_summed, decay_ready, spread, grow_ready, total_ready,
         proj, tap0, conv_step, x_act, b_act, z_act, c_act, xdt_ready,
         x_turned, x_turned_copied, b_turned, b_turned_copied, xe_ready, states, states_copied,
         scores, m_ready, inter, inter_read, intra, y_sum, y_total, yg_ready) = [S[n] for n in names]

        N_DT = 17
        DT_NEG, DT_A = 2, 17
        N_CONV = NCH * (TAPS - 1)
        N_ROUTE, R_BOTH, R_DIFF = 27, 12, 14

        def conv_at(chunk, tap):
            return (chunk // 2) * 2 * (TAPS - 1) + (tap - 1) * 2 + chunk % 2 + 1

        def conv_all(chunk):
            return conv_at(chunk, TAPS - 1)

        def by_chunk(buf):
            return buf.rearrange("p i c (t r) -> p i (c t) r", r=RANK)

        loads = [(c128[:, :], c128_d), (c88[:, :], c88_d), (wt[:, :, :], w_tok.rearrange("p (k d) -> p k d", d=D)),
                 (wtt[:, :], w_tok_tail), (tcol[:, :], tok_cols), (win[:, :, :], w_in.rearrange("p (k d) -> p k d", d=D)),
                 (wdt[:, :], w_dt), (cv[:, :, :], conv.rearrange("p (k d) -> p k d", d=TAPS + 1)),
                 (dtr[:, :], dt_row), (dtc[:, :], dt_col),
                 (wo[:, :, :], w_out.rearrange("p (k d) -> p k d", d=D)), (gw[:, :], gate_w),
                 (seg_r[:, :, :], seg_d.rearrange("p (k d) -> p k d", d=Q))]
        N_LOADS = 16 * len(loads)
        experts_loaded = sem("experts_loaded")

        onehot = [sb(f"onehot{i}", [TT, JT, E_N]) for i in range(2)]
        both = sb("both", [TT, JT, E_N])
        ra = sb("ra", [TT, JT, E_N])
        rb = sb("rb", [TT, JT, E_N])
        top = [sb(f"top{i}", [TT, JT]) for i in range(2)]
        idx = sb("idx", [TT, JT])
        rd = sb("rd", [TT, JT])
        rsum = sb("rsum", [TT, E_N, JT])
        rtot = sb("rtot", [TT, E_N, JT])
        cmp_k = sb("cmp_k", [TT, E_N, KMAX])
        ntile = sb("ntile", [TT, E_N])
        endt = sb("endt", [TT, E_N])
        base = sb("base", [TT, E_N])
        ones_e = sb("ones_e", [TT, E_N])
        cmp_t = sb("cmp_t", [TT, NT, E_N])
        tile_f = sb("tile_f", [TT, NT])
        wgt = [sb(f"wgt{i}", [TT, PARTS, JT]) for i in range(2)]
        slot_f = sb("slot_f", [TT, JT])
        slot_u = [sb(f"slot_u{i}", [TT, PARTS, JT], U32) for i in range(2)]
        tile_e = sb("tile_e", [1, PARTS, NT], I32)

        mark = sb("mark", [1, 1])
        sc_x = [sb(f"sc_x{i}", [TT, D]) for i in range(2)]
        sc_i = [[sb(f"sc_i{i}{k}", [TT, 1], U32) for k in range(2)] for i in range(2)]
        cols = np.cumsum([0, D, D, W1C, W2C, FC * SL]).tolist()
        assert 2 * (cols[-1] + D) <= NC * GI * HEADS * QR

        def part_of_m(s, k, width):
            o = s * (cols[-1] + D) + cols[k]
            return m_buf[:, o:o + width]

        fx = [part_of_m(i, 0, D) for i in range(2)]
        fxt = [part_of_m(i, 1, SL) for i in range(2)]
        fw1 = [part_of_m(i, 2, W1C) for i in range(2)]
        fw2 = [part_of_m(i, 3, W2C) for i in range(2)]
        fh = [part_of_m(i, 4, FC * SL).rearrange("p (k t) -> p k t", k=FC) for i in range(2)]
        fy = [part_of_m(i, 5, D) for i in range(2)]
        gy = [[sb(f"gy{i}{k}", [TT, D]) for k in range(2)] for i in range(2)]
        gi = [[sb(f"gi{i}{k}", [TT, 1], U32) for k in range(2)] for i in range(2)]
        gh = [sb(f"gh{i}", [TT, D]) for i in range(2)]
        go = [sb(f"go{i}", [TT, D]) for i in range(2)]

        route_step, route_mm, route_exp, routed = map(sem, ["route_step", "route_mm", "route_exp", "routed"])
        slot_step, xe_part, sc_copied = map(sem, ["slot_step", "xe_part", "sc_copied"])
        sent = [sem(f"sent{i}") for i in range(2)]
        fx_loaded = [sem(f"fx_loaded{i}") for i in range(2)]
        fx_turned, fx_copied, w1_staged, w2_staged, hidden_mm, hidden_act, y_mm, y_biased = map(
            sem, ["fx_turned", "fx_copied", "w1_staged", "w2_staged", "hidden_mm", "hidden_act", "y_mm", "y_biased"])
        fy_stored = [sem(f"fy_stored{i}") for i in range(2)]
        ga_index = sem("ga_index")
        gathered = [sem(f"gathered{i}") for i in range(2)]
        gh_loaded = [sem(f"gh_loaded{i}") for i in range(2)]
        first_added, combined = sem("first_added"), sem("combined")
        out_stored = [sem(f"out_stored{i}") for i in range(2)]

        def over_groups(eng, body):
            body(Group(0, 0, 0))
            with eng.Fori(0, (NG - 2) // 2) as i:
                body(Group(2 * i + 1, 1, i))
                body(Group(2 * i + 2, 0, i + 1))
            body(Group(NG - 1, 1, (NG - 2) // 2))

        def is_last(g):
            return isinstance(g.n, int) and g.n == NG - 1

        block = ctx.enter_context(nc.Block())

        @block.sync
        def _(sp):
            for dst, src in loads:
                sp.dma_start(dst, src).then_inc(loaded, 16)

            def load_x(g):
                sp.dma_start(xm[g.parity][:, :, :], x_main[bass.ds(g.n, 1), :, :].rearrange("o p (k d) -> (o p) k d", k=KC)
                             ).then_inc(x_loaded[g.parity], 16)
                sp.dma_start(xt[g.parity][:, :], x_tail[bass.ds(g.n, 1), :, :].rearrange("o p d -> (o p) d")
                             ).then_inc(x_loaded[g.parity], 16)

            def store_rows(g):
                sp.wait_ge(rows_copied, g.n + 1)
                sp.dma_start(h1_rows[bass.ds(g.n * TPG, TPG), :, :].rearrange("k p d -> p k d"),
                             h1_t[:, :].rearrange("p (k d) -> p k d", d=D)).then_inc(rows_stored, 16)

            load_x(Group(0, 0, 0))
            load_x(Group(1, 1, 0))
            sp.wait_ge(zeroed, 1)
            half = NT * D // 2
            for p in range(PARTS):
                for k in range(2):
                    sp.dma_start(slot_x[p].rearrange("(p k) d -> p (k d)", p=128)[:, k * half:(k + 1) * half],
                                 acc[:, :, :].rearrange("p k t -> p (k t)")[:, :half]).then_inc(zeroed, 16)

            def body(g):
                sp.wait_ge(tok_summed, g.n + 1)
                load_x(g.after_next())
                if not g.first():
                    store_rows(g.last())

            body(Group(0, 0, 0))
            with sp.Fori(0, (NG - 4) // 2) as i:
                body(Group(2 * i + 1, 1, i))
                body(Group(2 * i + 2, 0, i + 1))
            body(Group(NG - 3, 1, (NG - 4) // 2))
            sp.wait_ge(tok_summed, NG)
            sp.dma_start(wall, experts.rearrange("p (e c) -> p e c", e=E_N)).then_inc(experts_loaded, 16)
            for n in range(NG - 3, NG):
                store_rows(Group(n, n % 2, n // 2))
            sp.wait_ge(rows_stored, 16 * NG)

            def load_fx(p, i, s):
                if not isinstance(i, int) or p or i >= 2:
                    sp.wait_ge(fx_turned, i + (p * NT - 1))
                sp.dma_start(fx[s], slot_x[p][bass.ds(i * SL, SL), :]).then_inc(fx_loaded[s], 16)

            def store_fy(p, i, s):
                sp.wait_ge(y_biased, i + (p * NT + 1))
                sp.dma_start(slot_y[p][bass.ds(i * SL, SL), :], fy[s]).then_inc(fy_stored[s], 16)

            def all_sent(p):
                for s in range(2):
                    sp.wait_ge(sent[s], 32 * (p + 1) * (JT // 2))

            AHEAD = 4

            def combine_io(p):
                def load_h1(j, s):
                    sp.dma_start(gh[s][:, :], h1_rows[bass.ds(p * JT + j, 1), :, :].rearrange("o p d -> (o p) d")
                                 ).then_inc(gh_loaded[s], 16)

                def store_out(j, s):
                    sp.wait_ge(combined, p * JT + j + 1)
                    rows = out.rearrange("b l d -> (b l) d").rearrange("(k q) d -> k q d", q=TT)
                    sp.dma_start(rows[bass.ds(p * JT + j, 1), :, :].rearrange("o p d -> (o p) d"), go[s][:, :]
                                 ).then_inc(out_stored[s], 16)

                for s in range(2):
                    if p:
                        sp.wait_ge(combined, p * JT)
                    load_h1(s, s)
                with sp.Fori(0, JT // 2 - 1) as i:
                    for s in range(2):
                        store_out(2 * i + s, s)
                        load_h1(2 * i + (2 + s), s)
                for s in range(2):
                    store_out(JT - 2 + s, s)

            all_sent(0)
            for k in range(AHEAD):
                load_fx(0, k, k % 2)
            for p in range(PARTS):
                with sp.Fori(0, (NT - AHEAD) // 2) as i:
                    for s in range(2):
                        load_fx(p, 2 * i + (AHEAD + s), s)
                        store_fy(p, 2 * i + s, s)
                if p + 1 < PARTS:
                    all_sent(p + 1)
                for k in range(AHEAD):
                    if p + 1 < PARTS:
                        load_fx(p + 1, k, k % 2)
                    store_fy(p, NT - AHEAD + k, k % 2)
            for p in range(PARTS):
                combine_io(p)
            for s in range(2):
                sp.wait_ge(out_stored[s], 16 * PARTS * JT // 2)

        @block.tensor
        def _(pe):
            mm = nc.tensor.matmul

            def turn(dst, src):
                return mm(dst, src, ident, start=True, stop=True, is_transpose=True)

            def tokens(g):
                pe.wait_ge(x_loaded[g.parity], 32 * g.before + 32)
                if not (isinstance(g.n, int) and g.n < 2):
                    pe.wait_ge(y_sum, NC * (g.n - 1))
                ps = b_tok[:, 0:GI * NPATCH]
                for k in range(KC):
                    mm(ps, wt[:, k, :], xm[g.parity][:, k, :], start=(k == 0), stop=False)
                mm(ps, wtt[:, :], xt[g.parity][:, :], start=False, stop=True).then_inc(tok_summed, 1)

            def ln1_center(g):
                pe.wait_ge(h_ready, g.n + 1)
                mm(b_c[:, 0:T], center, h[g.parity][:, :], start=True, stop=True).then_inc(ln_centered, 1)

            def ln1_var(g):
                pe.wait_ge(ln_squared, g.n + 1)
                mm(b_v[:, 0:T], mean, ln_sq[:, :], start=True, stop=True).then_inc(ln_var, 1)

            def dt_project(g):
                pe.wait_ge(xn_ready, g.n + 1)
                if not g.first():
                    pe.wait_ge(inter_read, 2 * g.n)
                for c in range(NC):
                    for i in range(GI):
                        o = (c * GI + i) * HEADS
                        last = mm(b_dt[0:Q, o:o + HEADS], xn[g.parity][:, i * L + c * Q:i * L + (c + 1) * Q], wdt[:, :],
                                  start=True, stop=True)
                last.then_inc(dt_raw, 1)

            def project(g, k):
                if k >= 4:
                    pe.wait_ge(conv_step, N_CONV * g.n + conv_all(k - 4))
                elif not g.first():
                    if k == 0:
                        pe.wait_ge(m_ready, NC * GI * g.n)
                    elif k == 1:
                        pe.wait_ge(inter_read, 2 * g.n)
                    else:
                        pe.wait_ge(y_sum, NC * (g.n - 1) + (1 if k == 2 else NC))
                mm(RING[k % 4][:, 0:T], win[:, k, :], xn[g.parity][:, :], start=True, stop=True).then_inc(proj, 1)

            def segments(g, c):
                if c == 0:
                    pe.wait_ge(seg_ready, g.n + 1)
                else:
                    pe.wait_ge(decay_ready, NC * g.n + c)
                n = GI * HEADS
                mm(b_dt[0:QR, 0:n * Q], c88[0:32 + Q, S_SEG:S_SEG + QR], seg_r[:, c * n:(c + 1) * n, :],
                   start=True, stop=True).then_inc(seg_summed, 1)

            def spread_dt(g):
                pe.wait_ge(decay_ready, NC * (g.n + 1))
                pe.wait_ge(dt_widened, g.n + 1)
                for c in range(NC):
                    for i in range(GI):
                        o = i * 5 * Q + (0, Q, 3 * Q)[c]
                        n = Q if c == 0 else 2 * Q
                        mm(b_dt[:, o:o + n], dt_wide[:, c * GI + i, :], c88[0:Q, S_IT:S_IT + n], start=True, stop=True)
                o = GI * 5 * Q
                mm(b_dt[0:QR, o:o + GI * HEADS], c88[0:Q, S_ONE:S_ONE + QR], da_s[:, 1, :, :].rearrange("p i h -> p (i h)"),
                   start=True, stop=True).then_inc(spread, 1)

            def out_project(g):
                pe.wait_ge(yg_ready, g.n + 1)
                for r in range(RANK):
                    last = mm(b_c[:, 0:T], wo[:, r, :], yg[:, r, :], start=(r == 0), stop=(r == RANK - 1))
                last.then_inc(out_proj, 1)

            def res_mean(g):
                pe.wait_ge(res_squared, g.n + 1)
                mm(b_v[:, 0:T], mean, po_sq[:, :], start=True, stop=True).then_inc(res_var, 1)

            def post_center(g):
                pe.wait_ge(h1_ready, g.n + 1)
                mm(b_c[:, 0:T], center, h1[:, :], start=True, stop=True).then_inc(po_centered, 1)

            def post_var(g):
                pe.wait_ge(po_squared, g.n + 1)
                mm(b_v[:, 0:T], mean, po_sq[:, :], start=True, stop=True).then_inc(po_var, 1)

            def rows_and_logits(g):
                pe.wait_ge(xs_ready, g.n + 1)
                for k in range(TPG):
                    turn(b_c[0:TT, k * D:(k + 1) * D], xs[:, k * TT:(k + 1) * TT])
                for k in range(TPG):
                    mm(b_c[0:TT, TPG * D + k * E_N:TPG * D + (k + 1) * E_N], xs[:, k * TT:(k + 1) * TT], gw[:, :],
                       start=True, stop=True)
                for k in range(TPG):
                    last = turn(b_v[0:TT, k * D:(k + 1) * D], h1[:, k * TT:(k + 1) * TT])
                last.then_inc(rows_turned, 1)

            def turn_x(g):
                pe.wait_ge(z_act, RANK * (g.n + 1))
                for c in range(NC):
                    pe.wait_ge(xdt_ready, NC * g.n + c + 1)
                    for i in range(GI):
                        last = turn(XT_B[c][0:QR, i * D:(i + 1) * D], xdt[:, c, i, :])
                    last.then_inc(x_turned, 1)

            def turn_b(g):
                pe.wait_ge(b_act, g.n + 1)
                pe.wait_ge(grow_ready, g.n + 1)
                pe.wait_ge(total_ready, g.n + 1)
                for c in range(2):
                    for i in range(GI):
                        last = turn(BT_B[c][0:QR, i * D:(i + 1) * D], bc[:, i, c, :])
                    last.then_inc(b_turned, 1)

            def score(g, c):
                if c == 0:
                    pe.wait_ge(c_act, g.n + 1)
                    if not is_last(g):
                        pe.wait_ge(h_ready, g.n + 2)
                else:
                    pe.wait_ge(x_turned_copied, NC * g.n + c)
                for i in range(GI):
                    last = mm(G_B[c][0:QR, i * QR:(i + 1) * QR], bc[:, i, c, :], cc[:, i, c, :], start=True, stop=True)
                last.then_inc(scores, 1)

            def state_sums(g):
                pe.wait_ge(xe_ready, g.n + 1)
                pe.wait_ge(b_turned_copied, 2 * (g.n + 1))
                pe.wait_ge(x_turned_copied, NC * (g.n + 1))
                n = HEADS * PC
                for i in range(GI):
                    o = 2 * i * n
                    mm(H_B[:, o:o + n], b_t[:, 0, i, :], xe[:, 0, i, :], start=True, stop=True)
                    mm(H_B[:, o + n:o + 2 * n], b_t[:, 0, i, :], xe[:, 2, i, :], start=True, stop=False)
                    last = mm(H_B[:, o + n:o + 2 * n], b_t[:, 1, i, :], xe[:, 1, i, :], start=False, stop=True)
                last.then_inc(states, 1)

            def inter_products(g):
                pe.wait_ge(states_copied, g.n + 1)
                for c in (1, 2):
                    for i in range(GI):
                        last = mm(I_B[c - 1][:, i * QR:(i + 1) * QR], hs[:, i, c - 1, :, :], cc[:, i, c, :],
                                  start=True, stop=True)
                    last.then_inc(inter, 1)

            def intra_products(g, c):
                for i in range(GI):
                    pe.wait_ge(m_ready, NC * GI * g.n + c * GI + i + 1)
                    for k in range(HEADS):
                        last = mm(Y_B[c][HP * k:HP * (k + 1), i * QR:(i + 1) * QR], xdt_t[:, c, i, HP * k:HP * (k + 1)],
                                  m[:, c, i, k, :], start=True, stop=True)
                last.then_inc(intra, 1)

            def body(g):
                more, before = not is_last(g), not g.first()
                dt_project(g)
                for k in range(4):
                    project(g, k)
                if before:
                    out_project(g.last())
                project(g, 4)
                project(g, 5)
                segments(g, 0)
                project(g, 6)
                project(g, 7)
                if before:
                    res_mean(g.last())
                segments(g, 1)
                project(g, 8)
                project(g, 9)
                segments(g, 2)
                if before:
                    post_center(g.last())
                project(g, 10)
                project(g, 11)
                if before:
                    post_var(g.last())
                spread_dt(g)
                project(g, 12)
                project(g, 13)
                if before:
                    rows_and_logits(g.last())
                project(g, 14)
                project(g, 15)
                if more:
                    tokens(g.next())
                turn_x(g)
                if more:
                    if before:
                        pe.wait_ge(rows_copied, g.n)
                    ln1_center(g.next())
                turn_b(g)
                for c in range(NC):
                    score(g, c)
                if more:
                    ln1_var(g.next())
                state_sums(g)
                inter_products(g)
                for c in range(NC):
                    intra_products(g, c)

            pe.wait_ge(loaded, N_LOADS)
            g0 = Group(0, 0, 0)
            tokens(g0)
            ln1_center(g0)
            ln1_var(g0)
            over_groups(pe, body)
            last_g = Group(NG - 1, 1, (NG - 2) // 2)
            out_project(last_g)
            res_mean(last_g)
            post_center(last_g)
            post_var(last_g)
            rows_and_logits(last_g)

            def route(p):
                pe.wait_ge(route_step, R_BOTH + p * N_ROUTE)
                flat = both[:, :, :].rearrange("p j e -> p (j e)")
                mm(b_tok[0:TT, 0:JT * E_N], c88[:, S_UP:S_UP + TT], flat, start=True, stop=True)
                mm(b_tok[0:TT, JT * E_N:2 * JT * E_N], c88[:, S_ONES:S_ONES + TT], flat, start=True, stop=True
                   ).then_inc(route_mm, 1)

            for p in range(PARTS):
                route(p)

            FT, FH, FY = [bank[0], bank[1]], [bank[2], bank[3]], [bank[4], bank[5]]

            def turn_rows(n, s, before):
                pe.wait_ge(fx_loaded[s], before * 16 + 16)
                turn(FT[s][:, 0:SL], fx[s]).then_inc(fx_turned, 1)

            def up(n, s):
                pe.wait_ge(fx_copied, n + 1)
                pe.wait_ge(w1_staged, n + 1)
                for k in range(FC):
                    last = mm(FH[s][:, k * SL:(k + 1) * SL], fw1[s][:, k * D:(k + 1) * D], fxt[s], start=True, stop=True)
                last.then_inc(hidden_mm, 1)

            def down(n, s, first=False):
                pe.wait_ge(hidden_act, n + 1)
                pe.wait_ge(w2_staged, n + 1)
                if not first:
                    pe.wait_ge(y_biased, n - 1)
                for k in range(FC):
                    last = mm(FY[s][:, 0:D], fh[s][:, k, :], fw2[s][:, k * D:(k + 1) * D], start=(k == 0), stop=(k == FC - 1))
                last.then_inc(y_mm, 1)

            pe.wait_ge(routed, PARTS)
            n = PARTS * NT
            turn_rows(0, 0, 0)
            turn_rows(1, 1, 0)
            up(0, 0)
            turn_rows(2, 0, 1)
            up(1, 1)
            down(0, 0, first=True)
            turn_rows(3, 1, 1)
            up(2, 0)
            down(1, 1, first=True)
            with pe.Fori(0, (n - 4) // 2) as i:
                turn_rows(2 * i + 4, 0, i + 2)
                up(2 * i + 3, 1)
                down(2 * i + 2, 0)
                turn_rows(2 * i + 5, 1, i + 2)
                up(2 * i + 4, 0)
                down(2 * i + 3, 1)
            up(n - 1, 1)
            down(n - 2, 0)
            down(n - 1, 1)

        @block.scalar
        def _(act):
            A = nc.scalar.activation

            def log_exp():
                nc.scalar.preload_act_table_set("natural_log_exp_and_others")

            def rstd(dst, var, ready, n, log_sem, out_sem):
                act.wait_ge(ready, n)
                A(dst, var, ACT.Ln, bias=eps[:, :]).then_inc(log_sem, 1)
                act.wait_ge(log_sem, n)
                A(dst, dst, ACT.Exp, scale=-0.5).then_inc(out_sem, 1)

            def ln1_square(g):
                act.wait_ge(ln_centered, g.n + 1)
                A(ln_sq[:, :], b_c[:, 0:T], ACT.Square).then_inc(ln_squared, 1)

            def ln1_rstd(g):
                rstd(ln_rs[:, :], b_v[:, 0:T], ln_var, g.n + 1, ln_log, ln_rstd)

            def dt_exponent(g):
                act.wait_ge(dt_step, N_DT * g.n + DT_NEG)
                A(de[:, :], dn[:, :], ACT.Exp).then_inc(dt_exp, 1)

            def first_tap(g, k):
                act.wait_ge(proj, 16 * g.n + k + 1)
                A(acc[:, k, :], RING[k % 4][:, 0:T], ACT.Identity, bias=cv[:, k, TAPS:TAPS + 1],
                  scale=cv[:, k, TAPS - 1:TAPS]).then_inc(tap0, 1)

            def decays(g, c):
                act.wait_ge(seg_summed, NC * g.n + c + 1)
                A(decay[:, c, :, :, :].rearrange("p i h t -> p (i h t)"), b_dt[0:QR, 0:GI * HEADS * Q], ACT.Exp
                  ).then_inc(decay_ready, 1)

            def growths(g):
                act.wait_ge(spread, g.n + 1)
                v = b_dt[:, 0:GI * 5 * Q].rearrange("p (i s t) -> p i s t", i=GI, s=5)
                A(grow[:, 0, :, :], v[:, :, 2, :], ACT.Exp, scale=nega_c[:, :])
                A(grow[:, 1, :, :], v[:, :, 4, :], ACT.Exp, scale=nega_c[:, :]).then_inc(grow_ready, 1)
                o = GI * 5 * Q
                A(total[:, :, :].rearrange("p i h -> p (i h)"), b_dt[0:QR, o:o + GI * HEADS], ACT.Exp).then_inc(total_ready, 1)

            def silu_chunk(g, dst, k0, done):
                act.wait_ge(conv_step, N_CONV * g.n + conv_all(k0 + RANK - 1))
                if not g.first():
                    act.wait_ge(y_sum, NC * g.n)
                for r in range(RANK):
                    v = by_chunk(dst[:, :, :, :])[:, :, :, r]
                    last = A(v, acc[:, k0 + r, :].rearrange("p (i t) -> p i t", i=GI), ACT.Silu)
                last.then_inc(done, 1)

            def silu_gate(g, r):
                act.wait_ge(proj, 16 * g.n + NCH + r + 1)
                if not g.first():
                    act.wait_ge(yg_ready, g.n)
                A(sz[:, r, :], RING[(NCH + r) % 4][:, 0:T], ACT.Silu).then_inc(z_act, 1)

            def copy_rows(g):
                act.wait_ge(rows_turned, g.n + 1)
                if not g.first():
                    act.wait_ge(rows_stored, 16 * g.n)
                A(xs_all[:, bass.ds(g.n * TPG, TPG), :].rearrange("p k d -> p (k d)"), b_c[0:TT, 0:TPG * D], ACT.Copy)
                A(logit[:, bass.ds(g.n, 1), :].rearrange("p o k -> p (o k)"), b_c[0:TT, TPG * D:TPG * (D + E_N)], ACT.Copy)
                A(h1_t[:, :], b_v[0:TT, 0:TPG * D], ACT.Copy).then_inc(rows_copied, 1)

            def copy_turned_x(g, c):
                act.wait_ge(x_turned, NC * g.n + c + 1)
                A(xdt_t[:, c, :, :].rearrange("p i d -> p (i d)"), XT_B[c][0:QR, 0:GI * D], ACT.Copy).then_inc(x_turned_copied, 1)

            def copy_turned_b(g):
                for c in range(2):
                    act.wait_ge(b_turned, 2 * g.n + c + 1)
                    A(b_t[:, c, :, :].rearrange("p i d -> p (i d)"), BT_B[c][0:QR, 0:GI * D], ACT.Copy
                      ).then_inc(b_turned_copied, 1)

            def copy_states(g):
                act.wait_ge(states, g.n + 1)
                A(hs[:, :, :, :, 0:PC].rearrange("p i c h q -> p (i c h) q"),
                  H_B[:, 0:GI * 2 * HEADS * PC].rearrange("p (k q) -> p k q", q=PC), ACT.Copy).then_inc(states_copied, 1)

            def res_square(g):
                act.wait_ge(res_ready, g.n + 1)
                A(po_sq[:, :], res[:, :], ACT.Square).then_inc(res_squared, 1)

            def res_norm(g):
                rstd(po_rs[:, :], b_v[:, 0:T], res_var, g.n + 1, res_log, res_rstd)

            def post_square(g):
                act.wait_ge(po_centered, g.n + 1)
                A(po_sq[:, :], b_c[:, 0:T], ACT.Square).then_inc(po_squared, 1)

            def post_norm(g):
                rstd(po_rs[:, :], b_v[:, 0:T], po_var, g.n + 1, po_log, po_rstd)

            def body(g):
                more, before = not is_last(g), not g.first()
                dt_exponent(g)
                for k in range(4):
                    first_tap(g, k)
                if before:
                    res_square(g.last())
                first_tap(g, 4)
                first_tap(g, 5)
                decays(g, 0)
                first_tap(g, 6)
                first_tap(g, 7)
                if before:
                    res_norm(g.last())
                decays(g, 1)
                first_tap(g, 8)
                first_tap(g, 9)
                decays(g, 2)
                if before:
                    post_square(g.last())
                first_tap(g, 10)
                first_tap(g, 11)
                if before:
                    post_norm(g.last())
                growths(g)
                silu_chunk(g, xc, 0, x_act)
                silu_chunk(g, bc, 4, b_act)
                silu_gate(g, 0)
                silu_gate(g, 1)
                if before:
                    copy_rows(g.last())
                silu_gate(g, 2)
                silu_gate(g, 3)
                silu_chunk(g, cc, 8, c_act)
                log_exp()
                for c in range(NC):
                    copy_turned_x(g, c)
                if more:
                    ln1_square(g.next())
                copy_turned_b(g)
                if more:
                    ln1_rstd(g.next())
                copy_states(g)

            log_exp()
            act.wait_ge(loaded, N_LOADS)
            A(nega_r[:, :], dtr[:, HEADS:2 * HEADS], ACT.Exp)
            A(nega_c[:, :], dtc[:, 0:1], ACT.Exp).then_inc(nega_done, 1)
            act.wait_ge(nega_done, 1)
            A(nega_c[:, :], nega_c[:, :], ACT.Copy, scale=-1.0)
            A(nega_r[:, :], nega_r[:, :], ACT.Copy, scale=-1.0).then_inc(nega_done, 1)
            act.wait_ge(setup_done, 1)
            act.wait_ge(nega_done, 2)
            act.wait_ge(zeroed, 1 + 32 * PARTS)
            act.wait_ge(hs_zeroed, 1)
            g0 = Group(0, 0, 0)
            ln1_square(g0)
            ln1_rstd(g0)
            over_groups(act, body)
            last_g = Group(NG - 1, 1, (NG - 2) // 2)
            res_square(last_g)
            res_norm(last_g)
            post_square(last_g)
            post_norm(last_g)
            copy_rows(last_g)
            for p in range(PARTS):
                act.wait_ge(route_step, R_DIFF + p * N_ROUTE)
                A(rd[:, :], rd[:, :], ACT.Exp).then_inc(route_exp, 1)

            def hidden(n, s):
                act.wait_ge(hidden_mm, n + 1)
                for k in range(FC):
                    last = A(fh[s][:, k, :], bank[2 + s][:, k * SL:(k + 1) * SL], ACT.Relu,
                             bias=fw1[s][:, FF + k:FF + k + 1])
                last.then_inc(hidden_act, 1)

            hidden(0, 0)
            hidden(1, 1)
            with act.Fori(1, PARTS * NT // 2) as i:
                for s in range(2):
                    act.wait_ge(y_mm, 2 * i + (s - 1))
                    hidden(2 * i + s, s)

        @block.vector
        def _(dve):
            V = nc.vector

            def tokens_bias(g):
                dve.wait_ge(tok_summed, g.n + 1)
                V.scalar_tensor_tensor(
                    out=h[g.parity][:, :].rearrange("p (i t) -> p i t", i=GI)[:, :, 2:L],
                    in0=b_tok[:, 0:GI * NPATCH].rearrange("p (i t) -> p i t", i=GI), scalar=tcol[:, 0:1],
                    in1=tcol[:, 4:4 + NPATCH].rearrange("p (o t) -> p o t", o=1).broadcast_to([128, GI, NPATCH]),
                    op0=ALU.add, op1=ALU.mult).then_inc(h_ready, 1)

            def ln1_scale(g):
                dve.wait_ge(ln_rstd, g.n + 1)
                V.tensor_tensor(xn[g.parity][:, :], b_c[:, 0:T], ln_rs[:, :], ALU.mult).then_inc(xn_ready, 1)

            def dt_begin(g):
                dve.wait_ge(dt_raw, g.n + 1)
                n = NC * GI
                bias = dtr[:, 0:HEADS].rearrange("p (o h) -> p o h", o=1).broadcast_to([Q, n, HEADS])
                V.tensor_tensor(du[:, :].rearrange("p (n h) -> p n h", n=n), b_dt[0:Q, 0:n * HEADS].rearrange("p (n h) -> p n h", n=n),
                                bias, ALU.add).then_inc(dt_step, 1)
                dve.wait_ge(dt_step, N_DT * g.n + 1)
                V.scalar_tensor_tensor(out=dn[:, :], in0=du[:, :], scalar=-1.0, in1=du[:, :], op0=ALU.mult, op1=ALU.min
                                       ).then_inc(dt_step, 1)

            def dt_finish(g):
                done = [2]

                def link(ins):
                    done[0] += 1
                    ins.then_inc(dt_step, 1)
                    dve.wait_ge(dt_step, N_DT * g.n + done[0])

                dve.wait_ge(dt_exp, g.n + 1)
                link(V.tensor_scalar(dr[:, :], de[:, :], 2.0, None, ALU.add))
                link(V.reciprocal(dr[:, :], dr[:, :]))
                link(V.tensor_tensor(ds_[:, :], de[:, :], dr[:, :], ALU.mult))
                link(V.tensor_tensor(dq[:, :], ds_[:, :], ds_[:, :], ALU.mult))
                link(V.tensor_scalar(dp[:, :], dq[:, :], 1.0 / 15.0, None, ALU.mult))
                for k in (13, 11, 9, 7, 5, 3):
                    link(V.scalar_tensor_tensor(out=dp[:, :], in0=dp[:, :], scalar=1.0 / k, in1=dq[:, :], op0=ALU.add, op1=ALU.mult))
                link(V.scalar_tensor_tensor(out=dp[:, :], in0=dp[:, :], scalar=1.0, in1=ds_[:, :], op0=ALU.add, op1=ALU.mult))
                link(V.tensor_scalar(du[:, :], du[:, :], 0.0, None, ALU.max))
                link(V.scalar_tensor_tensor(out=dt_s[:, :, :, :].rearrange("p c i h -> p (c i h)"), in0=dp[:, :], scalar=2.0,
                                            in1=du[:, :], op0=ALU.mult, op1=ALU.add))
                n = NC * GI
                V.tensor_tensor(da_s[:, :, :, :].rearrange("p c i h -> p (c i) h"), dt_s[:, :, :, :].rearrange("p c i h -> p (c i) h"),
                                nega_r[:, :].rearrange("p (o h) -> p o h", o=1).broadcast_to([Q, n, HEADS]), ALU.mult
                                ).then_inc(dt_step, 1)

            def conv_pair(g, k0):
                for tap in range(1, TAPS):
                    for k in (k0, k0 + 1):
                        if tap == 1:
                            dve.wait_ge(tap0, NCH * g.n + k + 1)
                        else:
                            dve.wait_ge(conv_step, N_CONV * g.n + conv_at(k, tap - 1))
                        src = RING[k % 4][:, 0:T].rearrange("p (i t) -> p i t", i=GI)[:, :, 0:L - tap]
                        dst = acc[:, k, :].rearrange("p (i t) -> p i t", i=GI)[:, :, tap:L]
                        V.scalar_tensor_tensor(out=dst, in0=src, scalar=cv[:, k, TAPS - 1 - tap:TAPS - tap], in1=dst,
                                               op0=ALU.mult, op1=ALU.add).then_inc(conv_step, 1)

            def residual(g):
                dve.wait_ge(out_proj, g.n + 1)
                V.tensor_tensor(res[:, :], b_c[:, 0:T], xn[g.parity][:, :], ALU.add).then_inc(res_ready, 1)

            def residual_norm(g):
                dve.wait_ge(res_rstd, g.n + 1)
                V.tensor_tensor(res[:, :], res[:, :], po_rs[:, :], ALU.mult).then_inc(res_scaled, 1)
                dve.wait_ge(res_scaled, g.n + 1)
                V.tensor_tensor(h1[:, :], res[:, :], h[g.parity][:, :], ALU.add).then_inc(h1_ready, 1)

            def post_scale(g):
                dve.wait_ge(po_rstd, g.n + 1)
                V.tensor_tensor(xs[:, :], b_c[:, 0:T], po_rs[:, :], ALU.mult).then_inc(xs_ready, 1)

            def x_times_dt(g):
                dve.wait_ge(x_act, g.n + 1)
                dve.wait_ge(spread, g.n + 1)
                if not g.first():
                    dve.wait_ge(yg_ready, g.n)
                v = b_dt[:, 0:GI * 5 * Q].rearrange("p (i s t) -> p i s t", i=GI, s=5)
                for c in range(NC):
                    dt_v = v[:, :, (0, 1, 3)[c], :].rearrange("p i (t o) -> p i t o", o=1).broadcast_to([128, GI, Q, RANK])
                    V.tensor_tensor(xdt[:, c, :, :].rearrange("p i (t r) -> p i t r", r=RANK), dt_v,
                                    xc[:, :, c, :].rearrange("p i (t r) -> p i t r", r=RANK), ALU.mult).then_inc(xdt_ready, 1)

            def weigh(g, c):
                dve.wait_ge(scores, NC * g.n + c + 1)
                dve.wait_ge(decay_ready, NC * g.n + c + 1)
                if not g.first():
                    dve.wait_ge(intra, NC * (g.n - 1) + c + 1)
                for i in range(GI):
                    s = G_B[c][0:QR, i * QR:(i + 1) * QR].rearrange("p (o t r) -> p o t r", o=1, r=RANK)
                    d = decay[:, c, i, :, :].rearrange("p h (t o) -> p h t o", o=1)
                    V.tensor_tensor(m[:, c, i, :, :].rearrange("p h (t r) -> p h t r", r=RANK),
                                    s.broadcast_to([QR, HEADS, Q, RANK]), d.broadcast_to([QR, HEADS, Q, RANK]), ALU.mult
                                    ).then_inc(m_ready, 1)

            def scale_inter(g):
                for c in (1, 2):
                    dve.wait_ge(inter, 2 * g.n + c)
                    if not g.first() and c == 1:
                        dve.wait_ge(y_total, g.n)
                    gr = grow[:, c - 1, :, :].rearrange("p i (t o) -> p i t o", o=1).broadcast_to([128, GI, Q, RANK])
                    V.tensor_tensor(t1[:, c - 1, :, :].rearrange("p i (t r) -> p i t r", r=RANK),
                                    I_B[c - 1][:, 0:GI * QR].rearrange("p (i t r) -> p i t r", i=GI, r=RANK), gr, ALU.mult
                                    ).then_inc(inter_read, 1)

            def skip_and_intra(g, c):
                dve.wait_ge(intra, NC * g.n + c + 1)
                V.scalar_tensor_tensor(out=y[:, c, :, :], in0=xc[:, :, c, :], scalar=dtc[:, 1:2],
                                       in1=Y_B[c][:, 0:GI * QR].rearrange("p (i t) -> p i t", i=GI), op0=ALU.mult, op1=ALU.add
                                       ).then_inc(y_sum, 1)

            def body(g):
                more, before = not is_last(g), not g.first()
                dt_begin(g)
                conv_pair(g, 0)
                dt_finish(g)
                conv_pair(g, 2)
                if before:
                    residual(g.last())
                conv_pair(g, 4)
                if before:
                    residual_norm(g.last())
                conv_pair(g, 6)
                conv_pair(g, 8)
                if before:
                    post_scale(g.last())
                conv_pair(g, 10)
                x_times_dt(g)
                if more:
                    tokens_bias(g.next())
                weigh(g, 0)
                weigh(g, 1)
                if more:
                    ln1_scale(g.next())
                weigh(g, 2)
                scale_inter(g)
                for c in range(NC):
                    skip_and_intra(g, c)

            V.memset(eps[:, :], EPS).then_inc(setup_done, 1)
            V.memset(ones_e[:, :], 1.0).then_inc(setup_done, 1)
            dve.wait_ge(loaded, N_LOADS)
            for par in range(2):
                hv = h[par][:, :].rearrange("p (i t) -> p i t", i=GI)
                V.tensor_copy(hv[:, :, 0:1], tcol[:, 1:2].rearrange("p (o t) -> p o t", o=1).broadcast_to([128, GI, 1]))
                V.tensor_scalar(hv[:, :, 1:2], tcol[:, 3:4].rearrange("p (o t) -> p o t", o=1).broadcast_to([128, GI, 1]),
                                tcol[:, 2:3], None, ALU.mult)
            dve.wait_ge(nega_done, 2)
            g0 = Group(0, 0, 0)
            tokens_bias(g0)
            ln1_scale(g0)
            over_groups(dve, body)
            last_g = Group(NG - 1, 1, (NG - 2) // 2)
            residual(last_g)
            residual_norm(last_g)
            post_scale(last_g)

            def route(p):
                done = [p * N_ROUTE]

                def link(ins):
                    done[0] += 1
                    ins.then_inc(route_step, 1)
                    dve.wait_ge(route_step, done[0])

                lg = logit[:, p * GPP:(p + 1) * GPP, :].rearrange("p g (k e) -> p (g k) e", e=E_N)
                full = [TT, JT, E_N]

                def row(col):
                    return c88[:, col:col + E_N].rearrange("p (o e) -> p o e", o=1).broadcast_to(full)

                def per_token(t):
                    return t.rearrange("p (j o) -> p j o", o=1).broadcast_to(full)

                src = lg
                for k in range(2):
                    link(V.tensor_reduce(top[k][:, :], src, AX.X, ALU.max))
                    link(V.tensor_tensor(ra[:, :, :], src, per_token(top[k][:, :]), ALU.is_equal))
                    link(V.scalar_tensor_tensor(out=ra[:, :, :], in0=ra[:, :, :], scalar=-float(E_N), in1=row(S_IOTA8),
                                                op0=ALU.mult, op1=ALU.add))
                    link(V.tensor_reduce(idx[:, :], ra[:, :, :], AX.X, ALU.min))
                    link(V.tensor_tensor(onehot[k][:, :, :], row(S_IOTA), per_token(idx[:, :]), ALU.is_equal))
                    if k == 0:
                        link(V.scalar_tensor_tensor(out=rb[:, :, :], in0=onehot[0][:, :, :], scalar=-HIDDEN, in1=lg,
                                                    op0=ALU.mult, op1=ALU.add))
                        src = rb[:, :, :]
                link(V.tensor_tensor(both[:, :, :], onehot[0][:, :, :], onehot[1][:, :, :], ALU.add))
                assert done[0] == p * N_ROUTE + R_BOTH, done
                link(V.tensor_scalar(slot_f[:, :], top[0][:, :], -1.0, None, ALU.mult))
                link(V.tensor_tensor(rd[:, :], top[1][:, :], slot_f[:, :], ALU.add))
                assert done[0] == p * N_ROUTE + R_DIFF, done
                dve.wait_ge(route_exp, p + 1)
                link(V.tensor_scalar(idx[:, :], rd[:, :], 1.0, None, ALU.add))
                link(V.reciprocal(wgt[0][:, p, :], idx[:, :]))
                link(V.tensor_tensor(wgt[1][:, p, :], rd[:, :], wgt[0][:, p, :], ALU.mult))
                dve.wait_ge(route_mm, p + 1)
                n = JT * E_N
                link(V.tensor_copy(rtot[:, :, :], b_tok[0:TT, n:2 * n].rearrange("p (j e) -> p e j", e=E_N)))
                link(V.tensor_tensor_scan(rsum[:, :, :].rearrange("p e j -> p (e j)"), c88[:, S_MASK:S_MASK + n],
                                          rtot[:, :, :].rearrange("p e j -> p (e j)"), 0.0, ALU.mult, ALU.add))
                kfull = [TT, E_N, KMAX]
                link(V.tensor_tensor(cmp_k[:, :, :], rsum[:, :, JT - 1:JT].broadcast_to(kfull),
                                     c88[:, S_KIO:S_KIO + E_N * KMAX].rearrange("p (e k) -> p e k", e=E_N), ALU.is_gt))
                link(V.tensor_reduce(ntile[:, :], cmp_k[:, :, :], AX.X, ALU.add))
                link(V.tensor_tensor_scan(endt[:, :], ones_e[:, :], ntile[:, :], 0.0, ALU.mult, ALU.add))
                link(V.tensor_tensor(base[:, :], endt[:, :], ntile[:, :], ALU.subtract))
                tfull = [TT, NT, E_N]
                link(V.tensor_tensor(cmp_t[:, :, :], c88[:, S_TIO:S_TIO + NT * E_N].rearrange("p (t e) -> p t e", e=E_N),
                                     endt[:, :].rearrange("p (o e) -> p o e", o=1).broadcast_to(tfull), ALU.is_ge))
                link(V.tensor_reduce(tile_f[:, :], cmp_t[:, :, :], AX.X, ALU.add))
                link(V.tensor_scalar(tile_e[0:1, p, :], tile_f[0:1, :], float(E_N - 1), None, ALU.min))
                link(V.tensor_tensor(rsum[:, :, :], rsum[:, :, :], rtot[:, :, :], ALU.subtract))
                assert done[0] == (p + 1) * N_ROUTE, done
                V.tensor_tensor(ra[:, :, :], b_tok[0:TT, 0:n].rearrange("p (j e) -> p j e", e=E_N),
                                rsum[:, :, :].rearrange("p e j -> p j e"), ALU.add).then_inc(slot_step, 1)
                dve.wait_ge(slot_step, 7 * p + 1)
                V.scalar_tensor_tensor(out=ra[:, :, :], in0=base[:, :].rearrange("p (o e) -> p o e", o=1).broadcast_to(full),
                                       scalar=float(SL), in1=ra[:, :, :], op0=ALU.mult, op1=ALU.add).then_inc(slot_step, 1)
                dve.wait_ge(slot_step, 7 * p + 2)
                V.tensor_tensor(rb[:, :, :], ra[:, :, :], onehot[0][:, :, :], ALU.mult)
                V.tensor_tensor(both[:, :, :], ra[:, :, :], onehot[1][:, :, :], ALU.mult).then_inc(slot_step, 1)
                dve.wait_ge(slot_step, 7 * p + 3)
                for k, src in enumerate((rb, both)):
                    V.tensor_reduce(slot_f[:, :], src[:, :, :], AX.X, ALU.add).then_inc(slot_step, 1)
                    dve.wait_ge(slot_step, 7 * p + 4 + 2 * k)
                    V.tensor_copy(slot_u[k][:, p, :], slot_f[:, :]).then_inc(slot_step, 1)
                    dve.wait_ge(slot_step, 7 * p + 5 + 2 * k)
                V.tensor_copy(idx[:, :], slot_f[:, :]).then_inc(routed, 1)
                dve.wait_ge(routed, p + 1)

            dve.wait_ge(rows_copied, NG)
            for p in range(PARTS):
                route(p)

            tiles = tile_e[:, :, :].rearrange("o p t -> o (p t)")

            def expert(n):
                return dve.value_load(tiles[0:1, bass.ds(n, 1)], min_val=0, max_val=E_N - 1)

            def turned(n, s):
                dve.wait_ge(fx_turned, n + 1)
                if not isinstance(n, int) or n >= 2:
                    dve.wait_ge(hidden_mm, n - 1)
                V.tensor_copy(fxt[s], bank[s][:, 0:SL]).then_inc(fx_copied, 1)

            def stage_w1(n, s):
                e = expert(n)
                if not isinstance(n, int) or n >= 2:
                    dve.wait_ge(hidden_act, n - 1)
                V.tensor_copy(fw1[s], wall[:, bass.ds(e, 1), 0:W1C].rearrange("p o c -> p (o c)")).then_inc(w1_staged, 1)

            def stage_w2(n, s):
                e = expert(n)
                if not isinstance(n, int) or n >= 2:
                    dve.wait_ge(y_biased, n - 1)
                V.tensor_copy(fw2[s], wall[:, bass.ds(e, 1), W1C:WCOLS].rearrange("p o c -> p (o c)")).then_inc(w2_staged, 1)

            def add_bias(n, s, before):
                dve.wait_ge(y_mm, n + 1)
                if not isinstance(before, int) or before:
                    dve.wait_ge(fy_stored[s], before * 16)
                V.tensor_tensor(fy[s], bank[4 + s][:, 0:D], fw2[s][:, FF:W2C], ALU.add).then_inc(y_biased, 1)

            dve.wait_ge(experts_loaded, 16)
            n = PARTS * NT
            turned(0, 0)
            stage_w1(0, 0)
            turned(1, 1)
            stage_w1(1, 1)
            stage_w2(0, 0)
            turned(2, 0)
            stage_w1(2, 0)
            stage_w2(1, 1)
            with dve.Fori(0, (n - 4) // 2) as i:
                turned(2 * i + 3, 1)
                stage_w1(2 * i + 3, 1)
                add_bias(2 * i, 0, i)
                stage_w2(2 * i + 2, 0)
                turned(2 * i + 4, 0)
                stage_w1(2 * i + 4, 0)
                add_bias(2 * i + 1, 1, i)
                stage_w2(2 * i + 3, 1)
            turned(n - 1, 1)
            stage_w1(n - 1, 1)
            add_bias(n - 4, 0, n // 2 - 2)
            stage_w2(n - 2, 0)
            add_bias(n - 3, 1, n // 2 - 2)
            stage_w2(n - 1, 1)
            add_bias(n - 2, 0, n // 2 - 1)
            add_bias(n - 1, 1, n // 2 - 1)

            def combine(p, j, s, k):
                dve.wait_ge(gathered[s], k * 32 + 32)
                dve.wait_ge(gh_loaded[s], k * 16 + 16)
                V.scalar_tensor_tensor(out=gh[s][:, :], in0=gy[s][0][:, :], scalar=wgt[0][:, p, bass.ds(j, 1)], in1=gh[s][:, :],
                                       op0=ALU.mult, op1=ALU.add).then_inc(first_added, 1)
                dve.wait_ge(first_added, 2 * k + (s + 1))
                if not (isinstance(k, int) and k == 0):
                    dve.wait_ge(out_stored[s], k * 16)
                V.scalar_tensor_tensor(out=go[s][:, :], in0=gy[s][1][:, :], scalar=wgt[1][:, p, bass.ds(j, 1)], in1=gh[s][:, :],
                                       op0=ALU.mult, op1=ALU.add).then_inc(combined, 1)

            for p in range(PARTS):
                for s in range(2):
                    combine(p, s, s, p * JT // 2)
                with dve.Fori(1, JT // 2) as i:
                    for s in range(2):
                        combine(p, 2 * i + s, s, i + p * JT // 2)

        @block.gpsimd
        def _(pool):
            P = nc.gpsimd

            def segment_rows(g):
                pool.wait_ge(dt_step, N_DT * g.n + DT_A)
                if not g.first():
                    pool.wait_ge(seg_summed, NC * g.n)
                n = NC * GI * HEADS
                a = da_s[:, :, :, :].rearrange("p c i (h o) -> p (c i h) o", o=1).broadcast_to([Q, n, Q])
                tri = c88[0:Q, S_IT + Q:S_IT + 2 * Q].rearrange("p (o t) -> p o t", o=1).broadcast_to([Q, n, Q])
                P.tensor_tensor(seg_r[0:Q, :, :], a, tri, ALU.mult).then_inc(seg_ready, 1)
                P.tensor_copy(dt_wide[:, :, :].rearrange("p n (h q) -> p (n h) q", q=HP),
                              dt_s[:, :, :, :].rearrange("p c i (h o) -> p (c i h) o", o=1).broadcast_to([Q, n, HP])
                              ).then_inc(dt_widened, 1)

            def x_to_end(g):
                n = GI * HEADS
                for c in range(2):
                    pool.wait_ge(x_turned_copied, NC * g.n + c + 1)
                    if c == 0 and not g.first():
                        pool.wait_ge(states, g.n)
                    d = decay[:, c, :, :, Q - 1:Q].rearrange("p i h o -> p (i h) o").broadcast_to([QR, n, PC])
                    x = xdt_t[:, c, :, :].rearrange("p i (h q) -> p (i h) q", q=HP)[:, :, 0:PC]
                    P.tensor_tensor(xe[:, c, :, :].rearrange("p i (h q) -> p (i h) q", q=PC), x, d, ALU.mult).then_inc(xe_part, 1)
                pool.wait_ge(xe_part, 2 * g.n + 2)
                pool.wait_ge(total_ready, g.n + 1)
                t = total[:, :, :].rearrange("p i (h o) -> p (i h) o", o=1).broadcast_to([QR, n, PC])
                P.tensor_tensor(xe[:, 2, :, :].rearrange("p i (h q) -> p (i h) q", q=PC),
                                xe[:, 0, :, :].rearrange("p i (h q) -> p (i h) q", q=PC), t, ALU.mult).then_inc(xe_ready, 1)

            def gate(g):
                pool.wait_ge(y_sum, NC * (g.n + 1))
                pool.wait_ge(inter_read, 2 * (g.n + 1))
                v = y[:, 1:NC, :, :].rearrange("p c i t -> p (c i t)")
                P.tensor_tensor(v, v, t1[:, :, :, :].rearrange("p c i t -> p (c i t)"), ALU.add).then_inc(y_total, 1)
                pool.wait_ge(y_total, g.n + 1)
                pool.wait_ge(z_act, RANK * (g.n + 1))
                if not g.first():
                    pool.wait_ge(out_proj, g.n)
                for c in range(NC):
                    o = yg[:, :, :].rearrange("p r (i k t) -> p r i k t", i=GI, k=NC)[:, :, :, c, :].rearrange("p r i t -> p i t r")
                    z = sz[:, :, :].rearrange("p r (i k t) -> p r i k t", i=GI, k=NC)[:, :, :, c, :].rearrange("p r i t -> p i t r")
                    last = P.tensor_tensor(o, y[:, c, :, :].rearrange("p i (t r) -> p i t r", r=RANK), z, ALU.mult)
                last.then_inc(yg_ready, 1)

            P.memset(acc[:, :, :], 0.0)
            P.memset(hs[:, :, :, :, :], 0.0).then_inc(hs_zeroed, 1)
            pool.wait_ge(hs_zeroed, 1)
            P.memset(xe[0:QR, 0, 0, 0:1], 0.0).then_inc(zeroed, 1)
            pool.wait_ge(zeroed, 1)
            pool.wait_ge(loaded, N_LOADS)

            def body(g):
                segment_rows(g)
                x_to_end(g)
                gate(g)

            over_groups(pool, body)

            def take_wait():
                P.tensor_tensor(mark[0:1, 0:1], c88[0:1, 0:1], c88[0:1, 0:1], ALU.add)

            def send(p, j, s, k):
                if not (isinstance(k, int) and k == 0):
                    pool.wait_ge(sent[s], k * 32)
                for q in range(2):
                    P.tensor_copy(sc_i[s][q][:, :], slot_u[q][:, p, bass.ds(j, 1)])
                P.tensor_copy(sc_x[s][:, :], xs_all[:, bass.ds(p * JT + j, 1), :].rearrange("p o d -> p (o d)")).then_inc(sc_copied, 1)
                pool.wait_ge(sc_copied, 2 * k + (s + 1))
                take_wait()
                for q in range(2):
                    P.indirect_dma_start(slot_x[p], bass.IndirectOffsetOnAxis(ap=sc_i[s][q][:, 0:1], axis=0), sc_x[s][:, :], None
                                         ).then_inc(sent[s], 16)

            def gather(p, j, s, k):
                if not (isinstance(k, int) and k == 0):
                    pool.wait_ge(combined, 2 * k + (s - 1))
                for q in range(2):
                    last = P.tensor_copy(gi[s][q][:, :], slot_u[q][:, p, bass.ds(j, 1)])
                last.then_inc(ga_index, 1)
                pool.wait_ge(ga_index, 2 * k + (s + 1))
                take_wait()
                for q in range(2):
                    P.indirect_dma_start(gy[s][q][:, :], None, slot_y[p], bass.IndirectOffsetOnAxis(ap=gi[s][q][:, 0:1], axis=0)
                                         ).then_inc(gathered[s], 16)

            def over_tiles(p, step):
                for s in range(2):
                    step(p, s, s, p * JT // 2)
                with pool.Fori(1, JT // 2) as i:
                    for s in range(2):
                        step(p, 2 * i + s, s, i + p * JT // 2)

            pool.wait_ge(routed, PARTS)
            pool.wait_ge(zeroed, 1 + 32 * PARTS)
            for p in range(PARTS):
                over_tiles(p, send)
            for p in range(PARTS):
                for s in range(2):
                    pool.wait_ge(fy_stored[s], 16 * (p + 1) * NT // 2)
                over_tiles(p, gather)
            for s in range(2):
                pool.wait_ge(gathered[s], 32 * PARTS * JT // 2)


def kernel(**inputs):
    import concourse.bacc as bacc
    from concourse.bass_utils import run_bass_kernel_spmd

    a = {k: np.ascontiguousarray(v) for k, v in inputs.items()}
    side = 224 // PATCH

    x = a["x"].reshape(NG, GI, CH, side, PATCH, side, PATCH).transpose(0, 2, 4, 6, 1, 3, 5).reshape(NG, K_TOK, GI * NPATCH)
    x_main = x[:, :KC * D].reshape(NG, KC, D, GI * NPATCH).transpose(0, 2, 1, 3).reshape(NG, D, KC * GI * NPATCH)
    w = a["L0_tok_W"].T
    tok_cols = np.concatenate([a["L0_tok_b"][:, None], a["cls_tok"].reshape(D, 1), a["L0_tok_class_token"].reshape(D, 1),
                               a["L0_tok_pos_embed"].T], axis=1)

    def padded(v):
        o = np.zeros(v.shape[:-1] + (HP,), v.dtype)
        o[..., :PC] = v
        return o.reshape(v.shape[:-2] + (HEADS * HP,))

    inner, wide = HEADS * RANK * PC, NST * RANK
    w_in = a["L0_attn_W_in"]

    def by_rank(v):
        return padded(v.reshape(-1, HEADS, RANK, PC).transpose(0, 2, 1, 3))

    def states_by_rank(v):
        return v.reshape(-1, NST, RANK).transpose(0, 2, 1)

    o = 2 * inner
    w_proj = np.concatenate([by_rank(w_in[:, inner:o]), states_by_rank(w_in[:, o:o + wide]),
                             states_by_rank(w_in[:, o + wide:o + 2 * wide]), by_rank(w_in[:, :inner])], axis=1)
    taps = np.concatenate([a["L0_attn_conv_w"], a["L0_attn_conv_b"][:, None]], axis=1).T
    conv = np.concatenate([by_rank(taps[:, :inner]), states_by_rank(taps[:, inner:inner + wide]),
                           states_by_rank(taps[:, inner + wide:])], axis=1)
    heads = np.stack([a["L0_attn_A_log"], a["L0_attn_D_skip"]], axis=1)
    w1 = a["L0_ffn_w1"].transpose(1, 0, 2)
    w2 = a["L0_ffn_w2"].reshape(E_N, FC, D, D).transpose(2, 0, 1, 3).reshape(D, E_N, FF)
    b1 = a["L0_ffn_b1"].reshape(E_N, FC, D).transpose(2, 0, 1)
    b2 = np.broadcast_to(a["L0_ffn_b2"][None], (D, E_N, D))
    c128, c88, seg = constants()
    arrays = {
        "x_main": x_main,
        "x_tail": x[:, KC * D:],
        "w_tok": w[:KC * D].reshape(KC, D, D).transpose(1, 0, 2).reshape(D, KC * D),
        "w_tok_tail": w[KC * D:],
        "tok_cols": tok_cols,
        "w_in": w_proj.reshape(D, -1),
        "w_dt": w_in[:, o + 2 * wide:],
        "conv": conv.transpose(2, 1, 0).reshape(D, -1),
        "dt_row": np.tile(np.concatenate([a["L0_attn_dt_bias"], a["L0_attn_A_log"]])[None], (Q, 1)),
        "dt_col": np.repeat(heads, HP, axis=0),
        "w_out": by_rank(a["L0_attn_W_out"].T).transpose(2, 1, 0).reshape(D, -1),
        "gate_w": a["L0_ffn_gate_w"].T,
        "experts": np.concatenate([w1, b1, w2, b2], axis=2).reshape(D, -1),
        "c128": c128,
        "c88": c88,
        "seg": seg,
    }
    arrays = {k: np.ascontiguousarray(v) for k, v in arrays.items()}
    nc = bacc.Bacc("TRN2", target_bir_lowering=False, num_devices=1)
    args = [nc.dram_tensor("in_" + k, v.shape, mybir.dt.from_np(v.dtype), kind="ExternalInput").ap() for k, v in arrays.items()]
    out = nc.dram_tensor("out", (B, L, D), FP32, kind="ExternalOutput").ap()
    tower(nc, *args, out)
    r = run_bass_kernel_spmd(nc, [{"in_" + k: v for k, v in arrays.items()}], core_ids=[0])
    return r.results[0]["out"]
```

```python
from contextlib import ExitStack

import numpy as np

import concourse.bass as bass
from concourse import mybir
from concourse.alu_op_type import AluOpType as ALU

FP32 = mybir.dt.float32
U32 = mybir.dt.uint32
I32 = mybir.dt.int32
ACT = mybir.ActivationFunctionType
AX = mybir.AxisListType

B, NPATCH, PATCH, CH = 64, 64, 28, 3
K_TOK = CH * PATCH * PATCH
D = 128
KC = K_TOK // D
K_TAIL = K_TOK - KC * D
L = NPATCH + 2
GI = 4
NG = B // GI
T = GI * L
HEADS, RANK, PC, NST = 4, 4, 16, 128
HP = 32
TAPS = 4
Q, NC = 22, 3
QR = Q * RANK
EPS = 1e-5
E_N, FF = 8, 512
FC = FF // D
TT = QR
TPG = T // TT
PARTS = 2
GPP = NG // PARTS
JT = GPP * TPG
TOKP = JT * TT
SL = 128
KMAX = -(-TOKP // SL)
NT = (2 * TOKP + E_N * (SL - 1)) // SL
W1C, W2C = FF + FC, FF + D
WCOLS = W1C + W2C
NCH = 12
MASKED = 1.0e4
HIDDEN = 1.0e30

C_ID, C_CEN, C_MEAN = 0, D, 2 * D
S_SEG, S_IT, S_ONE, S_UP, S_ONES, S_IOTA, S_IOTA8, S_KIO, S_TIO, S_MASK = np.cumsum(
    [0, QR, 2 * Q, QR, TT, TT, E_N, E_N, E_N * KMAX, E_N * NT]).tolist()
S_END = S_MASK + E_N * JT


def constants():
    eye = np.eye(D, dtype=np.float32)
    mean = np.full((D, D), 1.0 / D, np.float32)
    c128 = np.concatenate([eye, eye - mean, mean], axis=1)
    c88 = np.zeros((TT, S_END), np.float32)
    u, s = np.arange(Q)[:, None], np.arange(QR)[None, :] // RANK
    c88[:Q, S_SEG:S_SEG + QR] = u > s
    c88[32:32 + Q, S_SEG:S_SEG + QR] = -MASKED * (u <= s)
    t = np.arange(Q)[None, :]
    c88[:Q, S_IT:S_IT + Q] = u == t
    c88[:Q, S_IT + Q:S_IT + 2 * Q] = u <= t
    c88[:Q, S_ONE:S_ONE + QR] = 1.0
    k, p = np.arange(TT)[:, None], np.arange(TT)[None, :]
    c88[:, S_UP:S_UP + TT] = k < p
    c88[:, S_ONES:S_ONES + TT] = 1.0
    c88[:, S_IOTA:S_IOTA + E_N] = np.arange(E_N)
    c88[:, S_IOTA8:S_IOTA8 + E_N] = np.arange(E_N) + E_N
    c88[:, S_KIO:S_KIO + E_N * KMAX] = np.tile(np.arange(KMAX) * SL, E_N)
    c88[:, S_TIO:S_TIO + E_N * NT] = np.repeat(np.arange(NT), E_N)
    c88[:, S_MASK:S_MASK + E_N * JT] = np.tile(np.arange(JT) > 0, E_N)
    seg_rhs = np.zeros((32 + Q, NC * GI * HEADS, Q), np.float32)
    seg_rhs[32:] = (u > t)[:, None, :]
    return c128, c88, seg_rhs.reshape(32 + Q, -1)


class Group:

    def __init__(self, n, parity, before):
        self.n, self.parity, self.before = n, parity, before

    def next(self):
        return Group(self.n + 1, 1 - self.parity, self.before + self.parity)

    def after_next(self):
        return Group(self.n + 2, self.parity, self.before + 1)

    def last(self):
        return Group(self.n - 1, 1 - self.parity, self.before - (1 - self.parity))

    def first(self):
        return isinstance(self.n, int) and self.n == 0


def tower(nc, x_main, x_tail, w_tok, w_tok_tail, tok_cols, w_in, w_dt, conv, dt_row, dt_col, w_out,
          gate_w, experts, c128_d, c88_d, seg_d, out):
    ctx = ExitStack()
    with ctx:
        def sb(name, shape, dt=FP32):
            return ctx.enter_context(nc.sbuf_tensor(name, shape, dt))

        def sem(name):
            return ctx.enter_context(nc.semaphore(name))

        h1_rows = nc.dram_tensor("h1_rows", [NG * TPG, TT, D], FP32).ap()
        slot_x = [nc.dram_tensor(f"slot_x{p}", [NT * SL, D], FP32).ap() for p in range(PARTS)]
        slot_y = [nc.dram_tensor(f"slot_y{p}", [NT * SL, D], FP32).ap() for p in range(PARTS)]

        c128 = sb("c128", [128, 3 * D])
        c88 = sb("c88", [TT, S_END])
        wt = sb("wt", [128, KC, D])
        wtt = sb("wtt", [K_TAIL, D])
        tcol = sb("tcol", [128, 3 + L - 1])
        win = sb("win", [128, 16, D])
        wdt = sb("wdt", [128, HEADS])
        cv = sb("cv", [128, NCH, TAPS + 1])
        dtr = sb("dtr", [Q, 2 * HEADS])
        dtc = sb("dtc", [128, 2])
        wo = sb("wo", [128, RANK, D])
        gw = sb("gw", [128, E_N])
        eps = sb("eps", [128, 1])
        ident, center, mean = c128[:, C_ID:C_ID + D], c128[:, C_CEN:C_CEN + D], c128[:, C_MEAN:C_MEAN + D]

        XCOLS = KC * GI * NPATCH
        big = sb("big", [128, max(2 * XCOLS, E_N * WCOLS)])
        xm = [big[:, i * XCOLS:(i + 1) * XCOLS].rearrange("p (k t) -> p k t", k=KC) for i in range(2)]
        wall = big[:, 0:E_N * WCOLS].rearrange("p (e c) -> p e c", e=E_N)
        xt = [sb(f"xt{i}", [K_TAIL, GI * NPATCH]) for i in range(2)]
        h = [sb(f"h{i}", [128, T]) for i in range(2)]
        xn = [sb(f"xn{i}", [128, T]) for i in range(2)]
        ln_sq = sb("ln_sq_b", [128, T])
        ln_rs = sb("ln_rs_b", [128, T])
        res = sb("res_b", [128, T])
        po_sq = sb("po_sq_b", [128, T])
        po_rs = sb("po_rs_b", [128, T])
        h1 = sb("h1_b", [128, T])
        xs = sb("xs_b", [128, T])
        xs_all = sb("xs_all", [TT, NG * TPG, D])
        h1_t = sb("h1_t", [TT, TPG * D])
        logit = sb("logit", [TT, NG, TPG * E_N])
        NDT = NC * GI * HEADS
        du = sb("du", [Q, NDT])
        dn = sb("dn", [Q, NDT])
        de = sb("de", [Q, NDT])
        dr = sb("dr", [Q, NDT])
        ds_ = sb("ds_", [Q, NDT])
        dq = sb("dq", [Q, NDT])
        dp = sb("dp", [Q, NDT])
        dt_s = sb("dt_s", [Q, NC, GI, HEADS])
        dt_diag = sb("dt_diag", [Q, NDT, Q])
        da_s = sb("da_s", [Q, NC, GI, HEADS])
        nega_r = sb("nega_r", [Q, HEADS])
        seg_r = sb("seg_r", [32 + Q, NDT, Q])
        acc = sb("acc", [128, NCH, T])
        xc = sb("xc", [128, GI, NC, QR])
        bc = sb("bc", [128, GI, NC, QR])
        cc = sb("cc", [128, GI, NC, QR])
        sz = sb("sz", [128, RANK, T])
        decay = sb("decay", [QR, NC, GI, HEADS, Q])
        grow = sb("grow", [128, 2, GI, Q])
        total = sb("total", [QR, GI, HEADS])
        xdt = sb("xdt", [128, NC, GI, QR])
        xdt_t = sb("xdt_t", [QR, NC, GI, D])
        b_t = sb("b_t", [QR, 2, GI, D])
        xe = sb("xe", [QR, 3, GI, HEADS * PC])
        hs = sb("hs", [128, GI, 2, HEADS, HP])
        m_buf = sb("m_buf", [128, NC * GI * HEADS * QR])
        m = m_buf[0:QR, :].rearrange("p (c i h t) -> p c i h t", c=NC, i=GI, h=HEADS)
        t1 = sb("t1", [128, 2, GI, QR])
        y = xdt
        yg = sb("yg", [128, RANK, T])

        bank = [ctx.enter_context(nc.psum_tensor(f"bank{i}", [128, 512], FP32)) for i in range(8)]
        b_tok, b_c, b_v, b_dt, b_sp = bank[:5]
        RING = bank[5:8]
        NR = len(RING)
        XT_B, BT_B, G_B, I_B, Y_B, H_B = [b_dt, b_v, b_c], [b_c, b_sp], [b_sp, b_v, b_sp], [b_dt, b_sp], [b_c, b_v, b_dt], b_c

        loaded, zeroed, hs_zeroed, setup_done = map(sem, ["loaded", "zeroed", "hs_zeroed", "setup_done"])
        x_loaded = [sem(f"x_loaded{i}") for i in range(2)]
        names = """tok_summed h_ready ln_centered ln_squared ln_var ln_log ln_rstd xn_ready
            out_proj res_ready res_squared res_var res_log res_rstd res_scaled h1_ready po_centered po_squared po_var
            po_log po_rstd xs_ready rows_turned rows_copied rows_stored
            dt_raw dt_exp dt_step seg_ready dt_widened seg_summed decay_ready spread grow_ready total_ready
            proj tap0 conv_step x_act b_act z_act c_act xdt_ready
            x_turned x_turned_copied b_turned b_turned_copied xe_ready states states_copied
            scores m_ready inter inter_read intra y_sum y_total yg_ready""".split()
        S = {n: sem(n) for n in names}
        (tok_summed, h_ready, ln_centered, ln_squared, ln_var, ln_log, ln_rstd, xn_ready,
         out_proj, res_ready, res_squared, res_var, res_log, res_rstd, res_scaled, h1_ready, po_centered, po_squared,
         po_var, po_log, po_rstd, xs_ready, rows_turned, rows_copied, rows_stored,
         dt_raw, dt_exp, dt_step, seg_ready, dt_widened, seg_summed, decay_ready, spread, grow_ready, total_ready,
         proj, tap0, conv_step, x_act, b_act, z_act, c_act, xdt_ready,
         x_turned, x_turned_copied, b_turned, b_turned_copied, xe_ready, states, states_copied,
         scores, m_ready, inter, inter_read, intra, y_sum, y_total, yg_ready) = [S[n] for n in names]

        SP_G = NC * GI * Q
        SP_T = SP_G + (NC - 1) * GI * Q
        N_DT = 17
        DT_NEG, DT_A = 2, 17
        N_CONV = NCH * (TAPS - 1)
        N_ROUTE, R_BOTH, R_DIFF = 27, 12, 14

        def conv_at(chunk, tap):
            return (chunk // 2) * 2 * (TAPS - 1) + (tap - 1) * 2 + chunk % 2 + 1

        def conv_all(chunk):
            return conv_at(chunk, TAPS - 1)

        def by_chunk(buf):
            return buf.rearrange("p i c (t r) -> p i (c t) r", r=RANK)

        token_loads = [(wt[:, :, :], w_tok.rearrange("p (k d) -> p k d", d=D)), (wtt[:, :], w_tok_tail)]
        loads = [(tcol[:, :], tok_cols), (c128[:, :], c128_d), (c88[:, :], c88_d), (win[:, :, :], w_in.rearrange("p (k d) -> p k d", d=D)),
                 (wdt[:, :], w_dt), (cv[:, :, :], conv.rearrange("p (k d) -> p k d", d=TAPS + 1)),
                 (dtr[:, :], dt_row), (dtc[:, :], dt_col),
                 (wo[:, :, :], w_out.rearrange("p (k d) -> p k d", d=D)), (gw[:, :], gate_w),
                 (seg_r[:, :, :], seg_d.rearrange("p (k d) -> p k d", d=Q))]
        N_LOADS = 16 * len(loads)
        tokens_loaded, experts_loaded = sem("tokens_loaded"), sem("experts_loaded")

        onehot = [sb(f"onehot{i}", [TT, JT, E_N]) for i in range(2)]
        both = sb("both", [TT, JT, E_N])
        ra = sb("ra", [TT, JT, E_N])
        rb = sb("rb", [TT, JT, E_N])
        top = [sb(f"top{i}", [TT, JT]) for i in range(2)]
        idx = sb("idx", [TT, JT])
        rd = sb("rd", [TT, JT])
        rsum = sb("rsum", [TT, E_N, JT])
        rtot = sb("rtot", [TT, E_N, JT])
        cmp_k = sb("cmp_k", [TT, E_N, KMAX])
        ntile = sb("ntile", [TT, E_N])
        endt = sb("endt", [TT, E_N])
        base = sb("base", [TT, E_N])
        ones_e = sb("ones_e", [TT, E_N])
        cmp_t = sb("cmp_t", [TT, NT, E_N])
        tile_f = sb("tile_f", [TT, NT])
        wgt = [sb(f"wgt{i}", [TT, PARTS, JT]) for i in range(2)]
        slot_f = sb("slot_f", [TT, JT])
        slot_u = sb("slot_u", [TT, PARTS, JT, 2], U32)
        tile_e = sb("tile_e", [1, PARTS, NT], I32)

        mark = sb("mark", [1, 5])
        sc_x = [sb(f"sc_x{i}", [TT, D]) for i in range(2)]
        sc_i = [[sb(f"sc_i{i}{k}", [TT, 1], U32) for k in range(2)] for i in range(2)]
        cols = np.cumsum([0, D, D, W1C, W2C, FC * SL]).tolist()
        assert 2 * (cols[-1] + D) <= NC * GI * HEADS * QR

        def part_of_m(s, k, width):
            o = s * (cols[-1] + D) + cols[k]
            return m_buf[:, o:o + width]

        fx = [part_of_m(i, 0, D) for i in range(2)]
        fxt = [part_of_m(i, 1, SL) for i in range(2)]
        fw1 = [part_of_m(i, 2, W1C) for i in range(2)]
        fw2 = [part_of_m(i, 3, W2C) for i in range(2)]
        fh = [part_of_m(i, 4, FC * SL).rearrange("p (k t) -> p k t", k=FC) for i in range(2)]
        fy = [part_of_m(i, 5, D) for i in range(2)]
        gy = [[sb(f"gy{i}{k}", [TT, D]) for k in range(2)] for i in range(4)]
        gi = [sb(f"gi{i}", [TT, 4], U32) for i in range(2)]
        gh = [sb(f"gh{i}", [TT, D]) for i in range(2)]
        go = [sb(f"go{i}", [TT, D]) for i in range(2)]

        route_step, route_mm, route_exp, routed = map(sem, ["route_step", "route_mm", "route_exp", "routed"])
        slot_step, xe_part, sc_copied = map(sem, ["slot_step", "xe_part", "sc_copied"])
        sent = [sem(f"sent{i}") for i in range(2)]
        fx_loaded = [sem(f"fx_loaded{i}") for i in range(2)]
        fx_turned, fx_copied, w1_staged, w2_staged, hidden_mm, hidden_act, y_mm, y_biased = map(
            sem, ["fx_turned", "fx_copied", "w1_staged", "w2_staged", "hidden_mm", "hidden_act", "y_mm", "y_biased"])
        fy_stored = [sem(f"fy_stored{i}") for i in range(2)]
        ga_index = sem("ga_index")
        gathered = [sem(f"gathered{i}") for i in range(2)]
        gh_loaded = [sem(f"gh_loaded{i}") for i in range(2)]
        weighed, first_added, combined = sem("weighed"), sem("first_added"), sem("combined")
        out_stored = [sem(f"out_stored{i}") for i in range(2)]

        def over_groups(eng, body, between, send=None):
            body(Group(0, 0, 0))
            with eng.Fori(0, GPP // 2) as i:
                body(Group(2 * i + 1, 1, i))
                body(Group(2 * i + 2, 0, i + 1))
            between()
            if send:
                for s in range(2):
                    send(0, s, s, 0)
            with eng.Fori(GPP // 2, (NG - 2) // 2) as i:
                for half in range(2):
                    body(Group(2 * i + 1 + half, 1 - half, i + half))
                    for o in range(3 * half, 3 * half + 3):
                        if send:
                            send(0, 6 * i + (2 + o - 3 * GPP), o % 2, 3 * i + (1 + o // 2 - 3 * GPP // 2))
            for n in (NG - 1, NG):
                body(Group(n, n % 2, n // 2))
                for s in range(2):
                    if send:
                        send(0, JT + 2 * (n - NG) - 2 + s, s, JT // 2 + (n - NG) - 1)

        def stages(g):
            n = g.n if isinstance(g.n, int) else 1
            return n > 0, n < NG, n < NG - 1

        block = ctx.enter_context(nc.Block())

        @block.sync
        def _(sp):
            def load_x(g):
                sp.dma_start(xm[g.parity][:, :, :], x_main[bass.ds(g.n, 1), :, :].rearrange("o p (k d) -> (o p) k d", k=KC)
                             ).then_inc(x_loaded[g.parity], 16)
                sp.dma_start(xt[g.parity][:, :], x_tail[bass.ds(g.n, 1), :, :].rearrange("o p d -> (o p) d")
                             ).then_inc(x_loaded[g.parity], 16)

            def store_rows(g):
                sp.wait_ge(rows_copied, g.n + 2)
                sp.dma_start(h1_rows[bass.ds(g.n * TPG, TPG), :, :].rearrange("k p d -> p k d"),
                             h1_t[:, :].rearrange("p (k d) -> p k d", d=D)).then_inc(rows_stored, 16)

            for dst, src in token_loads:
                sp.dma_start(dst, src).then_inc(tokens_loaded, 16)
            load_x(Group(0, 0, 0))
            for dst, src in loads:
                sp.dma_start(dst, src).then_inc(loaded, 16)
            load_x(Group(1, 1, 0))
            sp.wait_ge(zeroed, 1)
            half = NT * D // 2
            for p in range(PARTS):
                for k in range(2):
                    sp.dma_start(slot_x[p].rearrange("(p k) d -> p (k d)", p=128)[:, k * half:(k + 1) * half],
                                 acc[:, :, :].rearrange("p k t -> p (k t)")[:, :half]).then_inc(zeroed, 16)

            def body(g):
                sp.wait_ge(tok_summed, g.n + 1)
                load_x(g.after_next())
                if not g.first():
                    store_rows(g.last())

            body(Group(0, 0, 0))
            with sp.Fori(0, (NG - 4) // 2) as i:
                body(Group(2 * i + 1, 1, i))
                body(Group(2 * i + 2, 0, i + 1))
            body(Group(NG - 3, 1, (NG - 4) // 2))
            sp.wait_ge(tok_summed, NG)
            sp.dma_start(wall, experts.rearrange("p (e c) -> p e c", e=E_N)).then_inc(experts_loaded, 16)
            for n in range(NG - 3, NG):
                store_rows(Group(n, n % 2, n // 2))
            sp.wait_ge(rows_stored, 16 * (NG + 1))

            def load_fx(p, i, s):
                if not isinstance(i, int) or p or i >= 2:
                    sp.wait_ge(fx_turned, i + (p * NT - 1))
                sp.dma_start(fx[s], slot_x[p][bass.ds(i * SL, SL), :]).then_inc(fx_loaded[s], 16)

            def store_fy(p, i, s):
                sp.wait_ge(y_biased, i + (p * NT + 1))
                sp.dma_start(slot_y[p][bass.ds(i * SL, SL), :], fy[s]).then_inc(fy_stored[s], 16)

            def all_sent(p):
                for s in range(2):
                    sp.wait_ge(sent[s], 32 * (p + 1) * (JT // 2))

            AHEAD = 4

            def load_h1(p, j, s):
                sp.dma_start(gh[s][:, :], h1_rows[bass.ds(p * JT + j, 1), :, :].rearrange("o p d -> (o p) d")
                             ).then_inc(gh_loaded[s], 16)

            def store_out(p, j, s):
                sp.wait_ge(combined, p * JT + j + 1)
                rows = out.rearrange("b l d -> (b l) d").rearrange("(k q) d -> k q d", q=TT)
                sp.dma_start(rows[bass.ds(p * JT + j, 1), :, :].rearrange("o p d -> (o p) d"), go[s][:, :]
                             ).then_inc(out_stored[s], 16)

            all_sent(0)
            for k in range(AHEAD):
                load_fx(0, k, k % 2)
            with sp.Fori(0, (NT - AHEAD) // 2) as i:
                for s in range(2):
                    load_fx(0, 2 * i + (AHEAD + s), s)
                    store_fy(0, 2 * i + s, s)
            all_sent(1)
            for k in range(AHEAD):
                load_fx(1, k, k % 2)
                store_fy(0, NT - AHEAD + k, k % 2)
            for s in range(2):
                load_h1(0, s, s)
            STEPS = (NT - AHEAD) // 6
            assert 6 * STEPS == NT - AHEAD and 4 * STEPS == JT
            with sp.Fori(0, STEPS - 1) as i:
                for k in range(6):
                    load_fx(1, 6 * i + (AHEAD + k), k % 2)
                    store_fy(1, 6 * i + k, k % 2)
                    if k in (0, 2, 3, 5):
                        o = (0, 2, 3, 5).index(k)
                        store_out(0, 4 * i + o, o % 2)
                        load_h1(0, 4 * i + (2 + o), o % 2)
            for k in range(6):
                load_fx(1, 6 * (STEPS - 1) + (AHEAD + k), k % 2)
                store_fy(1, 6 * (STEPS - 1) + k, k % 2)
            for k in range(AHEAD):
                store_fy(1, NT - AHEAD + k, k % 2)
            for o in range(4):
                store_out(0, JT - 4 + o, o % 2)
                load_h1(0 if o < 2 else 1, JT - 2 + o if o < 2 else o - 2, o % 2)
            with sp.Fori(0, JT // 2 - 1) as i:
                for s in range(2):
                    store_out(1, 2 * i + s, s)
                    load_h1(1, 2 * i + (2 + s), s)
            for s in range(2):
                store_out(1, JT - 2 + s, s)
            for s in range(2):
                sp.wait_ge(out_stored[s], 16 + 16 * PARTS * JT // 2)

        @block.tensor
        def _(pe):
            mm = nc.tensor.matmul

            def turn(dst, src):
                return mm(dst, src, ident, start=True, stop=True, is_transpose=True)

            def tokens(g, k0, k1):
                if k0 == 0:
                    pe.wait_ge(x_loaded[g.parity], 32 * g.before + 32)
                    if not g.first():
                        pe.wait_ge(xn_ready, g.n)
                ps = b_tok[:, 0:GI * NPATCH]
                for k in range(k0, min(k1, KC)):
                    mm(ps, wt[:, k, :], xm[g.parity][:, k, :], start=(k == 0), stop=False)
                if k1 > KC:
                    mm(ps, wtt[:, :], xt[g.parity][:, :], start=False, stop=True).then_inc(tok_summed, 1)

            def ln1_center(g):
                pe.wait_ge(h_ready, g.n + 1)
                mm(b_tok[:, 0:T], center, h[g.parity][:, :], start=True, stop=True).then_inc(ln_centered, 1)

            def ln1_var(g):
                pe.wait_ge(ln_squared, g.n + 1)
                if not g.first():
                    pe.wait_ge(x_turned_copied, NC * (g.n - 1) + 1)
                mm(b_dt[:, 0:T], mean, ln_sq[:, :], start=True, stop=True).then_inc(ln_var, 1)

            def dt_project(g):
                pe.wait_ge(xn_ready, g.n + 1)
                for c in range(NC):
                    for i in range(GI):
                        o = (c * GI + i) * HEADS
                        last = mm(b_dt[0:Q, o:o + HEADS], xn[g.parity][:, i * L + c * Q:i * L + (c + 1) * Q], wdt[:, :],
                                  start=True, stop=True)
                last.then_inc(dt_raw, 1)

            def project(g, k):
                if k == 15:
                    pe.wait_ge(z_act, RANK * g.n + 1)
                elif k >= NR:
                    pe.wait_ge(conv_step, N_CONV * g.n + conv_all(k - NR))
                elif k == 0 and not g.first():
                    pe.wait_ge(z_act, RANK * g.n)
                mm(RING[k % NR][:, 0:T], win[:, k, :], xn[g.parity][:, :], start=True, stop=True).then_inc(proj, 1)

            def segments(g, c):
                if c == 0:
                    pe.wait_ge(seg_ready, g.n + 1)
                    if not g.first():
                        pe.wait_ge(y_sum, NC * g.n)
                else:
                    pe.wait_ge(decay_ready, NC * g.n + c)
                n = GI * HEADS
                mm(b_dt[0:QR, 0:n * Q], c88[0:32 + Q, S_SEG:S_SEG + QR], seg_r[:, c * n:(c + 1) * n, :],
                   start=True, stop=True).then_inc(seg_summed, 1)

            def spread_dt(g):
                pe.wait_ge(dt_widened, g.n + 1)
                if not g.first():
                    pe.wait_ge(inter_read, 2 * g.n)
                mm(b_sp[0:QR, SP_T:SP_T + GI * HEADS], c88[0:Q, S_ONE:S_ONE + QR], da_s[:, 1, :, :].rearrange("p i h -> p (i h)"),
                   start=True, stop=True)
                ones = c88[0:Q, S_ONES:S_ONES + HP]
                for k in range(HEADS):
                    dt_k = dt_diag[:, :, :].rearrange("p (n h) t -> p n h t", h=HEADS)[:, :, k, :]
                    mm(b_sp[HP * k:HP * (k + 1), 0:NC * GI * Q], ones, dt_k, start=True, stop=True)
                for k in range(HEADS):
                    sum_k = seg_r[0:Q, GI * HEADS:NDT, :].rearrange("p (n h) t -> p n h t", h=HEADS)[:, :, k, :]
                    last = mm(b_sp[HP * k:HP * (k + 1), SP_G:SP_T], ones, sum_k, start=True, stop=True)
                last.then_inc(spread, 1)

            def out_project(g):
                pe.wait_ge(yg_ready, g.n + 1)
                for r in range(RANK):
                    last = mm(b_c[:, 0:T], wo[:, r, :], yg[:, r, :], start=(r == 0), stop=(r == RANK - 1))
                last.then_inc(out_proj, 1)

            def res_mean(g):
                pe.wait_ge(res_squared, g.n + 1)
                mm(b_v[:, 0:T], mean, po_sq[:, :], start=True, stop=True).then_inc(res_var, 1)

            def post_center(g):
                pe.wait_ge(h1_ready, g.n + 1)
                mm(b_c[:, 0:T], center, h1[:, :], start=True, stop=True).then_inc(po_centered, 1)

            def post_var(g):
                pe.wait_ge(po_squared, g.n + 1)
                mm(b_v[:, 0:T], mean, po_sq[:, :], start=True, stop=True).then_inc(po_var, 1)

            def rows_and_logits(g):
                pe.wait_ge(xs_ready, g.n + 1)
                for k in range(TPG):
                    turn(b_c[0:TT, k * D:(k + 1) * D], xs[:, k * TT:(k + 1) * TT])
                for k in range(TPG):
                    mm(b_c[0:TT, TPG * D + k * E_N:TPG * D + (k + 1) * E_N], xs[:, k * TT:(k + 1) * TT], gw[:, :],
                       start=True, stop=True)
                for k in range(TPG):
                    last = turn(b_v[0:TT, k * D:(k + 1) * D], h1[:, k * TT:(k + 1) * TT])
                last.then_inc(rows_turned, 1)

            def turn_b(g):
                pe.wait_ge(b_act, g.n + 1)
                pe.wait_ge(rows_copied, g.n + 1)
                pe.wait_ge(xdt_ready, NC * (g.n + 1))
                pe.wait_ge(total_ready, g.n + 1)
                for c in range(2):
                    for i in range(GI):
                        last = turn(BT_B[c][0:QR, i * D:(i + 1) * D], bc[:, i, c, :])
                    last.then_inc(b_turned, 1)

            def turn_x(g):
                for c in range(NC):
                    if c == 2:
                        pe.wait_ge(b_turned_copied, 2 * g.n + 1)
                    for i in range(GI):
                        last = turn(XT_B[c][0:QR, i * D:(i + 1) * D], xdt[:, c, i, :])
                    last.then_inc(x_turned, 1)

            def score(g, c):
                if c == 0:
                    pe.wait_ge(c_act, g.n + 1)
                    pe.wait_ge(b_turned_copied, 2 * g.n + 2)
                elif c == 1:
                    pe.wait_ge(x_turned_copied, NC * g.n + 2)
                else:
                    pe.wait_ge(m_ready, NC * GI * g.n + GI)
                for i in range(GI):
                    last = mm(G_B[c][0:QR, i * QR:(i + 1) * QR], bc[:, i, c, :], cc[:, i, c, :], start=True, stop=True)
                last.then_inc(scores, 1)

            def state_sums(g):
                pe.wait_ge(xe_ready, g.n + 1)
                pe.wait_ge(b_turned_copied, 2 * (g.n + 1))
                pe.wait_ge(x_turned_copied, NC * (g.n + 1))
                n = HEADS * PC
                for i in range(GI):
                    o = 2 * i * n
                    mm(H_B[:, o:o + n], b_t[:, 0, i, :], xe[:, 0, i, :], start=True, stop=True)
                    mm(H_B[:, o + n:o + 2 * n], b_t[:, 0, i, :], xe[:, 2, i, :], start=True, stop=False)
                    last = mm(H_B[:, o + n:o + 2 * n], b_t[:, 1, i, :], xe[:, 1, i, :], start=False, stop=True)
                last.then_inc(states, 1)

            def inter_product(g, c):
                if c == 1:
                    pe.wait_ge(states_copied, g.n + 1)
                    if not isinstance(g.n, int) or g.n < NG - 1:
                        pe.wait_ge(dt_step, N_DT * (g.n + 1) + 1)
                else:
                    pe.wait_ge(m_ready, NC * GI * (g.n + 1))
                for i in range(GI):
                    last = mm(I_B[c - 1][:, i * QR:(i + 1) * QR], hs[:, i, c - 1, :, :], cc[:, i, c, :], start=True, stop=True)
                last.then_inc(inter, 1)

            def intra_products(g, c):
                if c == 0:
                    pe.wait_ge(states_copied, g.n + 1)
                elif c == 2:
                    pe.wait_ge(inter_read, 2 * g.n + 1)
                for i in range(GI):
                    if i == 0 and Y_B[c] is G_B[c]:
                        pe.wait_ge(m_ready, NC * GI * g.n + (c + 1) * GI)
                    elif Y_B[c] is not G_B[c]:
                        pe.wait_ge(m_ready, NC * GI * g.n + c * GI + i + 1)
                    for k in range(HEADS):
                        last = mm(Y_B[c][HP * k:HP * (k + 1), i * QR:(i + 1) * QR], xdt_t[:, c, i, HP * k:HP * (k + 1)],
                                  m[:, c, i, k, :], start=True, stop=True)
                last.then_inc(intra, 1)

            def body(g):
                mix, own, begin = stages(g)
                p = g.last()
                if mix:
                    turn_b(p)
                    turn_x(p)
                if own:
                    ln1_center(g)
                if mix:
                    score(p, 0)
                    score(p, 1)
                if own:
                    ln1_var(g)
                if mix:
                    state_sums(p)
                if own:
                    dt_project(g)
                    for k in range(3):
                        project(g, k)
                if mix:
                    score(p, 2)
                    inter_product(p, 1)
                    intra_products(p, 0)
                    intra_products(p, 1)
                if begin:
                    tokens(g.next(), 0, 3)
                if mix:
                    inter_product(p, 2)
                if own:
                    project(g, 3)
                    project(g, 4)
                if begin:
                    tokens(g.next(), 3, 5)
                if mix:
                    intra_products(p, 2)
                if begin:
                    tokens(g.next(), 5, 7)
                if own:
                    project(g, 5)
                    project(g, 6)
                    segments(g, 0)
                if begin:
                    tokens(g.next(), 7, 8)
                if own:
                    segments(g, 1)
                    project(g, 7)
                if begin:
                    tokens(g.next(), 8, 9)
                if own:
                    segments(g, 2)
                    project(g, 8)
                    spread_dt(g)
                if mix:
                    out_project(p)
                if own:
                    project(g, 9)
                if begin:
                    tokens(g.next(), 9, 11)
                if mix:
                    res_mean(p)
                if own:
                    project(g, 10)
                if begin:
                    tokens(g.next(), 11, 13)
                if own:
                    project(g, 11)
                if mix:
                    post_center(p)
                if own:
                    project(g, 12)
                if begin:
                    tokens(g.next(), 13, 15)
                if mix:
                    post_var(p)
                if own:
                    project(g, 13)
                    project(g, 14)
                if begin:
                    tokens(g.next(), 15, 16)
                if mix:
                    rows_and_logits(p)
                if own:
                    project(g, 15)
                if begin:
                    tokens(g.next(), 16, KC + 1)

            pe.wait_ge(tokens_loaded, 16 * len(token_loads))
            tokens(Group(0, 0, 0), 0, KC + 1)
            pe.wait_ge(loaded, N_LOADS)

            def route(p):
                pe.wait_ge(route_step, R_BOTH + p * N_ROUTE)
                flat = both[:, :, :].rearrange("p j e -> p (j e)")
                mm(b_tok[0:TT, 0:JT * E_N], c88[:, S_UP:S_UP + TT], flat, start=True, stop=True)
                mm(b_tok[0:TT, JT * E_N:2 * JT * E_N], c88[:, S_ONES:S_ONES + TT], flat, start=True, stop=True
                   ).then_inc(route_mm, 1)
                pe.wait_ge(routed, p + 1)

            over_groups(pe, body, lambda: route(0))
            route(1)

            FT, FH, FY = [bank[0], bank[1]], [bank[2], bank[3]], [bank[4], bank[5]]

            def turn_rows(n, s, before):
                pe.wait_ge(fx_loaded[s], before * 16 + 16)
                turn(FT[s][:, 0:SL], fx[s]).then_inc(fx_turned, 1)

            def up(n, s):
                pe.wait_ge(fx_copied, n + 1)
                pe.wait_ge(w1_staged, n + 1)
                for k in range(FC):
                    last = mm(FH[s][:, k * SL:(k + 1) * SL], fw1[s][:, k * D:(k + 1) * D], fxt[s], start=True, stop=True)
                last.then_inc(hidden_mm, 1)

            def down(n, s, first=False):
                pe.wait_ge(hidden_act, n + 1)
                pe.wait_ge(w2_staged, n + 1)
                if not first:
                    pe.wait_ge(y_biased, n - 1)
                for k in range(FC):
                    last = mm(FY[s][:, 0:D], fh[s][:, k, :], fw2[s][:, k * D:(k + 1) * D], start=(k == 0), stop=(k == FC - 1))
                last.then_inc(y_mm, 1)

            n = PARTS * NT
            turn_rows(0, 0, 0)
            turn_rows(1, 1, 0)
            up(0, 0)
            turn_rows(2, 0, 1)
            up(1, 1)
            down(0, 0, first=True)
            turn_rows(3, 1, 1)
            up(2, 0)
            down(1, 1, first=True)
            with pe.Fori(0, (n - 4) // 2) as i:
                turn_rows(2 * i + 4, 0, i + 2)
                up(2 * i + 3, 1)
                down(2 * i + 2, 0)
                turn_rows(2 * i + 5, 1, i + 2)
                up(2 * i + 4, 0)
                down(2 * i + 3, 1)
            up(n - 1, 1)
            down(n - 2, 0)
            down(n - 1, 1)

        @block.scalar
        def _(act):
            A = nc.scalar.activation

            def log_exp():
                nc.scalar.preload_act_table_set("natural_log_exp_and_others")

            def rstd(dst, var, ready, n, log_sem, out_sem):
                act.wait_ge(ready, n)
                A(dst, var, ACT.Ln, bias=eps[:, :]).then_inc(log_sem, 1)
                act.wait_ge(log_sem, n)
                A(dst, dst, ACT.Exp, scale=-0.5).then_inc(out_sem, 1)

            def ln1_square(g):
                act.wait_ge(ln_centered, g.n + 1)
                A(ln_sq[:, :], b_tok[:, 0:T], ACT.Square).then_inc(ln_squared, 1)

            def ln1_rstd(g):
                rstd(ln_rs[:, :], b_dt[:, 0:T], ln_var, g.n + 1, ln_log, ln_rstd)

            def dt_exponent(g):
                act.wait_ge(dt_step, N_DT * g.n + DT_NEG)
                A(de[:, :], dn[:, :], ACT.Exp).then_inc(dt_exp, 1)

            def first_tap(g, k):
                act.wait_ge(proj, 16 * g.n + k + 1)
                A(acc[:, k, :], RING[k % NR][:, 0:T], ACT.Identity, bias=cv[:, k, TAPS:TAPS + 1],
                  scale=cv[:, k, TAPS - 1:TAPS]).then_inc(tap0, 1)

            def decays(g, c):
                act.wait_ge(seg_summed, NC * g.n + c + 1)
                if c == 0 and not g.first():
                    act.wait_ge(m_ready, NC * GI * g.n)
                    act.wait_ge(xe_ready, g.n)
                A(decay[:, c, :, :, :].rearrange("p i h t -> p (i h t)"), b_dt[0:QR, 0:GI * HEADS * Q], ACT.Exp
                  ).then_inc(decay_ready, 1)

            def growths(g):
                act.wait_ge(spread, g.n + 1)
                A(grow[:, :, :, :].rearrange("p c i t -> p (c i t)"), b_sp[:, SP_G:SP_T], ACT.Exp).then_inc(grow_ready, 1)
                A(total[:, :, :].rearrange("p i h -> p (i h)"), b_sp[0:QR, SP_T:SP_T + GI * HEADS], ACT.Exp).then_inc(total_ready, 1)

            def silu_chunk(g, dst, k0, done):
                act.wait_ge(conv_step, N_CONV * g.n + conv_all(k0 + RANK - 1))
                if not g.first():
                    act.wait_ge(y_sum, NC * g.n)
                for r in range(RANK):
                    v = by_chunk(dst[:, :, :, :])[:, :, :, r]
                    last = A(v, acc[:, k0 + r, :].rearrange("p (i t) -> p i t", i=GI), ACT.Silu)
                last.then_inc(done, 1)

            def silu_gate(g, r):
                act.wait_ge(proj, 16 * g.n + NCH + r + 1)
                if not g.first():
                    act.wait_ge(yg_ready, g.n)
                A(sz[:, r, :], RING[(NCH + r) % NR][:, 0:T], ACT.Silu).then_inc(z_act, 1)

            def copy_states(g):
                act.wait_ge(states, g.n + 1)
                A(hs[:, :, :, :, 0:PC].rearrange("p i c h q -> p (i c h) q"),
                  H_B[:, 0:GI * 2 * HEADS * PC].rearrange("p (k q) -> p k q", q=PC), ACT.Copy).then_inc(states_copied, 1)

            def res_square(g):
                act.wait_ge(res_ready, g.n + 1)
                A(po_sq[:, :], res[:, :], ACT.Square).then_inc(res_squared, 1)

            def res_norm(g):
                rstd(po_rs[:, :], b_v[:, 0:T], res_var, g.n + 1, res_log, res_rstd)

            def post_square(g):
                act.wait_ge(po_centered, g.n + 1)
                A(po_sq[:, :], b_c[:, 0:T], ACT.Square).then_inc(po_squared, 1)

            def post_norm(g):
                rstd(po_rs[:, :], b_v[:, 0:T], po_var, g.n + 1, po_log, po_rstd)

            def body(g):
                mix, own, _ = stages(g)
                p = g.last()
                if own:
                    ln1_square(g)
                    ln1_rstd(g)
                if mix:
                    copy_states(p)
                if own:
                    dt_exponent(g)
                    for k in range(7):
                        first_tap(g, k)
                    decays(g, 0)
                    decays(g, 1)
                    first_tap(g, 7)
                    decays(g, 2)
                    first_tap(g, 8)
                    growths(g)
                    first_tap(g, 9)
                if mix:
                    res_square(p)
                if own:
                    first_tap(g, 10)
                if mix:
                    res_norm(p)
                if own:
                    first_tap(g, 11)
                if mix:
                    post_square(p)
                if mix:
                    post_norm(p)
                if own:
                    for r in range(RANK - 1):
                        silu_gate(g, r)
                    silu_chunk(g, xc, 0, x_act)
                    silu_gate(g, RANK - 1)
                    silu_chunk(g, bc, 4, b_act)
                    silu_chunk(g, cc, 8, c_act)
                    log_exp()

            log_exp()
            act.wait_ge(loaded, N_LOADS)
            A(nega_r[:, :], dtr[:, HEADS:2 * HEADS], ACT.Exp).then_inc(rows_stored, 16)
            act.wait_ge(rows_stored, 16)
            A(nega_r[:, :], nega_r[:, :], ACT.Copy, scale=-1.0).then_inc(rows_copied, 1)
            act.wait_ge(setup_done, 1)
            act.wait_ge(zeroed, 1 + 32 * PARTS)
            act.wait_ge(hs_zeroed, 1)

            def route(p):
                act.wait_ge(route_step, R_DIFF + p * N_ROUTE)
                A(rd[:, :], rd[:, :], ACT.Exp).then_inc(route_exp, 1)

            over_groups(act, body, lambda: route(0))
            route(1)

            def hidden(n, s):
                act.wait_ge(hidden_mm, n + 1)
                for k in range(FC):
                    last = A(fh[s][:, k, :], bank[2 + s][:, k * SL:(k + 1) * SL], ACT.Relu,
                             bias=fw1[s][:, FF + k:FF + k + 1])
                last.then_inc(hidden_act, 1)

            hidden(0, 0)
            hidden(1, 1)
            with act.Fori(1, PARTS * NT // 2) as i:
                for s in range(2):
                    act.wait_ge(y_mm, 2 * i + (s - 1))
                    hidden(2 * i + s, s)

        @block.vector
        def _(dve):
            V = nc.vector

            def tokens_bias(g):
                dve.wait_ge(tok_summed, g.n + 1)
                V.scalar_tensor_tensor(
                    out=h[g.parity][:, :].rearrange("p (i t) -> p i t", i=GI)[:, :, 2:L],
                    in0=b_tok[:, 0:GI * NPATCH].rearrange("p (i t) -> p i t", i=GI), scalar=tcol[:, 0:1],
                    in1=tcol[:, 4:4 + NPATCH].rearrange("p (o t) -> p o t", o=1).broadcast_to([128, GI, NPATCH]),
                    op0=ALU.add, op1=ALU.mult).then_inc(h_ready, 1)

            def ln1_scale(g):
                dve.wait_ge(ln_rstd, g.n + 1)
                V.tensor_tensor(xn[g.parity][:, :], b_tok[:, 0:T], ln_rs[:, :], ALU.mult).then_inc(xn_ready, 1)

            def dt_begin(g):
                dve.wait_ge(dt_raw, g.n + 1)
                n = NC * GI
                bias = dtr[:, 0:HEADS].rearrange("p (o h) -> p o h", o=1).broadcast_to([Q, n, HEADS])
                V.tensor_tensor(du[:, :].rearrange("p (n h) -> p n h", n=n), b_dt[0:Q, 0:n * HEADS].rearrange("p (n h) -> p n h", n=n),
                                bias, ALU.add).then_inc(dt_step, 1)
                dve.wait_ge(dt_step, N_DT * g.n + 1)
                V.scalar_tensor_tensor(out=dn[:, :], in0=du[:, :], scalar=-1.0, in1=du[:, :], op0=ALU.mult, op1=ALU.min
                                       ).then_inc(dt_step, 1)

            def dt_steps(g):
                done = [2]

                def link(ins):
                    done[0] += 1
                    ins.then_inc(dt_step, 1)
                    yield
                    dve.wait_ge(dt_step, N_DT * g.n + done[0])

                dve.wait_ge(dt_exp, g.n + 1)
                yield from link(V.tensor_scalar(dr[:, :], de[:, :], 2.0, None, ALU.add))
                yield from link(V.reciprocal(dr[:, :], dr[:, :]))
                yield from link(V.tensor_tensor(ds_[:, :], de[:, :], dr[:, :], ALU.mult))
                yield from link(V.tensor_tensor(dq[:, :], ds_[:, :], ds_[:, :], ALU.mult))
                yield from link(V.tensor_scalar(dp[:, :], dq[:, :], 1.0 / 15.0, None, ALU.mult))
                for k in (13, 11, 9, 7, 5, 3):
                    yield from link(V.scalar_tensor_tensor(out=dp[:, :], in0=dp[:, :], scalar=1.0 / k, in1=dq[:, :], op0=ALU.add, op1=ALU.mult))
                yield from link(V.scalar_tensor_tensor(out=dp[:, :], in0=dp[:, :], scalar=1.0, in1=ds_[:, :], op0=ALU.add, op1=ALU.mult))
                yield from link(V.tensor_scalar(du[:, :], du[:, :], 0.0, None, ALU.max))
                yield from link(V.scalar_tensor_tensor(out=dt_s[:, :, :, :].rearrange("p c i h -> p (c i h)"), in0=dp[:, :], scalar=2.0,
                                            in1=du[:, :], op0=ALU.mult, op1=ALU.add))
                n = NC * GI
                V.tensor_tensor(da_s[:, :, :, :].rearrange("p c i h -> p (c i) h"), dt_s[:, :, :, :].rearrange("p c i h -> p (c i) h"),
                                nega_r[:, :].rearrange("p (o h) -> p o h", o=1).broadcast_to([Q, n, HEADS]), ALU.mult
                                ).then_inc(dt_step, 1)

            def conv_steps(g, k0):
                for tap in range(1, TAPS):
                    for k in (k0, k0 + 1):
                        if tap == 1:
                            dve.wait_ge(tap0, NCH * g.n + k + 1)
                        else:
                            dve.wait_ge(conv_step, N_CONV * g.n + conv_at(k, tap - 1))
                        src = RING[k % NR][:, 0:T].rearrange("p (i t) -> p i t", i=GI)[:, :, 0:L - tap]
                        dst = acc[:, k, :].rearrange("p (i t) -> p i t", i=GI)[:, :, tap:L]
                        V.scalar_tensor_tensor(out=dst, in0=src, scalar=cv[:, k, TAPS - 1 - tap:TAPS - tap], in1=dst,
                                               op0=ALU.mult, op1=ALU.add).then_inc(conv_step, 1)
                        yield

            def conv_pair(g, k0):
                for _ in conv_steps(g, k0):
                    pass

            def dt_and_conv(g):
                convolution = conv_steps(g, 0)
                for n, _ in enumerate(dt_steps(g)):
                    if n >= 2 and n % 2 == 0:
                        next(convolution, None)
                for _ in convolution:
                    pass

            def residual(g):
                dve.wait_ge(out_proj, g.n + 1)
                V.tensor_tensor(res[:, :], b_c[:, 0:T], xn[g.parity][:, :], ALU.add).then_inc(res_ready, 1)

            def residual_norm(g):
                dve.wait_ge(res_rstd, g.n + 1)
                V.tensor_tensor(res[:, :], res[:, :], po_rs[:, :], ALU.mult).then_inc(res_scaled, 1)
                dve.wait_ge(res_scaled, g.n + 1)
                V.tensor_tensor(h1[:, :], res[:, :], h[g.parity][:, :], ALU.add).then_inc(h1_ready, 1)

            def post_scale(g):
                dve.wait_ge(po_rstd, g.n + 1)
                V.tensor_tensor(xs[:, :], b_c[:, 0:T], po_rs[:, :], ALU.mult).then_inc(xs_ready, 1)

            def copy_rows(g):
                dve.wait_ge(rows_turned, g.n + 1)
                dve.wait_ge(rows_stored, 16 * g.n + 16)
                V.tensor_copy(xs_all[:, bass.ds(g.n * TPG, TPG), :].rearrange("p k d -> p (k d)"), b_c[0:TT, 0:TPG * D])
                V.tensor_copy(logit[:, bass.ds(g.n, 1), :].rearrange("p o k -> p (o k)"), b_c[0:TT, TPG * D:TPG * (D + E_N)])
                V.tensor_copy(h1_t[:, :], b_v[0:TT, 0:TPG * D]).then_inc(rows_copied, 1)

            def copy_turned_x(g, c):
                dve.wait_ge(x_turned, NC * g.n + c + 1)
                V.tensor_copy(xdt_t[:, c, :, :].rearrange("p i d -> p (i d)"), XT_B[c][0:QR, 0:GI * D]).then_inc(x_turned_copied, 1)

            def copy_turned_b(g):
                for c in range(2):
                    dve.wait_ge(b_turned, 2 * g.n + c + 1)
                    V.tensor_copy(b_t[:, c, :, :].rearrange("p i d -> p (i d)"), BT_B[c][0:QR, 0:GI * D]
                      ).then_inc(b_turned_copied, 1)

            def x_times_dt(g):
                dve.wait_ge(x_act, g.n + 1)
                dve.wait_ge(spread, g.n + 1)
                if not g.first():
                    dve.wait_ge(yg_ready, g.n)
                v = b_sp[:, 0:SP_G].rearrange("p (c i t) -> p c i t", c=NC, i=GI)
                for c in range(NC):
                    dt_v = v[:, c, :, :].rearrange("p i (t o) -> p i t o", o=1).broadcast_to([128, GI, Q, RANK])
                    V.tensor_tensor(xdt[:, c, :, :].rearrange("p i (t r) -> p i t r", r=RANK), dt_v,
                                    xc[:, :, c, :].rearrange("p i (t r) -> p i t r", r=RANK), ALU.mult).then_inc(xdt_ready, 1)

            def weigh(g, c):
                dve.wait_ge(scores, NC * g.n + c + 1)
                dve.wait_ge(decay_ready, NC * g.n + c + 1)
                for i in range(GI):
                    s = G_B[c][0:QR, i * QR:(i + 1) * QR].rearrange("p (o t r) -> p o t r", o=1, r=RANK)
                    d = decay[:, c, i, :, :].rearrange("p h (t o) -> p h t o", o=1)
                    V.tensor_tensor(m[:, c, i, :, :].rearrange("p h (t r) -> p h t r", r=RANK),
                                    s.broadcast_to([QR, HEADS, Q, RANK]), d.broadcast_to([QR, HEADS, Q, RANK]), ALU.mult
                                    ).then_inc(m_ready, 1)

            def scale_inter(g):
                for c in (1, 2):
                    dve.wait_ge(inter, 2 * g.n + c)
                    gr = grow[:, c - 1, :, :].rearrange("p i (t o) -> p i t o", o=1).broadcast_to([128, GI, Q, RANK])
                    V.tensor_tensor(t1[:, c - 1, :, :].rearrange("p i (t r) -> p i t r", r=RANK),
                                    I_B[c - 1][:, 0:GI * QR].rearrange("p (i t r) -> p i t r", i=GI, r=RANK), gr, ALU.mult
                                    ).then_inc(inter_read, 1)

            def skip_and_intra(g, c):
                dve.wait_ge(intra, NC * g.n + c + 1)
                V.scalar_tensor_tensor(out=y[:, c, :, :], in0=xc[:, :, c, :], scalar=dtc[:, 1:2],
                                       in1=Y_B[c][:, 0:GI * QR].rearrange("p (i t) -> p i t", i=GI), op0=ALU.mult, op1=ALU.add
                                       ).then_inc(y_sum, 1)

            def body(g):
                mix, own, begin = stages(g)
                p = g.last()
                if mix:
                    copy_turned_b(p)
                    for c in range(NC):
                        copy_turned_x(p, c)
                    weigh(p, 0)
                if own:
                    ln1_scale(g)
                if mix:
                    weigh(p, 1)
                if own:
                    dt_begin(g)
                    dt_and_conv(g)
                if mix:
                    weigh(p, 2)
                if mix:
                    scale_inter(p)
                    skip_and_intra(p, 0)
                    skip_and_intra(p, 1)
                if own:
                    conv_pair(g, 2)
                if mix:
                    skip_and_intra(p, 2)
                if own:
                    conv_pair(g, 4)
                    conv_pair(g, 6)
                if mix:
                    residual(p)
                if own:
                    conv_pair(g, 8)
                if mix:
                    residual_norm(p)
                if own:
                    conv_pair(g, 10)
                if mix:
                    post_scale(p)
                    copy_rows(p)
                if own:
                    x_times_dt(g)
                if begin:
                    tokens_bias(g.next())

            V.memset(eps[:, :], EPS).then_inc(setup_done, 1)
            V.memset(ones_e[:, :], 1.0).then_inc(setup_done, 1)
            dve.wait_ge(loaded, N_LOADS)
            for par in range(2):
                hv = h[par][:, :].rearrange("p (i t) -> p i t", i=GI)
                V.tensor_copy(hv[:, :, 0:1], tcol[:, 1:2].rearrange("p (o t) -> p o t", o=1).broadcast_to([128, GI, 1]))
                V.tensor_scalar(hv[:, :, 1:2], tcol[:, 3:4].rearrange("p (o t) -> p o t", o=1).broadcast_to([128, GI, 1]),
                                tcol[:, 2:3], None, ALU.mult)
            dve.wait_ge(rows_copied, 1)

            def route(p):
                done = [p * N_ROUTE]

                def link(ins):
                    done[0] += 1
                    ins.then_inc(route_step, 1)
                    dve.wait_ge(route_step, done[0])

                dve.wait_ge(rows_copied, (p + 1) * GPP + 1)
                lg = logit[:, p * GPP:(p + 1) * GPP, :].rearrange("p g (k e) -> p (g k) e", e=E_N)
                full = [TT, JT, E_N]

                def row(col):
                    return c88[:, col:col + E_N].rearrange("p (o e) -> p o e", o=1).broadcast_to(full)

                def per_token(t):
                    return t.rearrange("p (j o) -> p j o", o=1).broadcast_to(full)

                src = lg
                for k in range(2):
                    link(V.tensor_reduce(top[k][:, :], src, AX.X, ALU.max))
                    link(V.tensor_tensor(ra[:, :, :], src, per_token(top[k][:, :]), ALU.is_equal))
                    link(V.scalar_tensor_tensor(out=ra[:, :, :], in0=ra[:, :, :], scalar=-float(E_N), in1=row(S_IOTA8),
                                                op0=ALU.mult, op1=ALU.add))
                    link(V.tensor_reduce(idx[:, :], ra[:, :, :], AX.X, ALU.min))
                    link(V.tensor_tensor(onehot[k][:, :, :], row(S_IOTA), per_token(idx[:, :]), ALU.is_equal))
                    if k == 0:
                        link(V.scalar_tensor_tensor(out=rb[:, :, :], in0=onehot[0][:, :, :], scalar=-HIDDEN, in1=lg,
                                                    op0=ALU.mult, op1=ALU.add))
                        src = rb[:, :, :]
                link(V.tensor_tensor(both[:, :, :], onehot[0][:, :, :], onehot[1][:, :, :], ALU.add))
                assert done[0] == p * N_ROUTE + R_BOTH, done
                link(V.tensor_scalar(slot_f[:, :], top[0][:, :], -1.0, None, ALU.mult))
                link(V.tensor_tensor(rd[:, :], top[1][:, :], slot_f[:, :], ALU.add))
                assert done[0] == p * N_ROUTE + R_DIFF, done
                dve.wait_ge(route_exp, p + 1)
                link(V.tensor_scalar(idx[:, :], rd[:, :], 1.0, None, ALU.add))
                link(V.reciprocal(wgt[0][:, p, :], idx[:, :]))
                link(V.tensor_tensor(wgt[1][:, p, :], rd[:, :], wgt[0][:, p, :], ALU.mult))
                dve.wait_ge(route_mm, p + 1)
                n = JT * E_N
                link(V.tensor_copy(rtot[:, :, :], b_tok[0:TT, n:2 * n].rearrange("p (j e) -> p e j", e=E_N)))
                link(V.tensor_tensor_scan(rsum[:, :, :].rearrange("p e j -> p (e j)"), c88[:, S_MASK:S_MASK + n],
                                          rtot[:, :, :].rearrange("p e j -> p (e j)"), 0.0, ALU.mult, ALU.add))
                kfull = [TT, E_N, KMAX]
                link(V.tensor_tensor(cmp_k[:, :, :], rsum[:, :, JT - 1:JT].broadcast_to(kfull),
                                     c88[:, S_KIO:S_KIO + E_N * KMAX].rearrange("p (e k) -> p e k", e=E_N), ALU.is_gt))
                link(V.tensor_reduce(ntile[:, :], cmp_k[:, :, :], AX.X, ALU.add))
                link(V.tensor_tensor_scan(endt[:, :], ones_e[:, :], ntile[:, :], 0.0, ALU.mult, ALU.add))
                link(V.tensor_tensor(base[:, :], endt[:, :], ntile[:, :], ALU.subtract))
                tfull = [TT, NT, E_N]
                link(V.tensor_tensor(cmp_t[:, :, :], c88[:, S_TIO:S_TIO + NT * E_N].rearrange("p (t e) -> p t e", e=E_N),
                                     endt[:, :].rearrange("p (o e) -> p o e", o=1).broadcast_to(tfull), ALU.is_ge))
                link(V.tensor_reduce(tile_f[:, :], cmp_t[:, :, :], AX.X, ALU.add))
                link(V.tensor_scalar(tile_e[0:1, p, :], tile_f[0:1, :], float(E_N - 1), None, ALU.min))
                link(V.tensor_tensor(rsum[:, :, :], rsum[:, :, :], rtot[:, :, :], ALU.subtract))
                assert done[0] == (p + 1) * N_ROUTE, done
                V.tensor_tensor(ra[:, :, :], b_tok[0:TT, 0:n].rearrange("p (j e) -> p j e", e=E_N),
                                rsum[:, :, :].rearrange("p e j -> p j e"), ALU.add).then_inc(slot_step, 1)
                dve.wait_ge(slot_step, 7 * p + 1)
                V.scalar_tensor_tensor(out=ra[:, :, :], in0=base[:, :].rearrange("p (o e) -> p o e", o=1).broadcast_to(full),
                                       scalar=float(SL), in1=ra[:, :, :], op0=ALU.mult, op1=ALU.add).then_inc(slot_step, 1)
                dve.wait_ge(slot_step, 7 * p + 2)
                V.tensor_tensor(rb[:, :, :], ra[:, :, :], onehot[0][:, :, :], ALU.mult)
                V.tensor_tensor(both[:, :, :], ra[:, :, :], onehot[1][:, :, :], ALU.mult).then_inc(slot_step, 1)
                dve.wait_ge(slot_step, 7 * p + 3)
                for k, src in enumerate((rb, both)):
                    V.tensor_reduce(slot_f[:, :], src[:, :, :], AX.X, ALU.add).then_inc(slot_step, 1)
                    dve.wait_ge(slot_step, 7 * p + 4 + 2 * k)
                    V.tensor_copy(slot_u[:, p, :, k], slot_f[:, :]).then_inc(slot_step, 1)
                    dve.wait_ge(slot_step, 7 * p + 5 + 2 * k)
                V.tensor_copy(idx[:, :], slot_f[:, :]).then_inc(routed, 1)
                dve.wait_ge(routed, p + 1)

            tokens_bias(Group(0, 0, 0))
            over_groups(dve, body, lambda: route(0))
            route(1)

            tiles = tile_e[:, :, :].rearrange("o p t -> o (p t)")

            def expert(n):
                return dve.value_load(tiles[0:1, bass.ds(n, 1)], min_val=0, max_val=E_N - 1)

            def turned(n, s):
                dve.wait_ge(fx_turned, n + 1)
                if not isinstance(n, int) or n >= 2:
                    dve.wait_ge(hidden_mm, n - 1)
                V.tensor_copy(fxt[s], bank[s][:, 0:SL]).then_inc(fx_copied, 1)

            def stage_w1(n, s):
                e = expert(n)
                if not isinstance(n, int) or n >= 2:
                    dve.wait_ge(hidden_act, n - 1)
                V.tensor_copy(fw1[s], wall[:, bass.ds(e, 1), 0:W1C].rearrange("p o c -> p (o c)")).then_inc(w1_staged, 1)

            def stage_w2(n, s):
                e = expert(n)
                if not isinstance(n, int) or n >= 2:
                    dve.wait_ge(y_biased, n - 1)
                V.tensor_copy(fw2[s], wall[:, bass.ds(e, 1), W1C:WCOLS].rearrange("p o c -> p (o c)")).then_inc(w2_staged, 1)

            def add_bias(n, s, before):
                dve.wait_ge(y_mm, n + 1)
                dve.wait_ge(fy_stored[s], before * 16 + 16)
                V.tensor_tensor(fy[s], bank[4 + s][:, 0:D], fw2[s][:, FF:W2C], ALU.add).then_inc(y_biased, 1)

            dve.wait_ge(experts_loaded, 16)
            n = PARTS * NT
            turned(0, 0)
            stage_w1(0, 0)
            turned(1, 1)
            stage_w1(1, 1)
            stage_w2(0, 0)
            turned(2, 0)
            stage_w1(2, 0)
            stage_w2(1, 1)
            with dve.Fori(0, (n - 4) // 2) as i:
                turned(2 * i + 3, 1)
                stage_w1(2 * i + 3, 1)
                add_bias(2 * i, 0, i)
                stage_w2(2 * i + 2, 0)
                turned(2 * i + 4, 0)
                stage_w1(2 * i + 4, 0)
                add_bias(2 * i + 1, 1, i)
                stage_w2(2 * i + 3, 1)
            turned(n - 1, 1)
            stage_w1(n - 1, 1)
            add_bias(n - 4, 0, n // 2 - 2)
            stage_w2(n - 2, 0)
            add_bias(n - 3, 1, n // 2 - 2)
            stage_w2(n - 1, 1)
            add_bias(n - 2, 0, n // 2 - 1)
            add_bias(n - 1, 1, n // 2 - 1)

            def combine(k, b):
                s = b % 2
                dve.wait_ge(gathered[b // 2], 64 * k + 64)
                dve.wait_ge(gh_loaded[s], 32 * k + (16 * (b // 2) + 16))
                j = 4 * k + (b - JT)
                V.scalar_tensor_tensor(out=gh[s][:, :], in0=gy[b][0][:, :], scalar=wgt[0][:, 1, bass.ds(j, 1)], in1=gh[s][:, :],
                                       op0=ALU.mult, op1=ALU.add).then_inc(first_added, 1)
                dve.wait_ge(first_added, 4 * k + (b + 1))
                dve.wait_ge(out_stored[s], 32 * k + (16 * (b // 2) + 16))
                V.scalar_tensor_tensor(out=go[s][:, :], in0=gy[b][1][:, :], scalar=wgt[1][:, 1, bass.ds(j, 1)], in1=gh[s][:, :],
                                       op0=ALU.mult, op1=ALU.add).then_inc(combined, 1)

            with dve.Fori(JT // 4, JT // 2) as i:
                for b in range(4):
                    combine(i, b)

        @block.gpsimd
        def _(pool):
            P = nc.gpsimd

            def segment_rows(g):
                pool.wait_ge(dt_step, N_DT * g.n + DT_A)
                if not g.first():
                    pool.wait_ge(seg_summed, NC * g.n)
                    pool.wait_ge(spread, g.n)
                n = NC * GI * HEADS
                a = da_s[:, :, :, :].rearrange("p c i (h o) -> p (c i h) o", o=1).broadcast_to([Q, n, Q])
                tri = c88[0:Q, S_IT + Q:S_IT + 2 * Q].rearrange("p (o t) -> p o t", o=1).broadcast_to([Q, n, Q])
                P.tensor_tensor(seg_r[0:Q, :, :], a, tri, ALU.mult).then_inc(seg_ready, 1)
                a = dt_s[:, :, :, :].rearrange("p c i (h o) -> p (c i h) o", o=1).broadcast_to([Q, n, Q])
                one = c88[0:Q, S_IT:S_IT + Q].rearrange("p (o t) -> p o t", o=1).broadcast_to([Q, n, Q])
                P.tensor_tensor(dt_diag[:, :, :], a, one, ALU.mult).then_inc(dt_widened, 1)

            def x_to_end(g):
                n = GI * HEADS
                for c in range(2):
                    pool.wait_ge(x_turned_copied, NC * g.n + c + 1)
                    d = decay[:, c, :, :, Q - 1:Q].rearrange("p i h o -> p (i h) o").broadcast_to([QR, n, PC])
                    x = xdt_t[:, c, :, :].rearrange("p i (h q) -> p (i h) q", q=HP)[:, :, 0:PC]
                    P.tensor_tensor(xe[:, c, :, :].rearrange("p i (h q) -> p (i h) q", q=PC), x, d, ALU.mult).then_inc(xe_part, 1)
                pool.wait_ge(xe_part, 2 * g.n + 2)
                pool.wait_ge(total_ready, g.n + 1)
                t = total[:, :, :].rearrange("p i (h o) -> p (i h) o", o=1).broadcast_to([QR, n, PC])
                P.tensor_tensor(xe[:, 2, :, :].rearrange("p i (h q) -> p (i h) q", q=PC),
                                xe[:, 0, :, :].rearrange("p i (h q) -> p (i h) q", q=PC), t, ALU.mult).then_inc(xe_ready, 1)

            def gate(g):
                pool.wait_ge(z_act, RANK * (g.n + 1))
                for c in range(NC):
                    pool.wait_ge(y_sum, NC * g.n + c + 1)
                    if c:
                        pool.wait_ge(inter_read, 2 * g.n + c)
                        P.tensor_tensor(y[:, c, :, :], y[:, c, :, :], t1[:, c - 1, :, :], ALU.add).then_inc(y_total, 1)
                        pool.wait_ge(y_total, 2 * g.n + c)
                    o = yg[:, :, :].rearrange("p r (i k t) -> p r i k t", i=GI, k=NC)[:, :, :, c, :].rearrange("p r i t -> p i t r")
                    z = sz[:, :, :].rearrange("p r (i k t) -> p r i k t", i=GI, k=NC)[:, :, :, c, :].rearrange("p r i t -> p i t r")
                    last = P.tensor_tensor(o, y[:, c, :, :].rearrange("p i (t r) -> p i t r", r=RANK), z, ALU.mult)
                last.then_inc(yg_ready, 1)

            for s in range(2):
                P.memset(mark[0:1, s:s + 1], 0.0).then_inc(fy_stored[s], 16)
                P.memset(mark[0:1, 2 + s:3 + s], 0.0).then_inc(out_stored[s], 16)
            P.memset(acc[:, :, :], 0.0)
            P.memset(hs[:, :, :, :, :], 0.0).then_inc(hs_zeroed, 1)
            pool.wait_ge(hs_zeroed, 1)
            P.memset(xe[0:QR, 0, 0, 0:1], 0.0).then_inc(zeroed, 1)
            pool.wait_ge(zeroed, 1)
            pool.wait_ge(loaded, N_LOADS)

            def body(g):
                mix, own, _ = stages(g)
                if mix:
                    x_to_end(g.last())
                if own:
                    segment_rows(g)
                if mix:
                    gate(g.last())


            def take_wait():
                P.tensor_tensor(mark[0:1, 4:5], c88[0:1, 0:1], c88[0:1, 0:1], ALU.add)

            def send(p, j, s, k):
                if not (isinstance(k, int) and k == 0):
                    pool.wait_ge(sent[s], k * 32)
                for q in range(2):
                    P.tensor_copy(sc_i[s][q][:, :], slot_u[:, p, bass.ds(j, 1), q])
                P.tensor_copy(sc_x[s][:, :], xs_all[:, bass.ds(p * JT + j, 1), :].rearrange("p o d -> p (o d)")).then_inc(sc_copied, 1)
                pool.wait_ge(sc_copied, 2 * k + (s + 1))
                take_wait()
                for q in range(2):
                    P.indirect_dma_start(slot_x[p], bass.IndirectOffsetOnAxis(ap=sc_i[s][q][:, 0:1], axis=0), sc_x[s][:, :], None
                                         ).then_inc(sent[s], 16)

            def gather(p, j, h, k):
                if not (isinstance(k, int) and k == 0):
                    pool.wait_ge(combined, 4 * k + (2 * h - 2))
                P.tensor_copy(gi[h][:, :], slot_u[:, p, bass.ds(j, 2), :].rearrange("p j q -> p (j q)")).then_inc(ga_index, 1)
                pool.wait_ge(ga_index, 2 * k + (h + 1))
                take_wait()
                for o in range(2):
                    for q in range(2):
                        c = 2 * o + q
                        P.indirect_dma_start(gy[2 * h + o][q][:, :], None, slot_y[p],
                                             bass.IndirectOffsetOnAxis(ap=gi[h][:, c:c + 1], axis=0)).then_inc(gathered[h], 16)

            def combine(k, b):
                s = b % 2
                pool.wait_ge(gathered[b // 2], 64 * k + 64)
                pool.wait_ge(gh_loaded[s], 32 * k + (16 * (b // 2) + 16))
                pool.wait_ge(out_stored[s], 32 * k + (16 * (b // 2) + 16))
                for q in range(2):
                    w = wgt[q][:, 0, bass.ds(4 * k + b, 1)].broadcast_to([TT, D])
                    P.tensor_tensor(gy[b][q][:, :], gy[b][q][:, :], w, ALU.mult).then_inc(weighed, 1)
                pool.wait_ge(weighed, 8 * k + (2 * b + 1))
                P.tensor_tensor(gh[s][:, :], gh[s][:, :], gy[b][0][:, :], ALU.add).then_inc(first_added, 1)
                pool.wait_ge(weighed, 8 * k + (2 * b + 2))
                pool.wait_ge(first_added, 4 * k + (b + 1))
                P.tensor_tensor(go[s][:, :], gh[s][:, :], gy[b][1][:, :], ALU.add).then_inc(combined, 1)

            def route_waits():
                pool.wait_ge(routed, 1)
                pool.wait_ge(zeroed, 1 + 32 * PARTS)

            over_groups(pool, body, route_waits, send)
            pool.wait_ge(routed, PARTS)
            with pool.Fori(0, JT // 2) as i:
                for s in range(2):
                    send(1, 2 * i + s, s, i + JT // 2)
            for s in range(2):
                pool.wait_ge(fy_stored[s], 16 + 16 * NT // 2)
            gather(0, 0, 0, 0)
            gather(0, 2, 1, 0)
            combine(0, 0)
            combine(0, 1)
            with pool.Fori(1, JT // 4) as i:
                gather(0, 4 * i, 0, i)
                combine(i - 1, 2)
                combine(i - 1, 3)
                gather(0, 4 * i + 2, 1, i)
                combine(i, 0)
                combine(i, 1)
            combine(JT // 4 - 1, 2)
            combine(JT // 4 - 1, 3)
            for s in range(2):
                pool.wait_ge(fy_stored[s], 16 + 16 * NT)
            with pool.Fori(JT // 4, JT // 2) as i:
                for h in range(2):
                    gather(1, 4 * i + (2 * h - JT), h, i)
            for s in range(2):
                pool.wait_ge(gathered[s], 32 * PARTS * JT // 2)


def kernel(**inputs):
    import concourse.bacc as bacc
    from concourse.bass_utils import run_bass_kernel_spmd

    a = {k: np.ascontiguousarray(v) for k, v in inputs.items()}
    side = 224 // PATCH

    x = a["x"].reshape(NG, GI, CH, side, PATCH, side, PATCH).transpose(0, 2, 4, 6, 1, 3, 5).reshape(NG, K_TOK, GI * NPATCH)
    x_main = x[:, :KC * D].reshape(NG, KC, D, GI * NPATCH).transpose(0, 2, 1, 3).reshape(NG, D, KC * GI * NPATCH)
    w = a["L0_tok_W"].T
    tok_cols = np.concatenate([a["L0_tok_b"][:, None], a["cls_tok"].reshape(D, 1), a["L0_tok_class_token"].reshape(D, 1),
                               a["L0_tok_pos_embed"].T], axis=1)

    def padded(v):
        o = np.zeros(v.shape[:-1] + (HP,), v.dtype)
        o[..., :PC] = v
        return o.reshape(v.shape[:-2] + (HEADS * HP,))

    inner, wide = HEADS * RANK * PC, NST * RANK
    w_in = a["L0_attn_W_in"]

    def by_rank(v):
        return padded(v.reshape(-1, HEADS, RANK, PC).transpose(0, 2, 1, 3))

    def states_by_rank(v):
        return v.reshape(-1, NST, RANK).transpose(0, 2, 1)

    o = 2 * inner
    w_proj = np.concatenate([by_rank(w_in[:, inner:o]), states_by_rank(w_in[:, o:o + wide]),
                             states_by_rank(w_in[:, o + wide:o + 2 * wide]), by_rank(w_in[:, :inner])], axis=1)
    taps = np.concatenate([a["L0_attn_conv_w"], a["L0_attn_conv_b"][:, None]], axis=1).T
    conv = np.concatenate([by_rank(taps[:, :inner]), states_by_rank(taps[:, inner:inner + wide]),
                           states_by_rank(taps[:, inner + wide:])], axis=1)
    heads = np.stack([a["L0_attn_A_log"], a["L0_attn_D_skip"]], axis=1)
    w1 = a["L0_ffn_w1"].transpose(1, 0, 2)
    w2 = a["L0_ffn_w2"].reshape(E_N, FC, D, D).transpose(2, 0, 1, 3).reshape(D, E_N, FF)
    b1 = a["L0_ffn_b1"].reshape(E_N, FC, D).transpose(2, 0, 1)
    b2 = np.broadcast_to(a["L0_ffn_b2"][None], (D, E_N, D))
    c128, c88, seg = constants()
    arrays = {
        "x_main": x_main,
        "x_tail": x[:, KC * D:],
        "w_tok": w[:KC * D].reshape(KC, D, D).transpose(1, 0, 2).reshape(D, KC * D),
        "w_tok_tail": w[KC * D:],
        "tok_cols": tok_cols,
        "w_in": w_proj.reshape(D, -1),
        "w_dt": w_in[:, o + 2 * wide:],
        "conv": conv.transpose(2, 1, 0).reshape(D, -1),
        "dt_row": np.tile(np.concatenate([a["L0_attn_dt_bias"], a["L0_attn_A_log"]])[None], (Q, 1)),
        "dt_col": np.repeat(heads, HP, axis=0),
        "w_out": by_rank(a["L0_attn_W_out"].T).transpose(2, 1, 0).reshape(D, -1),
        "gate_w": a["L0_ffn_gate_w"].T,
        "experts": np.concatenate([w1, b1, w2, b2], axis=2).reshape(D, -1),
        "c128": c128,
        "c88": c88,
        "seg": seg,
    }
    arrays = {k: np.ascontiguousarray(v) for k, v in arrays.items()}
    nc = bacc.Bacc("TRN2", target_bir_lowering=False, num_devices=1)
    args = [nc.dram_tensor("in_" + k, v.shape, mybir.dt.from_np(v.dtype), kind="ExternalInput").ap() for k, v in arrays.items()]
    out = nc.dram_tensor("out", (B, L, D), FP32, kind="ExternalOutput").ap()
    tower(nc, *args, out)
    r = run_bass_kernel_spmd(nc, [{"in_" + k: v for k, v in arrays.items()}], core_ids=[0])
    return r.results[0]["out"]
```

```python
from contextlib import ExitStack

import numpy as np

import concourse.bass as bass
from concourse import mybir
from concourse.alu_op_type import AluOpType as ALU

FP32 = mybir.dt.float32
U32 = mybir.dt.uint32
I32 = mybir.dt.int32
ACT = mybir.ActivationFunctionType
AX = mybir.AxisListType

B, NPATCH, PATCH, CH = 64, 64, 28, 3
K_TOK = CH * PATCH * PATCH
D = 128
KC = K_TOK // D
K_TAIL = K_TOK - KC * D
L = NPATCH + 2
GI = 4
NG = B // GI
T = GI * L
HEADS, RANK, PC, NST = 4, 4, 16, 128
HP = 32
TAPS = 4
Q, NC = 22, 3
QR = Q * RANK
EPS = 1e-5
E_N, FF = 8, 512
FC = FF // D
TT = QR
TPG = T // TT
PARTS = 2
GPP = NG // PARTS
JT = GPP * TPG
TOKP = JT * TT
SL = 128
KMAX = -(-TOKP // SL)
NT = (2 * TOKP + E_N * (SL - 1)) // SL
W1C, W2C = FF + FC, FF + D
WCOLS = W1C + W2C
NCH = 12
MASKED = 1.0e4
HIDDEN = 1.0e30

C_ID, C_CEN, C_MEAN = 0, D, 2 * D
S_SEG, S_IT, S_ONE, S_UP, S_ONES, S_IOTA, S_IOTA8, S_KIO, S_TIO, S_MASK = np.cumsum(
    [0, QR, 2 * Q, QR, TT, TT, E_N, E_N, E_N * KMAX, E_N * NT]).tolist()
S_END = S_MASK + E_N * JT


def constants():
    eye = np.eye(D, dtype=np.float32)
    mean = np.full((D, D), 1.0 / D, np.float32)
    c128 = np.concatenate([eye, eye - mean, mean], axis=1)
    c88 = np.zeros((TT, S_END), np.float32)
    u, s = np.arange(Q)[:, None], np.arange(QR)[None, :] // RANK
    c88[:Q, S_SEG:S_SEG + QR] = u > s
    c88[32:32 + Q, S_SEG:S_SEG + QR] = -MASKED * (u <= s)
    t = np.arange(Q)[None, :]
    c88[:Q, S_IT:S_IT + Q] = u == t
    c88[:Q, S_IT + Q:S_IT + 2 * Q] = u <= t
    c88[:Q, S_ONE:S_ONE + QR] = 1.0
    k, p = np.arange(TT)[:, None], np.arange(TT)[None, :]
    c88[:, S_UP:S_UP + TT] = k < p
    c88[:, S_ONES:S_ONES + TT] = 1.0
    c88[:, S_IOTA:S_IOTA + E_N] = np.arange(E_N)
    c88[:, S_IOTA8:S_IOTA8 + E_N] = np.arange(E_N) + E_N
    c88[:, S_KIO:S_KIO + E_N * KMAX] = np.tile(np.arange(KMAX) * SL, E_N)
    c88[:, S_TIO:S_TIO + E_N * NT] = np.repeat(np.arange(NT), E_N)
    c88[:, S_MASK:S_MASK + E_N * JT] = np.tile(np.arange(JT) > 0, E_N)
    seg_rhs = np.zeros((32 + Q, NC * GI * HEADS, Q), np.float32)
    seg_rhs[32:] = (u > t)[:, None, :]
    return c128, c88, seg_rhs.reshape(32 + Q, -1)


class Group:

    def __init__(self, n, parity, before):
        self.n, self.parity, self.before = n, parity, before

    def next(self):
        return Group(self.n + 1, 1 - self.parity, self.before + self.parity)

    def after_next(self):
        return Group(self.n + 2, self.parity, self.before + 1)

    def last(self):
        return Group(self.n - 1, 1 - self.parity, self.before - (1 - self.parity))

    def first(self):
        return isinstance(self.n, int) and self.n == 0


def tower(nc, x_main, x_tail, w_tok, w_tok_tail, tok_cols, w_in, w_dt, conv, dt_row, dt_col, w_out,
          gate_w, experts, c128_d, c88_d, seg_d, out):
    ctx = ExitStack()
    with ctx:
        def sb(name, shape, dt=FP32):
            return ctx.enter_context(nc.sbuf_tensor(name, shape, dt))

        def sem(name):
            return ctx.enter_context(nc.semaphore(name))

        h1_rows = nc.dram_tensor("h1_rows", [NG * TPG, TT, D], FP32).ap()
        slot_x = [nc.dram_tensor(f"slot_x{p}", [NT * SL, D], FP32).ap() for p in range(PARTS)]
        slot_y = [nc.dram_tensor(f"slot_y{p}", [NT * SL, D], FP32).ap() for p in range(PARTS)]

        c128 = sb("c128", [128, 3 * D])
        c88 = sb("c88", [TT, S_END])
        wt = sb("wt", [128, KC, D])
        wtt = sb("wtt", [K_TAIL, D])
        tcol = sb("tcol", [128, 3 + L - 1])
        win = sb("win", [128, 16, D])
        wdt = sb("wdt", [128, HEADS])
        cv = sb("cv", [128, NCH, TAPS + 1])
        dtr = sb("dtr", [Q, 2 * HEADS])
        dtc = sb("dtc", [128, 2])
        wo = sb("wo", [128, RANK, D])
        gw = sb("gw", [128, E_N])
        eps = sb("eps", [128, 1])
        ident, center, mean = c128[:, C_ID:C_ID + D], c128[:, C_CEN:C_CEN + D], c128[:, C_MEAN:C_MEAN + D]

        XCOLS = KC * GI * NPATCH
        big = sb("big", [128, max(2 * XCOLS, E_N * WCOLS)])
        xm = [big[:, i * XCOLS:(i + 1) * XCOLS].rearrange("p (k t) -> p k t", k=KC) for i in range(2)]
        wall = big[:, 0:E_N * WCOLS].rearrange("p (e c) -> p e c", e=E_N)
        xt = [sb(f"xt{i}", [K_TAIL, GI * NPATCH]) for i in range(2)]
        h = [sb(f"h{i}", [128, T]) for i in range(2)]
        xn = [sb(f"xn{i}", [128, T]) for i in range(2)]
        ln_sq = sb("ln_sq", [128, T])
        ln_rs = sb("ln_rs", [128, T])
        res = sb("res", [128, T])
        po_sq = sb("po_sq", [128, T])
        po_rs = sb("po_rs", [128, T])
        h1 = sb("h1_cols", [128, T])
        xs = sb("xs", [128, T])
        xs_all = sb("xs_all", [TT, NG * TPG, D])
        h1_t = sb("h1_t", [TT, TPG * D])
        logit = sb("logit", [TT, NG, TPG * E_N])
        NDT = NC * GI * HEADS
        du = sb("du", [Q, NDT])
        dn = sb("dn", [Q, NDT])
        de = sb("de", [Q, NDT])
        dr = sb("dr", [Q, NDT])
        ds_ = sb("ds_", [Q, NDT])
        dq = sb("dq", [Q, NDT])
        dp = sb("dp", [Q, NDT])
        dt_s = sb("dt_s", [Q, NC, GI, HEADS])
        dt_diag = sb("dt_diag", [Q, NDT, Q])
        da_s = sb("da_s", [Q, NC, GI, HEADS])
        nega_r = sb("nega_r", [Q, HEADS])
        seg_r = sb("seg_r", [32 + Q, NDT, Q])
        acc = sb("acc", [128, NCH, T])
        xc = sb("xc", [128, GI, NC, QR])
        bc = sb("bc", [128, GI, NC, QR])
        cc = sb("cc", [128, GI, NC, QR])
        sz = sb("sz", [128, RANK, T])
        decay = sb("decay", [QR, NC, GI, HEADS, Q])
        grow = sb("grow", [128, 2, GI, Q])
        total = sb("total", [QR, GI, HEADS])
        xdt = sb("xdt", [128, NC, GI, QR])
        xdt_t = sb("xdt_t", [QR, NC, GI, D])
        b_t = sb("b_t", [QR, 2, GI, D])
        xe = sb("xe", [QR, 3, GI, HEADS * PC])
        hs = sb("hs", [128, GI, 2, HEADS, HP])
        m_buf = sb("m_buf", [128, NC * GI * HEADS * QR])
        m = m_buf[0:QR, :].rearrange("p (c i h t) -> p c i h t", c=NC, i=GI, h=HEADS)
        t1 = sb("t1", [128, 2, GI, QR])
        y = xdt
        yg = sb("yg", [128, RANK, T])

        bank = [ctx.enter_context(nc.psum_tensor(f"bank{i}", [128, 512], FP32)) for i in range(8)]
        b_tok, b_c, b_v, b_dt, b_sp = bank[:5]
        RING = bank[5:8]
        NR = len(RING)
        XT_B, BT_B, G_B, I_B, Y_B, H_B = [b_dt, b_v, b_c], [b_c, b_sp], [b_sp, b_v, b_sp], [b_dt, b_sp], [b_c, b_v, b_dt], b_c

        loaded, zeroed, hs_zeroed, setup_done = map(sem, ["loaded", "zeroed", "hs_zeroed", "setup_done"])
        x_loaded = [sem(f"x_loaded{i}") for i in range(2)]
        names = """tok_summed h_ready ln_centered ln_squared ln_var ln_log ln_rstd xn_ready
            out_proj res_ready res_squared res_var res_log res_rstd res_scaled h1_ready po_centered po_squared po_var
            po_log po_rstd xs_ready rows_turned rows_copied rows_stored
            dt_raw dt_exp dt_step seg_ready dt_widened seg_summed decay_ready spread grow_ready total_ready
            proj tap0 conv_step x_act b_act z_act c_act xdt_ready
            x_turned x_turned_copied b_turned b_turned_copied xe_ready states states_copied
            scores m_ready inter inter_read intra y_sum y_total yg_ready""".split()
        S = {n: sem(n) for n in names}
        (tok_summed, h_ready, ln_centered, ln_squared, ln_var, ln_log, ln_rstd, xn_ready,
         out_proj, res_ready, res_squared, res_var, res_log, res_rstd, res_scaled, h1_ready, po_centered, po_squared,
         po_var, po_log, po_rstd, xs_ready, rows_turned, rows_copied, rows_stored,
         dt_raw, dt_exp, dt_step, seg_ready, dt_widened, seg_summed, decay_ready, spread, grow_ready, total_ready,
         proj, tap0, conv_step, x_act, b_act, z_act, c_act, xdt_ready,
         x_turned, x_turned_copied, b_turned, b_turned_copied, xe_ready, states, states_copied,
         scores, m_ready, inter, inter_read, intra, y_sum, y_total, yg_ready) = [S[n] for n in names]

        SP_G = NC * GI * Q
        SP_T = SP_G + (NC - 1) * GI * Q
        N_DT = 17
        DT_NEG, DT_A = 2, 17
        N_CONV = NCH * (TAPS - 1)
        N_ROUTE, R_BOTH, R_DIFF = 27, 12, 14

        def conv_at(chunk, tap):
            return (chunk // 2) * 2 * (TAPS - 1) + (tap - 1) * 2 + chunk % 2 + 1

        def conv_all(chunk):
            return conv_at(chunk, TAPS - 1)

        def by_chunk(buf):
            return buf.rearrange("p i c (t r) -> p i (c t) r", r=RANK)

        token_loads = [(wt[:, :, :], w_tok.rearrange("p (k d) -> p k d", d=D)), (wtt[:, :], w_tok_tail)]
        loads = [(tcol[:, :], tok_cols), (c128[:, :], c128_d), (c88[:, :], c88_d), (win[:, :, :], w_in.rearrange("p (k d) -> p k d", d=D)),
                 (wdt[:, :], w_dt), (cv[:, :, :], conv.rearrange("p (k d) -> p k d", d=TAPS + 1)),
                 (dtr[:, :], dt_row), (dtc[:, :], dt_col),
                 (wo[:, :, :], w_out.rearrange("p (k d) -> p k d", d=D)), (gw[:, :], gate_w),
                 (seg_r[:, :, :], seg_d.rearrange("p (k d) -> p k d", d=Q))]
        N_LOADS = 16 * len(loads)
        tokens_loaded, experts_loaded = sem("tokens_loaded"), sem("experts_loaded")

        onehot = [sb(f"onehot{i}", [TT, JT, E_N]) for i in range(2)]
        both = sb("both", [TT, JT, E_N])
        ra = sb("ra", [TT, JT, E_N])
        rb = sb("rb", [TT, JT, E_N])
        top = [sb(f"top{i}", [TT, JT]) for i in range(2)]
        idx = sb("idx", [TT, JT])
        rd = sb("rd", [TT, JT])
        rsum = sb("rsum", [TT, E_N, JT])
        rtot = sb("rtot", [TT, E_N, JT])
        cmp_k = sb("cmp_k", [TT, E_N, KMAX])
        ntile = sb("ntile", [TT, E_N])
        endt = sb("endt", [TT, E_N])
        base = sb("base", [TT, E_N])
        ones_e = sb("ones_e", [TT, E_N])
        cmp_t = sb("cmp_t", [TT, NT, E_N])
        tile_f = sb("tile_f", [TT, NT])
        wgt = [sb(f"wgt{i}", [TT, PARTS, JT]) for i in range(2)]
        slot_f = sb("slot_f", [TT, JT])
        slot_u = sb("slot_u", [TT, PARTS, JT, 2], U32)
        tile_e = sb("tile_e", [1, PARTS, NT], I32)

        mark = sb("mark", [1, 5])
        sc_x = [sb(f"sc_x{i}", [TT, D]) for i in range(2)]
        sc_i = [[sb(f"sc_i{i}{k}", [TT, 1], U32) for k in range(2)] for i in range(2)]
        acc_f = acc[:, :, :].rearrange("p k t -> p (k t)")
        in_m = np.cumsum([0] + [WCOLS] * 2 + [D] * 2 + [FC * SL] * 2 + [D] * 2).tolist()
        assert 4 * D + 2 * WCOLS <= NCH * T and in_m[-1] <= NC * GI * HEADS * QR

        def part_of_m(k):
            return m_buf[:, in_m[k]:in_m[k + 1]]

        fx = [acc_f[:, i * D:(i + 1) * D] for i in range(4)]
        fw = [part_of_m(i) for i in range(2)] + [
            acc_f[:, 4 * D + i * WCOLS:4 * D + (i + 1) * WCOLS] for i in range(2)]
        fxt = [part_of_m(2 + i) for i in range(2)]
        fh = [part_of_m(4 + i).rearrange("p (k t) -> p k t", k=FC) for i in range(2)]
        fy = [part_of_m(6 + i) for i in range(2)]
        gy = [[sb(f"gy{i}{k}", [TT, D]) for k in range(2)] for i in range(4)]
        gi = [sb(f"gi{i}", [TT, 4], U32) for i in range(2)]
        gh = [sb(f"gh{i}", [TT, D]) for i in range(2)]
        go = [sb(f"go{i}", [TT, D]) for i in range(2)]

        route_step, route_mm, route_exp, routed = map(sem, ["route_step", "route_mm", "route_exp", "routed"])
        slot_step, xe_part, sc_copied = map(sem, ["slot_step", "xe_part", "sc_copied"])
        sent = [sem(f"sent{i}") for i in range(2)]
        fx_loaded = [sem(f"fx_loaded{i}") for i in range(4)]
        fx_turned, fx_copied, w_staged, hidden_mm, hidden_act, y_mm, y_biased = map(
            sem, ["fx_turned", "fx_copied", "w_staged", "hidden_mm", "hidden_act", "y_mm", "y_biased"])
        fy_stored = [sem(f"fy_stored{i}") for i in range(2)]
        ga_index = sem("ga_index")
        gathered = [sem(f"gathered{i}") for i in range(2)]
        gh_loaded = [sem(f"gh_loaded{i}") for i in range(2)]
        first_added, combined = sem("first_added"), sem("combined")
        out_stored = [sem(f"out_stored{i}") for i in range(2)]

        def over_groups(eng, body, between, send=None):
            body(Group(0, 0, 0))
            with eng.Fori(0, GPP // 2) as i:
                body(Group(2 * i + 1, 1, i))
                body(Group(2 * i + 2, 0, i + 1))
            between()
            if send:
                for s in range(2):
                    send(0, s, s, 0)
            with eng.Fori(GPP // 2, (NG - 2) // 2) as i:
                for half in range(2):
                    body(Group(2 * i + 1 + half, 1 - half, i + half))
                    for o in range(3 * half, 3 * half + 3):
                        if send:
                            send(0, 6 * i + (2 + o - 3 * GPP), o % 2, 3 * i + (1 + o // 2 - 3 * GPP // 2))
            for n in (NG - 1, NG):
                body(Group(n, n % 2, n // 2))
                for s in range(2):
                    if send:
                        send(0, JT + 2 * (n - NG) - 2 + s, s, JT // 2 + (n - NG) - 1)

        def stages(g):
            n = g.n if isinstance(g.n, int) else 1
            return n > 0, n < NG, n < NG - 1

        MIXED = (NT - 8) // 16
        assert PARTS == 2 and 16 * MIXED == NT - 8 and 12 * MIXED == JT

        block = ctx.enter_context(nc.Block())

        @block.sync
        def _(sp):
            def load_x(g):
                sp.dma_start(xm[g.parity][:, :, :], x_main[bass.ds(g.n, 1), :, :].rearrange("o p (k d) -> (o p) k d", k=KC)
                             ).then_inc(x_loaded[g.parity], 16)
                sp.dma_start(xt[g.parity][:, :], x_tail[bass.ds(g.n, 1), :, :].rearrange("o p d -> (o p) d")
                             ).then_inc(x_loaded[g.parity], 16)

            def store_rows(g):
                sp.wait_ge(rows_copied, g.n + 2)
                sp.dma_start(h1_rows[bass.ds(g.n * TPG, TPG), :, :].rearrange("k p d -> p k d"),
                             h1_t[:, :].rearrange("p (k d) -> p k d", d=D)).then_inc(rows_stored, 16)

            for dst, src in token_loads:
                sp.dma_start(dst, src).then_inc(tokens_loaded, 16)
            load_x(Group(0, 0, 0))
            for dst, src in loads:
                sp.dma_start(dst, src).then_inc(loaded, 16)
            load_x(Group(1, 1, 0))
            sp.wait_ge(zeroed, 1)
            half = NT * D // 2
            for p in range(PARTS):
                for k in range(2):
                    sp.dma_start(slot_x[p].rearrange("(p k) d -> p (k d)", p=128)[:, k * half:(k + 1) * half],
                                 m_buf[:, :half]).then_inc(zeroed, 16)

            def body(g):
                sp.wait_ge(tok_summed, g.n + 1)
                load_x(g.after_next())
                if not g.first():
                    store_rows(g.last())

            body(Group(0, 0, 0))
            with sp.Fori(0, (NG - 4) // 2) as i:
                body(Group(2 * i + 1, 1, i))
                body(Group(2 * i + 2, 0, i + 1))
            body(Group(NG - 3, 1, (NG - 4) // 2))
            sp.wait_ge(tok_summed, NG)
            sp.dma_start(wall, experts.rearrange("p (e c) -> p e c", e=E_N)).then_inc(experts_loaded, 16)
            for n in range(NG - 3, NG):
                store_rows(Group(n, n % 2, n // 2))
            sp.wait_ge(rows_stored, 16 * (NG + 1))

            def load_fx(p, i, b):
                if not isinstance(i, int) or p or i >= 4:
                    sp.wait_ge(fx_turned, i + (p * NT - 3))
                sp.dma_start(fx[b], slot_x[p][bass.ds(i * SL, SL), :]).then_inc(fx_loaded[b], 16)

            def store_fy(p, i, s):
                sp.wait_ge(y_biased, i + (p * NT + 1))
                sp.dma_start(slot_y[p][bass.ds(i * SL, SL), :], fy[s]).then_inc(fy_stored[s], 16)

            def all_sent(p):
                for s in range(2):
                    sp.wait_ge(sent[s], 32 * (p + 1) * (JT // 2))

            AHEAD = 4

            def load_h1(j, s):
                sp.dma_start(gh[s][:, :], h1_rows[bass.ds(j, 1), :, :].rearrange("o p d -> (o p) d")).then_inc(gh_loaded[s], 16)

            def store_out(j, s):
                sp.wait_ge(combined, j + 1)
                rows = out.rearrange("b l d -> (b l) d").rearrange("(k q) d -> k q d", q=TT)
                sp.dma_start(rows[bass.ds(j, 1), :, :].rearrange("o p d -> (o p) d"), go[s][:, :]).then_inc(out_stored[s], 16)

            all_sent(0)
            for k in range(AHEAD):
                load_fx(0, k, k)
            with sp.Fori(0, (NT - AHEAD) // 4) as i:
                for k in range(4):
                    load_fx(0, 4 * i + (AHEAD + k), k)
                    store_fy(0, 4 * i + k, k % 2)
            all_sent(1)
            for k in range(AHEAD):
                load_fx(1, k, k)
                store_fy(0, NT - AHEAD + k, k % 2)
            for s in range(2):
                load_h1(s, s)
            for k in range(4):
                load_fx(1, AHEAD + k, k)
                store_fy(1, k, k % 2)
            with sp.Fori(0, MIXED) as i:
                for k in range(16):
                    load_fx(1, 16 * i + (4 + AHEAD + k), k % 4)
                    store_fy(1, 16 * i + (4 + k), k % 2)
                    if k % 4 < 3:
                        o = 3 * (k // 4) + k % 4
                        store_out(12 * i + o, o % 2)
                        load_h1(12 * i + (2 + o), o % 2)
            for k in range(AHEAD):
                store_fy(1, NT - AHEAD + k, k % 2)
            with sp.Fori(JT // 2, JT - 1) as i:
                for s in range(2):
                    store_out(2 * i + s, s)
                    load_h1(2 * i + (2 + s), s)
            for s in range(2):
                store_out(2 * JT - 2 + s, s)
            for s in range(2):
                sp.wait_ge(out_stored[s], 16 + 16 * PARTS * JT // 2)

        @block.tensor
        def _(pe):
            mm = nc.tensor.matmul

            def turn(dst, src):
                return mm(dst, src, ident, start=True, stop=True, is_transpose=True)

            def tokens(g, k0, k1):
                if k0 == 0:
                    pe.wait_ge(x_loaded[g.parity], 32 * g.before + 32)
                    if not g.first():
                        pe.wait_ge(xn_ready, g.n)
                ps = b_tok[:, 0:GI * NPATCH]
                for k in range(k0, min(k1, KC)):
                    mm(ps, wt[:, k, :], xm[g.parity][:, k, :], start=(k == 0), stop=False)
                if k1 > KC:
                    mm(ps, wtt[:, :], xt[g.parity][:, :], start=False, stop=True).then_inc(tok_summed, 1)

            def ln1_center(g):
                pe.wait_ge(h_ready, g.n + 1)
                mm(b_tok[:, 0:T], center, h[g.parity][:, :], start=True, stop=True).then_inc(ln_centered, 1)

            def ln1_var(g):
                pe.wait_ge(ln_squared, g.n + 1)
                if not g.first():
                    pe.wait_ge(x_turned_copied, NC * (g.n - 1) + 1)
                mm(b_dt[:, 0:T], mean, ln_sq[:, :], start=True, stop=True).then_inc(ln_var, 1)

            def dt_project(g):
                pe.wait_ge(xn_ready, g.n + 1)
                for c in range(NC):
                    for i in range(GI):
                        o = (c * GI + i) * HEADS
                        last = mm(b_dt[0:Q, o:o + HEADS], xn[g.parity][:, i * L + c * Q:i * L + (c + 1) * Q], wdt[:, :],
                                  start=True, stop=True)
                last.then_inc(dt_raw, 1)

            def project(g, k):
                if k == 15:
                    pe.wait_ge(z_act, RANK * g.n + 1)
                elif k >= NR:
                    pe.wait_ge(conv_step, N_CONV * g.n + conv_all(k - NR))
                elif k == 0 and not g.first():
                    pe.wait_ge(z_act, RANK * g.n)
                mm(RING[k % NR][:, 0:T], win[:, k, :], xn[g.parity][:, :], start=True, stop=True).then_inc(proj, 1)

            def segments(g, c):
                if c == 0:
                    pe.wait_ge(seg_ready, g.n + 1)
                    if not g.first():
                        pe.wait_ge(y_sum, NC * g.n)
                else:
                    pe.wait_ge(decay_ready, NC * g.n + c)
                n = GI * HEADS
                mm(b_dt[0:QR, 0:n * Q], c88[0:32 + Q, S_SEG:S_SEG + QR], seg_r[:, c * n:(c + 1) * n, :],
                   start=True, stop=True).then_inc(seg_summed, 1)

            def spread_dt(g):
                pe.wait_ge(dt_widened, g.n + 1)
                if not g.first():
                    pe.wait_ge(inter_read, 2 * g.n)
                mm(b_sp[0:QR, SP_T:SP_T + GI * HEADS], c88[0:Q, S_ONE:S_ONE + QR], da_s[:, 1, :, :].rearrange("p i h -> p (i h)"),
                   start=True, stop=True)
                ones = c88[0:Q, S_ONES:S_ONES + HP]
                for k in range(HEADS):
                    dt_k = dt_diag[:, :, :].rearrange("p (n h) t -> p n h t", h=HEADS)[:, :, k, :]
                    mm(b_sp[HP * k:HP * (k + 1), 0:NC * GI * Q], ones, dt_k, start=True, stop=True)
                for k in range(HEADS):
                    sum_k = seg_r[0:Q, GI * HEADS:NDT, :].rearrange("p (n h) t -> p n h t", h=HEADS)[:, :, k, :]
                    last = mm(b_sp[HP * k:HP * (k + 1), SP_G:SP_T], ones, sum_k, start=True, stop=True)
                last.then_inc(spread, 1)

            def out_project(g):
                pe.wait_ge(yg_ready, g.n + 1)
                for r in range(RANK):
                    last = mm(b_c[:, 0:T], wo[:, r, :], yg[:, r, :], start=(r == 0), stop=(r == RANK - 1))
                last.then_inc(out_proj, 1)

            def res_mean(g):
                pe.wait_ge(res_squared, g.n + 1)
                mm(b_v[:, 0:T], mean, po_sq[:, :], start=True, stop=True).then_inc(res_var, 1)

            def post_center(g):
                pe.wait_ge(h1_ready, g.n + 1)
                mm(b_c[:, 0:T], center, h1[:, :], start=True, stop=True).then_inc(po_centered, 1)

            def post_var(g):
                pe.wait_ge(po_squared, g.n + 1)
                mm(b_v[:, 0:T], mean, po_sq[:, :], start=True, stop=True).then_inc(po_var, 1)

            def rows_and_logits(g):
                pe.wait_ge(xs_ready, g.n + 1)
                for k in range(TPG):
                    turn(b_c[0:TT, k * D:(k + 1) * D], xs[:, k * TT:(k + 1) * TT])
                for k in range(TPG):
                    mm(b_c[0:TT, TPG * D + k * E_N:TPG * D + (k + 1) * E_N], xs[:, k * TT:(k + 1) * TT], gw[:, :],
                       start=True, stop=True)
                for k in range(TPG):
                    last = turn(b_v[0:TT, k * D:(k + 1) * D], h1[:, k * TT:(k + 1) * TT])
                last.then_inc(rows_turned, 1)

            def turn_b(g):
                pe.wait_ge(b_act, g.n + 1)
                pe.wait_ge(rows_copied, g.n + 1)
                pe.wait_ge(xdt_ready, NC * (g.n + 1))
                pe.wait_ge(total_ready, g.n + 1)
                for c in range(2):
                    for i in range(GI):
                        last = turn(BT_B[c][0:QR, i * D:(i + 1) * D], bc[:, i, c, :])
                    last.then_inc(b_turned, 1)

            def turn_x(g):
                for c in range(NC):
                    if c == 2:
                        pe.wait_ge(b_turned_copied, 2 * g.n + 1)
                    for i in range(GI):
                        last = turn(XT_B[c][0:QR, i * D:(i + 1) * D], xdt[:, c, i, :])
                    last.then_inc(x_turned, 1)

            def score(g, c):
                if c == 0:
                    pe.wait_ge(c_act, g.n + 1)
                    pe.wait_ge(b_turned_copied, 2 * g.n + 2)
                elif c == 1:
                    pe.wait_ge(x_turned_copied, NC * g.n + 2)
                else:
                    pe.wait_ge(m_ready, NC * GI * g.n + GI)
                for i in range(GI):
                    last = mm(G_B[c][0:QR, i * QR:(i + 1) * QR], bc[:, i, c, :], cc[:, i, c, :], start=True, stop=True)
                last.then_inc(scores, 1)

            def state_sums(g):
                pe.wait_ge(xe_ready, g.n + 1)
                pe.wait_ge(b_turned_copied, 2 * (g.n + 1))
                pe.wait_ge(x_turned_copied, NC * (g.n + 1))
                n = HEADS * PC
                for i in range(GI):
                    o = 2 * i * n
                    mm(H_B[:, o:o + n], b_t[:, 0, i, :], xe[:, 0, i, :], start=True, stop=True)
                    mm(H_B[:, o + n:o + 2 * n], b_t[:, 0, i, :], xe[:, 2, i, :], start=True, stop=False)
                    last = mm(H_B[:, o + n:o + 2 * n], b_t[:, 1, i, :], xe[:, 1, i, :], start=False, stop=True)
                last.then_inc(states, 1)

            def inter_product(g, c):
                if c == 1:
                    pe.wait_ge(states_copied, g.n + 1)
                    if not isinstance(g.n, int) or g.n < NG - 1:
                        pe.wait_ge(dt_step, N_DT * (g.n + 1) + 1)
                else:
                    pe.wait_ge(m_ready, NC * GI * (g.n + 1))
                for i in range(GI):
                    last = mm(I_B[c - 1][:, i * QR:(i + 1) * QR], hs[:, i, c - 1, :, :], cc[:, i, c, :], start=True, stop=True)
                last.then_inc(inter, 1)

            def intra_products(g, c):
                if c == 0:
                    pe.wait_ge(states_copied, g.n + 1)
                elif c == 2:
                    pe.wait_ge(inter_read, 2 * g.n + 1)
                for i in range(GI):
                    if i == 0 and Y_B[c] is G_B[c]:
                        pe.wait_ge(m_ready, NC * GI * g.n + (c + 1) * GI)
                    elif Y_B[c] is not G_B[c]:
                        pe.wait_ge(m_ready, NC * GI * g.n + c * GI + i + 1)
                    for k in range(HEADS):
                        last = mm(Y_B[c][HP * k:HP * (k + 1), i * QR:(i + 1) * QR], xdt_t[:, c, i, HP * k:HP * (k + 1)],
                                  m[:, c, i, k, :], start=True, stop=True)
                last.then_inc(intra, 1)

            def body(g):
                mix, own, begin = stages(g)
                p = g.last()
                if mix:
                    turn_b(p)
                    turn_x(p)
                if own:
                    ln1_center(g)
                if mix:
                    score(p, 0)
                    score(p, 1)
                if own:
                    ln1_var(g)
                if mix:
                    state_sums(p)
                if own:
                    dt_project(g)
                    for k in range(3):
                        project(g, k)
                if mix:
                    score(p, 2)
                    inter_product(p, 1)
                    intra_products(p, 0)
                    intra_products(p, 1)
                if begin:
                    tokens(g.next(), 0, 4)
                if own:
                    project(g, 3)
                if mix:
                    inter_product(p, 2)
                if own:
                    project(g, 4)
                if begin:
                    tokens(g.next(), 4, 5)
                if mix:
                    intra_products(p, 2)
                if begin:
                    tokens(g.next(), 5, 7)
                if own:
                    project(g, 5)
                    project(g, 6)
                    segments(g, 0)
                if begin:
                    tokens(g.next(), 7, 8)
                if own:
                    segments(g, 1)
                    project(g, 7)
                if begin:
                    tokens(g.next(), 8, 9)
                if own:
                    segments(g, 2)
                    project(g, 8)
                if mix:
                    out_project(p)
                if own:
                    spread_dt(g)
                if own:
                    project(g, 9)
                if begin:
                    tokens(g.next(), 9, 11)
                if mix:
                    res_mean(p)
                if own:
                    project(g, 10)
                if begin:
                    tokens(g.next(), 11, 13)
                if own:
                    project(g, 11)
                if mix:
                    post_center(p)
                if own:
                    project(g, 12)
                if begin:
                    tokens(g.next(), 13, 14)
                if mix:
                    post_var(p)
                if own:
                    project(g, 13)
                    project(g, 14)
                if begin:
                    tokens(g.next(), 14, 15)
                if mix:
                    rows_and_logits(p)
                if own:
                    project(g, 15)
                if begin:
                    tokens(g.next(), 15, KC + 1)

            pe.wait_ge(tokens_loaded, 16 * len(token_loads))
            tokens(Group(0, 0, 0), 0, KC + 1)
            pe.wait_ge(loaded, N_LOADS)

            def route(p):
                pe.wait_ge(route_step, R_BOTH + p * N_ROUTE)
                flat = both[:, :, :].rearrange("p j e -> p (j e)")
                mm(b_tok[0:TT, 0:JT * E_N], c88[:, S_UP:S_UP + TT], flat, start=True, stop=True)
                mm(b_tok[0:TT, JT * E_N:2 * JT * E_N], c88[:, S_ONES:S_ONES + TT], flat, start=True, stop=True
                   ).then_inc(route_mm, 1)
                pe.wait_ge(routed, p + 1)

            over_groups(pe, body, lambda: route(0))
            route(1)

            FT, FH, FY = [bank[0], bank[1]], [bank[2], bank[3]], [bank[4], bank[5]]

            def turn_rows(n, b, before):
                pe.wait_ge(fx_loaded[b], before * 16 + 16)
                turn(FT[b % 2][:, 0:SL], fx[b]).then_inc(fx_turned, 1)

            def up(n, b):
                s = b % 2
                pe.wait_ge(fx_copied, n + 1)
                pe.wait_ge(w_staged, n + 1)
                for k in range(FC):
                    last = mm(FH[s][:, k * SL:(k + 1) * SL], fw[b][:, k * D:(k + 1) * D], fxt[s], start=True, stop=True)
                last.then_inc(hidden_mm, 1)

            def down(n, b, first=False):
                s = b % 2
                pe.wait_ge(hidden_act, n + 1)
                if not first:
                    pe.wait_ge(y_biased, n - 1)
                for k in range(FC):
                    last = mm(FY[s][:, 0:D], fh[s][:, k, :], fw[b][:, W1C + k * D:W1C + (k + 1) * D], start=(k == 0),
                              stop=(k == FC - 1))
                last.then_inc(y_mm, 1)

            n = PARTS * NT
            turn_rows(0, 0, 0)
            turn_rows(1, 1, 0)
            up(0, 0)
            turn_rows(2, 2, 0)
            up(1, 1)
            down(0, 0, first=True)
            turn_rows(3, 3, 0)
            up(2, 2)
            down(1, 1, first=True)
            with pe.Fori(0, (n - 4) // 4) as i:
                for k in range(4):
                    turn_rows(4 * i + (4 + k), k, i + 1)
                    up(4 * i + (3 + k), (3 + k) % 4)
                    down(4 * i + (2 + k), (2 + k) % 4)
            up(n - 1, 3)
            down(n - 2, 2)
            down(n - 1, 3)

        @block.scalar
        def _(act):
            A = nc.scalar.activation

            def log_exp():
                nc.scalar.preload_act_table_set("natural_log_exp_and_others")

            def rstd(dst, var, ready, n, log_sem, out_sem):
                act.wait_ge(ready, n)
                A(dst, var, ACT.Ln, bias=eps[:, :]).then_inc(log_sem, 1)
                act.wait_ge(log_sem, n)
                A(dst, dst, ACT.Exp, scale=-0.5).then_inc(out_sem, 1)

            def ln1_square(g):
                act.wait_ge(ln_centered, g.n + 1)
                A(ln_sq[:, :], b_tok[:, 0:T], ACT.Square).then_inc(ln_squared, 1)

            def ln1_rstd(g):
                rstd(ln_rs[:, :], b_dt[:, 0:T], ln_var, g.n + 1, ln_log, ln_rstd)

            def dt_exponent(g):
                act.wait_ge(dt_step, N_DT * g.n + DT_NEG)
                A(de[:, :], dn[:, :], ACT.Exp).then_inc(dt_exp, 1)

            def first_tap(g, k):
                act.wait_ge(proj, 16 * g.n + k + 1)
                A(acc[:, k, :], RING[k % NR][:, 0:T], ACT.Identity, bias=cv[:, k, TAPS:TAPS + 1],
                  scale=cv[:, k, TAPS - 1:TAPS]).then_inc(tap0, 1)

            def decays(g, c):
                act.wait_ge(seg_summed, NC * g.n + c + 1)
                if c == 0 and not g.first():
                    act.wait_ge(m_ready, NC * GI * g.n)
                    act.wait_ge(xe_ready, g.n)
                A(decay[:, c, :, :, :].rearrange("p i h t -> p (i h t)"), b_dt[0:QR, 0:GI * HEADS * Q], ACT.Exp
                  ).then_inc(decay_ready, 1)

            def growths(g):
                act.wait_ge(spread, g.n + 1)
                A(grow[:, :, :, :].rearrange("p c i t -> p (c i t)"), b_sp[:, SP_G:SP_T], ACT.Exp).then_inc(grow_ready, 1)
                A(total[:, :, :].rearrange("p i h -> p (i h)"), b_sp[0:QR, SP_T:SP_T + GI * HEADS], ACT.Exp).then_inc(total_ready, 1)

            def silu_chunk(g, dst, k0, done):
                act.wait_ge(conv_step, N_CONV * g.n + conv_all(k0 + RANK - 1))
                if not g.first():
                    act.wait_ge(y_sum, NC * g.n)
                for r in range(RANK):
                    v = by_chunk(dst[:, :, :, :])[:, :, :, r]
                    last = A(v, acc[:, k0 + r, :].rearrange("p (i t) -> p i t", i=GI), ACT.Silu)
                last.then_inc(done, 1)

            def silu_gate(g, r):
                act.wait_ge(proj, 16 * g.n + NCH + r + 1)
                if not g.first():
                    act.wait_ge(yg_ready, g.n)
                A(sz[:, r, :], RING[(NCH + r) % NR][:, 0:T], ACT.Silu).then_inc(z_act, 1)

            def copy_states(g):
                act.wait_ge(states, g.n + 1)
                A(hs[:, :, :, :, 0:PC].rearrange("p i c h q -> p (i c h) q"),
                  H_B[:, 0:GI * 2 * HEADS * PC].rearrange("p (k q) -> p k q", q=PC), ACT.Copy).then_inc(states_copied, 1)

            def res_square(g):
                act.wait_ge(res_ready, g.n + 1)
                A(po_sq[:, :], res[:, :], ACT.Square).then_inc(res_squared, 1)

            def res_norm(g):
                rstd(po_rs[:, :], b_v[:, 0:T], res_var, g.n + 1, res_log, res_rstd)

            def post_square(g):
                act.wait_ge(po_centered, g.n + 1)
                A(po_sq[:, :], b_c[:, 0:T], ACT.Square).then_inc(po_squared, 1)

            def post_norm(g):
                rstd(po_rs[:, :], b_v[:, 0:T], po_var, g.n + 1, po_log, po_rstd)

            def body(g):
                mix, own, _ = stages(g)
                p = g.last()
                if own:
                    ln1_square(g)
                    ln1_rstd(g)
                if mix:
                    copy_states(p)
                if own:
                    dt_exponent(g)
                    for k in range(7):
                        first_tap(g, k)
                    decays(g, 0)
                    decays(g, 1)
                    first_tap(g, 7)
                    decays(g, 2)
                    first_tap(g, 8)
                    growths(g)
                    first_tap(g, 9)
                if mix:
                    res_square(p)
                if own:
                    first_tap(g, 10)
                if mix:
                    res_norm(p)
                if own:
                    first_tap(g, 11)
                if mix:
                    post_square(p)
                if mix:
                    post_norm(p)
                if own:
                    for r in range(RANK - 1):
                        silu_gate(g, r)
                    silu_chunk(g, xc, 0, x_act)
                    silu_chunk(g, bc, 4, b_act)
                    silu_gate(g, RANK - 1)
                    silu_chunk(g, cc, 8, c_act)
                    log_exp()

            log_exp()
            act.wait_ge(loaded, N_LOADS)
            A(nega_r[:, :], dtr[:, HEADS:2 * HEADS], ACT.Exp).then_inc(rows_stored, 16)
            act.wait_ge(rows_stored, 16)
            A(nega_r[:, :], nega_r[:, :], ACT.Copy, scale=-1.0).then_inc(rows_copied, 1)
            act.wait_ge(setup_done, 1)
            act.wait_ge(hs_zeroed, 1)

            def route(p):
                act.wait_ge(route_step, R_DIFF + p * N_ROUTE)
                A(rd[:, :], rd[:, :], ACT.Exp).then_inc(route_exp, 1)

            over_groups(act, body, lambda: route(0))
            route(1)

            def hidden(n, b):
                s = b % 2
                act.wait_ge(hidden_mm, n + 1)
                for k in range(FC):
                    last = A(fh[s][:, k, :], bank[2 + s][:, k * SL:(k + 1) * SL], ACT.Relu, bias=fw[b][:, FF + k:FF + k + 1])
                last.then_inc(hidden_act, 1)

            for k in range(4):
                if k >= 2:
                    act.wait_ge(y_mm, k - 1)
                hidden(k, k)
            with act.Fori(1, PARTS * NT // 4) as i:
                for k in range(4):
                    act.wait_ge(y_mm, 4 * i + (k - 1))
                    hidden(4 * i + k, k)

        @block.vector
        def _(dve):
            V = nc.vector

            def tokens_bias(g):
                dve.wait_ge(tok_summed, g.n + 1)
                V.scalar_tensor_tensor(
                    out=h[g.parity][:, :].rearrange("p (i t) -> p i t", i=GI)[:, :, 2:L],
                    in0=b_tok[:, 0:GI * NPATCH].rearrange("p (i t) -> p i t", i=GI), scalar=tcol[:, 0:1],
                    in1=tcol[:, 4:4 + NPATCH].rearrange("p (o t) -> p o t", o=1).broadcast_to([128, GI, NPATCH]),
                    op0=ALU.add, op1=ALU.mult).then_inc(h_ready, 1)

            def ln1_scale(g):
                dve.wait_ge(ln_rstd, g.n + 1)
                V.tensor_tensor(xn[g.parity][:, :], b_tok[:, 0:T], ln_rs[:, :], ALU.mult).then_inc(xn_ready, 1)

            def dt_begin(g):
                dve.wait_ge(dt_raw, g.n + 1)
                n = NC * GI
                bias = dtr[:, 0:HEADS].rearrange("p (o h) -> p o h", o=1).broadcast_to([Q, n, HEADS])
                V.tensor_tensor(du[:, :].rearrange("p (n h) -> p n h", n=n), b_dt[0:Q, 0:n * HEADS].rearrange("p (n h) -> p n h", n=n),
                                bias, ALU.add).then_inc(dt_step, 1)
                dve.wait_ge(dt_step, N_DT * g.n + 1)
                V.scalar_tensor_tensor(out=dn[:, :], in0=du[:, :], scalar=-1.0, in1=du[:, :], op0=ALU.mult, op1=ALU.min
                                       ).then_inc(dt_step, 1)

            def dt_steps(g):
                done = [2]

                def link(ins):
                    done[0] += 1
                    ins.then_inc(dt_step, 1)
                    yield
                    dve.wait_ge(dt_step, N_DT * g.n + done[0])

                dve.wait_ge(dt_exp, g.n + 1)
                yield from link(V.tensor_scalar(dr[:, :], de[:, :], 2.0, None, ALU.add))
                yield from link(V.reciprocal(dr[:, :], dr[:, :]))
                yield from link(V.tensor_tensor(ds_[:, :], de[:, :], dr[:, :], ALU.mult))
                yield from link(V.tensor_tensor(dq[:, :], ds_[:, :], ds_[:, :], ALU.mult))
                yield from link(V.tensor_scalar(dp[:, :], dq[:, :], 1.0 / 15.0, None, ALU.mult))
                for k in (13, 11, 9, 7, 5, 3):
                    yield from link(V.scalar_tensor_tensor(out=dp[:, :], in0=dp[:, :], scalar=1.0 / k, in1=dq[:, :], op0=ALU.add, op1=ALU.mult))
                yield from link(V.scalar_tensor_tensor(out=dp[:, :], in0=dp[:, :], scalar=1.0, in1=ds_[:, :], op0=ALU.add, op1=ALU.mult))
                yield from link(V.tensor_scalar(du[:, :], du[:, :], 0.0, None, ALU.max))
                yield from link(V.scalar_tensor_tensor(out=dt_s[:, :, :, :].rearrange("p c i h -> p (c i h)"), in0=dp[:, :], scalar=2.0,
                                            in1=du[:, :], op0=ALU.mult, op1=ALU.add))
                n = NC * GI
                V.tensor_tensor(da_s[:, :, :, :].rearrange("p c i h -> p (c i) h"), dt_s[:, :, :, :].rearrange("p c i h -> p (c i) h"),
                                nega_r[:, :].rearrange("p (o h) -> p o h", o=1).broadcast_to([Q, n, HEADS]), ALU.mult
                                ).then_inc(dt_step, 1)

            def conv_steps(g, k0):
                for tap in range(1, TAPS):
                    for k in (k0, k0 + 1):
                        if tap == 1:
                            dve.wait_ge(tap0, NCH * g.n + k + 1)
                        else:
                            dve.wait_ge(conv_step, N_CONV * g.n + conv_at(k, tap - 1))
                        src = RING[k % NR][:, 0:T].rearrange("p (i t) -> p i t", i=GI)[:, :, 0:L - tap]
                        dst = acc[:, k, :].rearrange("p (i t) -> p i t", i=GI)[:, :, tap:L]
                        V.scalar_tensor_tensor(out=dst, in0=src, scalar=cv[:, k, TAPS - 1 - tap:TAPS - tap], in1=dst,
                                               op0=ALU.mult, op1=ALU.add).then_inc(conv_step, 1)
                        yield

            def conv_pair(g, k0):
                for _ in conv_steps(g, k0):
                    pass

            def dt_and_conv(g):
                convolution = conv_steps(g, 0)
                for n, _ in enumerate(dt_steps(g)):
                    if n >= 2 and n % 2 == 0:
                        next(convolution, None)
                for _ in convolution:
                    pass

            def residual(g):
                dve.wait_ge(out_proj, g.n + 1)
                V.tensor_tensor(res[:, :], b_c[:, 0:T], xn[g.parity][:, :], ALU.add).then_inc(res_ready, 1)

            def residual_norm(g):
                dve.wait_ge(res_rstd, g.n + 1)
                V.tensor_tensor(res[:, :], res[:, :], po_rs[:, :], ALU.mult).then_inc(res_scaled, 1)
                dve.wait_ge(res_scaled, g.n + 1)
                V.tensor_tensor(h1[:, :], res[:, :], h[g.parity][:, :], ALU.add).then_inc(h1_ready, 1)

            def post_scale(g):
                dve.wait_ge(po_rstd, g.n + 1)
                V.tensor_tensor(xs[:, :], b_c[:, 0:T], po_rs[:, :], ALU.mult).then_inc(xs_ready, 1)

            def copy_rows(g):
                dve.wait_ge(rows_turned, g.n + 1)
                dve.wait_ge(rows_stored, 16 * g.n + 16)
                V.tensor_copy(xs_all[:, bass.ds(g.n * TPG, TPG), :].rearrange("p k d -> p (k d)"), b_c[0:TT, 0:TPG * D])
                V.tensor_copy(logit[:, bass.ds(g.n, 1), :].rearrange("p o k -> p (o k)"), b_c[0:TT, TPG * D:TPG * (D + E_N)])
                V.tensor_copy(h1_t[:, :], b_v[0:TT, 0:TPG * D]).then_inc(rows_copied, 1)

            def copy_turned_x(g, c):
                dve.wait_ge(x_turned, NC * g.n + c + 1)
                V.tensor_copy(xdt_t[:, c, :, :].rearrange("p i d -> p (i d)"), XT_B[c][0:QR, 0:GI * D]).then_inc(x_turned_copied, 1)

            def copy_turned_b(g):
                for c in range(2):
                    dve.wait_ge(b_turned, 2 * g.n + c + 1)
                    V.tensor_copy(b_t[:, c, :, :].rearrange("p i d -> p (i d)"), BT_B[c][0:QR, 0:GI * D]
                      ).then_inc(b_turned_copied, 1)

            def x_times_dt(g):
                dve.wait_ge(x_act, g.n + 1)
                dve.wait_ge(spread, g.n + 1)
                if not g.first():
                    dve.wait_ge(yg_ready, g.n)
                v = b_sp[:, 0:SP_G].rearrange("p (c i t) -> p c i t", c=NC, i=GI)
                for c in range(NC):
                    dt_v = v[:, c, :, :].rearrange("p i (t o) -> p i t o", o=1).broadcast_to([128, GI, Q, RANK])
                    V.tensor_tensor(xdt[:, c, :, :].rearrange("p i (t r) -> p i t r", r=RANK), dt_v,
                                    xc[:, :, c, :].rearrange("p i (t r) -> p i t r", r=RANK), ALU.mult).then_inc(xdt_ready, 1)

            def weigh(g, c):
                dve.wait_ge(scores, NC * g.n + c + 1)
                dve.wait_ge(decay_ready, NC * g.n + c + 1)
                for i in range(GI):
                    s = G_B[c][0:QR, i * QR:(i + 1) * QR].rearrange("p (o t r) -> p o t r", o=1, r=RANK)
                    d = decay[:, c, i, :, :].rearrange("p h (t o) -> p h t o", o=1)
                    V.tensor_tensor(m[:, c, i, :, :].rearrange("p h (t r) -> p h t r", r=RANK),
                                    s.broadcast_to([QR, HEADS, Q, RANK]), d.broadcast_to([QR, HEADS, Q, RANK]), ALU.mult
                                    ).then_inc(m_ready, 1)

            def scale_inter(g):
                dve.wait_ge(grow_ready, g.n + 1)
                for c in (1, 2):
                    dve.wait_ge(inter, 2 * g.n + c)
                    gr = grow[:, c - 1, :, :].rearrange("p i (t o) -> p i t o", o=1).broadcast_to([128, GI, Q, RANK])
                    V.tensor_tensor(t1[:, c - 1, :, :].rearrange("p i (t r) -> p i t r", r=RANK),
                                    I_B[c - 1][:, 0:GI * QR].rearrange("p (i t r) -> p i t r", i=GI, r=RANK), gr, ALU.mult
                                    ).then_inc(inter_read, 1)

            def skip_and_intra(g, c):
                dve.wait_ge(intra, NC * g.n + c + 1)
                V.scalar_tensor_tensor(out=y[:, c, :, :], in0=xc[:, :, c, :], scalar=dtc[:, 1:2],
                                       in1=Y_B[c][:, 0:GI * QR].rearrange("p (i t) -> p i t", i=GI), op0=ALU.mult, op1=ALU.add
                                       ).then_inc(y_sum, 1)

            def body(g):
                mix, own, begin = stages(g)
                p = g.last()
                if mix:
                    copy_turned_b(p)
                    for c in range(NC):
                        copy_turned_x(p, c)
                    weigh(p, 0)
                if own:
                    ln1_scale(g)
                if mix:
                    weigh(p, 1)
                if own:
                    dt_begin(g)
                    dt_and_conv(g)
                if mix:
                    weigh(p, 2)
                if mix:
                    scale_inter(p)
                    skip_and_intra(p, 0)
                    skip_and_intra(p, 1)
                if own:
                    conv_pair(g, 2)
                if mix:
                    skip_and_intra(p, 2)
                if own:
                    conv_pair(g, 4)
                    conv_pair(g, 6)
                if mix:
                    residual(p)
                if own:
                    conv_pair(g, 8)
                if mix:
                    residual_norm(p)
                if own:
                    conv_pair(g, 10)
                if mix:
                    post_scale(p)
                    copy_rows(p)
                if own:
                    x_times_dt(g)
                if begin:
                    tokens_bias(g.next())
                if g.first():
                    dve.wait_ge(zeroed, 1 + 32 * PARTS)

            V.memset(eps[:, :], EPS).then_inc(setup_done, 1)
            V.memset(ones_e[:, :], 1.0).then_inc(setup_done, 1)
            dve.wait_ge(loaded, N_LOADS)
            for par in range(2):
                hv = h[par][:, :].rearrange("p (i t) -> p i t", i=GI)
                V.tensor_copy(hv[:, :, 0:1], tcol[:, 1:2].rearrange("p (o t) -> p o t", o=1).broadcast_to([128, GI, 1]))
                V.tensor_scalar(hv[:, :, 1:2], tcol[:, 3:4].rearrange("p (o t) -> p o t", o=1).broadcast_to([128, GI, 1]),
                                tcol[:, 2:3], None, ALU.mult)
            dve.wait_ge(rows_copied, 1)

            def route(p):
                done = [p * N_ROUTE]

                def link(ins):
                    done[0] += 1
                    ins.then_inc(route_step, 1)
                    dve.wait_ge(route_step, done[0])

                dve.wait_ge(rows_copied, (p + 1) * GPP + 1)
                lg = logit[:, p * GPP:(p + 1) * GPP, :].rearrange("p g (k e) -> p (g k) e", e=E_N)
                full = [TT, JT, E_N]

                def row(col):
                    return c88[:, col:col + E_N].rearrange("p (o e) -> p o e", o=1).broadcast_to(full)

                def per_token(t):
                    return t.rearrange("p (j o) -> p j o", o=1).broadcast_to(full)

                src = lg
                for k in range(2):
                    link(V.tensor_reduce(top[k][:, :], src, AX.X, ALU.max))
                    link(V.tensor_tensor(ra[:, :, :], src, per_token(top[k][:, :]), ALU.is_equal))
                    link(V.scalar_tensor_tensor(out=ra[:, :, :], in0=ra[:, :, :], scalar=-float(E_N), in1=row(S_IOTA8),
                                                op0=ALU.mult, op1=ALU.add))
                    link(V.tensor_reduce(idx[:, :], ra[:, :, :], AX.X, ALU.min))
                    link(V.tensor_tensor(onehot[k][:, :, :], row(S_IOTA), per_token(idx[:, :]), ALU.is_equal))
                    if k == 0:
                        link(V.scalar_tensor_tensor(out=rb[:, :, :], in0=onehot[0][:, :, :], scalar=-HIDDEN, in1=lg,
                                                    op0=ALU.mult, op1=ALU.add))
                        src = rb[:, :, :]
                link(V.tensor_tensor(both[:, :, :], onehot[0][:, :, :], onehot[1][:, :, :], ALU.add))
                assert done[0] == p * N_ROUTE + R_BOTH, done
                link(V.tensor_scalar(slot_f[:, :], top[0][:, :], -1.0, None, ALU.mult))
                link(V.tensor_tensor(rd[:, :], top[1][:, :], slot_f[:, :], ALU.add))
                assert done[0] == p * N_ROUTE + R_DIFF, done
                dve.wait_ge(route_exp, p + 1)
                link(V.tensor_scalar(idx[:, :], rd[:, :], 1.0, None, ALU.add))
                link(V.reciprocal(wgt[0][:, p, :], idx[:, :]))
                link(V.tensor_tensor(wgt[1][:, p, :], rd[:, :], wgt[0][:, p, :], ALU.mult))
                dve.wait_ge(route_mm, p + 1)
                n = JT * E_N
                link(V.tensor_copy(rtot[:, :, :], b_tok[0:TT, n:2 * n].rearrange("p (j e) -> p e j", e=E_N)))
                link(V.tensor_tensor_scan(rsum[:, :, :].rearrange("p e j -> p (e j)"), c88[:, S_MASK:S_MASK + n],
                                          rtot[:, :, :].rearrange("p e j -> p (e j)"), 0.0, ALU.mult, ALU.add))
                kfull = [TT, E_N, KMAX]
                link(V.tensor_tensor(cmp_k[:, :, :], rsum[:, :, JT - 1:JT].broadcast_to(kfull),
                                     c88[:, S_KIO:S_KIO + E_N * KMAX].rearrange("p (e k) -> p e k", e=E_N), ALU.is_gt))
                link(V.tensor_reduce(ntile[:, :], cmp_k[:, :, :], AX.X, ALU.add))
                link(V.tensor_tensor_scan(endt[:, :], ones_e[:, :], ntile[:, :], 0.0, ALU.mult, ALU.add))
                link(V.tensor_tensor(base[:, :], endt[:, :], ntile[:, :], ALU.subtract))
                tfull = [TT, NT, E_N]
                link(V.tensor_tensor(cmp_t[:, :, :], c88[:, S_TIO:S_TIO + NT * E_N].rearrange("p (t e) -> p t e", e=E_N),
                                     endt[:, :].rearrange("p (o e) -> p o e", o=1).broadcast_to(tfull), ALU.is_ge))
                link(V.tensor_reduce(tile_f[:, :], cmp_t[:, :, :], AX.X, ALU.add))
                link(V.tensor_scalar(tile_e[0:1, p, :], tile_f[0:1, :], float(E_N - 1), None, ALU.min))
                link(V.tensor_tensor(rsum[:, :, :], rsum[:, :, :], rtot[:, :, :], ALU.subtract))
                assert done[0] == (p + 1) * N_ROUTE, done
                V.tensor_tensor(ra[:, :, :], b_tok[0:TT, 0:n].rearrange("p (j e) -> p j e", e=E_N),
                                rsum[:, :, :].rearrange("p e j -> p j e"), ALU.add).then_inc(slot_step, 1)
                dve.wait_ge(slot_step, 7 * p + 1)
                V.scalar_tensor_tensor(out=ra[:, :, :], in0=base[:, :].rearrange("p (o e) -> p o e", o=1).broadcast_to(full),
                                       scalar=float(SL), in1=ra[:, :, :], op0=ALU.mult, op1=ALU.add).then_inc(slot_step, 1)
                dve.wait_ge(slot_step, 7 * p + 2)
                V.tensor_tensor(rb[:, :, :], ra[:, :, :], onehot[0][:, :, :], ALU.mult)
                V.tensor_tensor(both[:, :, :], ra[:, :, :], onehot[1][:, :, :], ALU.mult).then_inc(slot_step, 1)
                dve.wait_ge(slot_step, 7 * p + 3)
                for k, src in enumerate((rb, both)):
                    V.tensor_reduce(slot_f[:, :], src[:, :, :], AX.X, ALU.add).then_inc(slot_step, 1)
                    dve.wait_ge(slot_step, 7 * p + 4 + 2 * k)
                    V.tensor_copy(slot_u[:, p, :, k], slot_f[:, :]).then_inc(slot_step, 1)
                    dve.wait_ge(slot_step, 7 * p + 5 + 2 * k)
                V.tensor_copy(idx[:, :], slot_f[:, :]).then_inc(routed, 1)
                dve.wait_ge(routed, p + 1)

            tokens_bias(Group(0, 0, 0))
            over_groups(dve, body, lambda: route(0))
            route(1)

            tiles = tile_e[:, :, :].rearrange("o p t -> o (p t)")

            def expert(n):
                return dve.value_load(tiles[0:1, bass.ds(n, 1)], min_val=0, max_val=E_N - 1)

            def turned(n, s):
                dve.wait_ge(fx_turned, n + 1)
                if not isinstance(n, int) or n >= 2:
                    dve.wait_ge(hidden_mm, n - 1)
                V.tensor_copy(fxt[s], bank[s][:, 0:SL]).then_inc(fx_copied, 1)

            def stage(n, b):
                e = expert(n)
                if not isinstance(n, int) or n >= 4:
                    dve.wait_ge(y_biased, n - 3)
                V.tensor_copy(fw[b], wall[:, bass.ds(e, 1), :].rearrange("p o c -> p (o c)")).then_inc(w_staged, 1)

            def add_bias(n, b, before):
                s = b % 2
                dve.wait_ge(y_mm, n + 1)
                dve.wait_ge(fy_stored[s], before * 16 + 16)
                V.tensor_tensor(fy[s], bank[4 + s][:, 0:D], fw[b][:, W1C + FF:WCOLS], ALU.add).then_inc(y_biased, 1)

            def combine(k, b):
                s = b % 2
                dve.wait_ge(gathered[b // 2], 64 * k + 64)
                dve.wait_ge(gh_loaded[s], 32 * k + (16 * (b // 2) + 16))
                w = [x[:, :, :].rearrange("p q j -> p (q j)")[:, bass.ds(4 * k + b, 1)] for x in wgt]
                V.scalar_tensor_tensor(out=gh[s][:, :], in0=gy[b][0][:, :], scalar=w[0], in1=gh[s][:, :],
                                       op0=ALU.mult, op1=ALU.add).then_inc(first_added, 1)
                dve.wait_ge(first_added, 4 * k + (b + 1))
                dve.wait_ge(out_stored[s], 32 * k + (16 * (b // 2) + 16))
                V.scalar_tensor_tensor(out=go[s][:, :], in0=gy[b][1][:, :], scalar=w[1], in1=gh[s][:, :],
                                       op0=ALU.mult, op1=ALU.add).then_inc(combined, 1)

            dve.wait_ge(experts_loaded, 16)
            n = PARTS * NT
            for k in range(3):
                stage(k, k)
                turned(k, k % 2)

            def tile_step(t, b, before):
                stage(t + 3, (b + 3) % 4)
                turned(t + 3, (b + 3) % 2)
                add_bias(t, b, before)

            with dve.Fori(0, (NT + 4) // 4) as i:
                for k in range(4):
                    tile_step(4 * i + k, k, 2 * i + k // 2)
            with dve.Fori(0, MIXED) as i:
                for k in range(16):
                    tile_step(16 * i + (NT + 4 + k), k % 4, 8 * i + (NT // 2 + 2 + k // 2))
                    if k % 4 < 3:
                        o = 3 * (k // 4) + k % 4
                        combine(3 * i + o // 4, o % 4)
            tile_step(n - 4, 0, n // 2 - 2)
            for k in range(1, 4):
                add_bias(n - 4 + k, k, n // 2 - 2 + k // 2)

            with dve.Fori(JT // 4, JT // 2) as i:
                for b in range(4):
                    combine(i, b)

        @block.gpsimd
        def _(pool):
            P = nc.gpsimd

            def segment_rows(g):
                pool.wait_ge(dt_step, N_DT * g.n + DT_A)
                if not g.first():
                    pool.wait_ge(seg_summed, NC * g.n)
                    pool.wait_ge(spread, g.n)
                n = NC * GI * HEADS
                a = da_s[:, :, :, :].rearrange("p c i (h o) -> p (c i h) o", o=1).broadcast_to([Q, n, Q])
                tri = c88[0:Q, S_IT + Q:S_IT + 2 * Q].rearrange("p (o t) -> p o t", o=1).broadcast_to([Q, n, Q])
                P.tensor_tensor(seg_r[0:Q, :, :], a, tri, ALU.mult).then_inc(seg_ready, 1)
                a = dt_s[:, :, :, :].rearrange("p c i (h o) -> p (c i h) o", o=1).broadcast_to([Q, n, Q])
                one = c88[0:Q, S_IT:S_IT + Q].rearrange("p (o t) -> p o t", o=1).broadcast_to([Q, n, Q])
                P.tensor_tensor(dt_diag[:, :, :], a, one, ALU.mult).then_inc(dt_widened, 1)

            def x_to_end(g):
                n = GI * HEADS
                for c in range(2):
                    pool.wait_ge(x_turned_copied, NC * g.n + c + 1)
                    d = decay[:, c, :, :, Q - 1:Q].rearrange("p i h o -> p (i h) o").broadcast_to([QR, n, PC])
                    x = xdt_t[:, c, :, :].rearrange("p i (h q) -> p (i h) q", q=HP)[:, :, 0:PC]
                    P.tensor_tensor(xe[:, c, :, :].rearrange("p i (h q) -> p (i h) q", q=PC), x, d, ALU.mult).then_inc(xe_part, 1)
                pool.wait_ge(xe_part, 2 * g.n + 2)
                pool.wait_ge(total_ready, g.n + 1)
                t = total[:, :, :].rearrange("p i (h o) -> p (i h) o", o=1).broadcast_to([QR, n, PC])
                P.tensor_tensor(xe[:, 2, :, :].rearrange("p i (h q) -> p (i h) q", q=PC),
                                xe[:, 0, :, :].rearrange("p i (h q) -> p (i h) q", q=PC), t, ALU.mult).then_inc(xe_ready, 1)

            def gate(g):
                pool.wait_ge(z_act, RANK * (g.n + 1))
                for c in range(NC):
                    pool.wait_ge(y_sum, NC * g.n + c + 1)
                    if c:
                        pool.wait_ge(inter_read, 2 * g.n + c)
                        P.tensor_tensor(y[:, c, :, :], y[:, c, :, :], t1[:, c - 1, :, :], ALU.add).then_inc(y_total, 1)
                        pool.wait_ge(y_total, 2 * g.n + c)
                    o = yg[:, :, :].rearrange("p r (i k t) -> p r i k t", i=GI, k=NC)[:, :, :, c, :].rearrange("p r i t -> p i t r")
                    z = sz[:, :, :].rearrange("p r (i k t) -> p r i k t", i=GI, k=NC)[:, :, :, c, :].rearrange("p r i t -> p i t r")
                    last = P.tensor_tensor(o, y[:, c, :, :].rearrange("p i (t r) -> p i t r", r=RANK), z, ALU.mult)
                last.then_inc(yg_ready, 1)

            for s in range(2):
                P.memset(mark[0:1, s:s + 1], 0.0).then_inc(fy_stored[s], 16)
                P.memset(mark[0:1, 2 + s:3 + s], 0.0).then_inc(out_stored[s], 16)
            P.memset(m_buf[:, :], 0.0)
            P.memset(hs[:, :, :, :, :], 0.0).then_inc(hs_zeroed, 1)
            pool.wait_ge(hs_zeroed, 1)
            P.memset(xe[0:QR, 0, 0, 0:1], 0.0).then_inc(zeroed, 1)
            pool.wait_ge(zeroed, 1)
            pool.wait_ge(loaded, N_LOADS)

            def body(g):
                mix, own, _ = stages(g)
                if mix:
                    x_to_end(g.last())
                if own:
                    segment_rows(g)
                if mix:
                    gate(g.last())

            def take_wait():
                P.tensor_tensor(mark[0:1, 4:5], c88[0:1, 0:1], c88[0:1, 0:1], ALU.add)

            def send(p, j, s, k):
                if not (isinstance(k, int) and k == 0):
                    pool.wait_ge(sent[s], k * 32)
                for q in range(2):
                    P.tensor_copy(sc_i[s][q][:, :], slot_u[:, p, bass.ds(j, 1), q])
                P.tensor_copy(sc_x[s][:, :], xs_all[:, bass.ds(p * JT + j, 1), :].rearrange("p o d -> p (o d)")).then_inc(sc_copied, 1)
                pool.wait_ge(sc_copied, 2 * k + (s + 1))
                take_wait()
                for q in range(2):
                    P.indirect_dma_start(slot_x[p], bass.IndirectOffsetOnAxis(ap=sc_i[s][q][:, 0:1], axis=0), sc_x[s][:, :], None
                                         ).then_inc(sent[s], 16)

            def gather(p, j, h, k):
                if not (isinstance(k, int) and k == 0):
                    pool.wait_ge(combined, 4 * k + (2 * h - 2))
                P.tensor_copy(gi[h][:, :], slot_u[:, p, bass.ds(j, 2), :].rearrange("p j q -> p (j q)")).then_inc(ga_index, 1)
                pool.wait_ge(ga_index, 2 * k + (h + 1))
                take_wait()
                for o in range(2):
                    for q in range(2):
                        c = 2 * o + q
                        P.indirect_dma_start(gy[2 * h + o][q][:, :], None, slot_y[p],
                                             bass.IndirectOffsetOnAxis(ap=gi[h][:, c:c + 1], axis=0)).then_inc(gathered[h], 16)

            def route_waits():
                pool.wait_ge(routed, 1)
                pool.wait_ge(zeroed, 1 + 32 * PARTS)

            over_groups(pool, body, route_waits, send)
            pool.wait_ge(routed, PARTS)
            with pool.Fori(0, JT // 2) as i:
                for s in range(2):
                    send(1, 2 * i + s, s, i + JT // 2)
            for s in range(2):
                pool.wait_ge(fy_stored[s], 16 + 16 * NT // 2)
            for h in range(2):
                gather(0, 2 * h, h, 0)
            with pool.Fori(1, JT // 4) as i:
                for h in range(2):
                    gather(0, 4 * i + 2 * h, h, i)
            for s in range(2):
                pool.wait_ge(fy_stored[s], 16 + 16 * NT)
            with pool.Fori(JT // 4, JT // 2) as i:
                for h in range(2):
                    gather(1, 4 * i + (2 * h - JT), h, i)
            for s in range(2):
                pool.wait_ge(gathered[s], 32 * PARTS * JT // 2)


def kernel(**inputs):
    import concourse.bacc as bacc
    from concourse.bass_utils import run_bass_kernel_spmd

    a = {k: np.ascontiguousarray(v) for k, v in inputs.items()}
    side = 224 // PATCH

    x = a["x"].reshape(NG, GI, CH, side, PATCH, side, PATCH).transpose(0, 2, 4, 6, 1, 3, 5).reshape(NG, K_TOK, GI * NPATCH)
    x_main = x[:, :KC * D].reshape(NG, KC, D, GI * NPATCH).transpose(0, 2, 1, 3).reshape(NG, D, KC * GI * NPATCH)
    w = a["L0_tok_W"].T
    tok_cols = np.concatenate([a["L0_tok_b"][:, None], a["cls_tok"].reshape(D, 1), a["L0_tok_class_token"].reshape(D, 1),
                               a["L0_tok_pos_embed"].T], axis=1)

    def padded(v):
        o = np.zeros(v.shape[:-1] + (HP,), v.dtype)
        o[..., :PC] = v
        return o.reshape(v.shape[:-2] + (HEADS * HP,))

    inner, wide = HEADS * RANK * PC, NST * RANK
    w_in = a["L0_attn_W_in"]

    def by_rank(v):
        return padded(v.reshape(-1, HEADS, RANK, PC).transpose(0, 2, 1, 3))

    def states_by_rank(v):
        return v.reshape(-1, NST, RANK).transpose(0, 2, 1)

    o = 2 * inner
    w_proj = np.concatenate([by_rank(w_in[:, inner:o]), states_by_rank(w_in[:, o:o + wide]),
                             states_by_rank(w_in[:, o + wide:o + 2 * wide]), by_rank(w_in[:, :inner])], axis=1)
    taps = np.concatenate([a["L0_attn_conv_w"], a["L0_attn_conv_b"][:, None]], axis=1).T
    conv = np.concatenate([by_rank(taps[:, :inner]), states_by_rank(taps[:, inner:inner + wide]),
                           states_by_rank(taps[:, inner + wide:])], axis=1)
    heads = np.stack([a["L0_attn_A_log"], a["L0_attn_D_skip"]], axis=1)
    w1 = a["L0_ffn_w1"].transpose(1, 0, 2)
    w2 = a["L0_ffn_w2"].reshape(E_N, FC, D, D).transpose(2, 0, 1, 3).reshape(D, E_N, FF)
    b1 = a["L0_ffn_b1"].reshape(E_N, FC, D).transpose(2, 0, 1)
    b2 = np.broadcast_to(a["L0_ffn_b2"][None], (D, E_N, D))
    c128, c88, seg = constants()
    arrays = {
        "x_main": x_main,
        "x_tail": x[:, KC * D:],
        "w_tok": w[:KC * D].reshape(KC, D, D).transpose(1, 0, 2).reshape(D, KC * D),
        "w_tok_tail": w[KC * D:],
        "tok_cols": tok_cols,
        "w_in": w_proj.reshape(D, -1),
        "w_dt": w_in[:, o + 2 * wide:],
        "conv": conv.transpose(2, 1, 0).reshape(D, -1),
        "dt_row": np.tile(np.concatenate([a["L0_attn_dt_bias"], a["L0_attn_A_log"]])[None], (Q, 1)),
        "dt_col": np.repeat(heads, HP, axis=0),
        "w_out": by_rank(a["L0_attn_W_out"].T).transpose(2, 1, 0).reshape(D, -1),
        "gate_w": a["L0_ffn_gate_w"].T,
        "experts": np.concatenate([w1, b1, w2, b2], axis=2).reshape(D, -1),
        "c128": c128,
        "c88": c88,
        "seg": seg,
    }
    arrays = {k: np.ascontiguousarray(v) for k, v in arrays.items()}
    nc = bacc.Bacc("TRN2", target_bir_lowering=False, num_devices=1)
    args = [nc.dram_tensor("in_" + k, v.shape, mybir.dt.from_np(v.dtype), kind="ExternalInput").ap() for k, v in arrays.items()]
    out = nc.dram_tensor("out", (B, L, D), FP32, kind="ExternalOutput").ap()
    tower(nc, *args, out)
    r = run_bass_kernel_spmd(nc, [{"in_" + k: v for k, v in arrays.items()}], core_ids=[0])
    return r.results[0]["out"]
```
